# Optimizing a Trainium2 kernel written in Bass

```python
import numpy as np
import jax
import jax.numpy as jnp

def _softmax(x, axis=-1):
    return jax.nn.softmax(x, axis=axis)

def _gelu(x):
    return jax.nn.gelu(x, approximate=True)

def _silu(x):
    return jax.nn.silu(x)

def _sigmoid(x):
    return jax.nn.sigmoid(x)

def _layernorm(x, axis=-1, eps=1e-05):
    m = jnp.mean(x, axis=axis, keepdims=True)
    v = jnp.var(x, axis=axis, keepdims=True)
    return (x - m) / jnp.sqrt(v + eps)

def _scatter_add(tgt, idx, src, axis=0):
    return tgt.at[idx].add(src)

def _segment_sum(src, seg, n):
    return jax.ops.segment_sum(src, seg, n)
kernel_name = 'mk_gnn_preln_d4_gnn_r8_617a9c'

def setup_inputs(seed: int=0):
    np.random.seed(seed)
    _w = jnp.asarray

    def _rec_inputs():
        import jax
        import jax.numpy as jnp
        _gk = jax.random.key(seed)
        x = -0.000202 + 1 * jax.random.normal(jax.random.fold_in(_gk, 1), (6250, 128), jnp.float32)
        src = jax.random.randint(jax.random.fold_in(_gk, 2), (100000,), 0, 6250, jnp.int32)
        dst = jnp.minimum((6250 * jax.random.uniform(jax.random.fold_in(_gk, 3), (100000,)) ** 2.0).astype(jnp.int32), 49999)
        _o = jnp.argsort(dst, stable=True)
        src = src[_o]
        dst = dst[_o]
        edge_attr_128 = -8.513e-05 + 0.999844 * jax.random.normal(jax.random.fold_in(_gk, 12), (100000, 128), jnp.float32)
        edge_weight = jax.random.uniform(jax.random.fold_in(_gk, 14), (100000,), jnp.float32, 0.0, 1)
        edge_weight1 = jax.random.uniform(jax.random.fold_in(_gk, 15), (100000, 1), jnp.float32, 0.0, 0.999998)
        return (x, src, dst, edge_attr_128, edge_weight, edge_weight1)
    x, src, dst, edge_attr_128, edge_weight, edge_weight1 = _rec_inputs()

    def _L0_gnn_setup():
        import jax, jax.numpy as jnp
        import numpy as np
        N = 6250
        E = 100000
        D_IN = 128
        D_HID = 128
        NUM_LAYERS = 3

        def _gcn_layer(h, src, dst, norm, W, b, n):
            h = h @ W
            msg = h[src] * norm[:, None]
            out = jax.ops.segment_sum(msg, dst, num_segments=n)
            return out + b
        key = jax.random.key(seed)
        ks = jax.random.split(key, 8)
        x = jax.random.normal(ks[0], (N, D_IN), dtype=jnp.float32)
        edge_index = jax.random.randint(ks[1], (2, E), 0, N, dtype=jnp.int64)
        edge_weight = jnp.ones((E,), dtype=jnp.float32)

        def w(k, fi, fo):
            return jax.random.normal(k, (fi, fo), dtype=jnp.float32) * (1.0 / np.sqrt(fi))
        W0 = w(ks[2], D_IN, D_HID)
        b0 = jnp.zeros((D_HID,), dtype=jnp.float32)
        W1 = w(ks[3], D_HID, D_HID)
        b1 = jnp.zeros((D_HID,), dtype=jnp.float32)
        W2 = w(ks[4], D_HID, D_HID)
        b2 = jnp.zeros((D_HID,), dtype=jnp.float32)
        return {'x': x, 'edge_index': edge_index, 'edge_weight': edge_weight, 'W0': W0, 'b0': b0, 'W1': W1, 'b1': b1, 'W2': W2, 'b2': b2}
    _L0_gnn_all = _L0_gnn_setup()
    _L0_gnn_in = {k: v for k, v in _L0_gnn_all.items() if k in ('W0', 'b0', 'W1', 'b1', 'W2', 'b2')}
    del _L0_gnn_all

    def _L1_gnn_setup():
        import jax, jax.numpy as jnp
        import numpy as np
        EPS = 0.0
        key = jax.random.key(seed)
        kx, ke, kw, k1, k2 = jax.random.split(key, 5)
        N, E, D, H = (12500, 75000, 128, 128)
        x = jax.random.normal(kx, (N, D), dtype=jnp.float32)
        edge_index = jax.random.randint(ke, (2, E), 0, N, dtype=jnp.int64)
        edge_weight = jax.random.uniform(kw, (E,), dtype=jnp.float32)
        W1 = jax.random.normal(k1, (D, H), dtype=jnp.float32) * (1.0 / np.sqrt(D))
        b1 = jnp.zeros((H,), dtype=jnp.float32)
        W2 = jax.random.normal(k2, (H, D), dtype=jnp.float32) * (1.0 / np.sqrt(H))
        b2 = jnp.zeros((D,), dtype=jnp.float32)
        return {'x': x, 'edge_index': edge_index, 'edge_weight': edge_weight, 'W1': W1, 'b1': b1, 'W2': W2, 'b2': b2}
    _L1_gnn_all = _L1_gnn_setup()
    _L1_gnn_in = {k: v for k, v in _L1_gnn_all.items() if k in ('W1', 'b1', 'W2', 'b2')}
    del _L1_gnn_all

    def _L2_gnn_setup():
        import jax, jax.numpy as jnp
        import numpy as np
        import math
        NUM_HEADS = 8
        HEAD_DIM = 16
        SCALE = 1.0 / math.sqrt(HEAD_DIM)

        def _segment_softmax(logits, seg, num):
            m = jax.ops.segment_max(logits, seg, num_segments=num)
            m = jax.lax.stop_gradient(jnp.where(jnp.isfinite(m), m, 0.0))
            e = jnp.exp(logits - m[seg])
            den = jax.ops.segment_sum(e, seg, num_segments=num)
            den = jnp.where(den == 0, 1.0, den)
            return e / den[seg]
        key = jax.random.key(seed)
        ks = jax.random.split(key, 9)
        N, E, F = (6250, 80000, 128)
        node_h = jax.random.normal(ks[0], (N, F), jnp.float32)
        edge_h = jax.random.normal(ks[1], (E, F), jnp.float32)
        distance = jax.random.uniform(ks[2], (E, 1), jnp.float32, minval=0.1, maxval=1.0)
        src = jax.random.randint(ks[3], (E,), 0, N, jnp.int32)
        dst = jax.random.randint(ks[4], (E,), 0, N, jnp.int32)

        def lin(k):
            kw, kb = jax.random.split(k)
            W = jax.random.normal(kw, (F, F), jnp.float32) / math.sqrt(F)
            b = jax.random.normal(kb, (F,), jnp.float32) * 0.02
            return (W, b)
        Wq, bq = lin(ks[5])
        Wk, bk = lin(ks[6])
        Wv, bv = lin(ks[7])
        Wo, bo = lin(ks[8])
        lam = jnp.array(1.0, jnp.float32)
        return dict(node_h=node_h, edge_h=edge_h, distance=distance, Wq=Wq, bq=bq, Wk=Wk, bk=bk, Wv=Wv, bv=bv, Wo=Wo, bo=bo, lam=lam, src=src, dst=dst)
    _L2_gnn_all = _L2_gnn_setup()
    _L2_gnn_in = {k: v for k, v in _L2_gnn_all.items() if k in ('Wq', 'bq', 'Wk', 'bk', 'Wv', 'bv', 'Wo', 'bo', 'lam')}
    del _L2_gnn_all

    def _L3_gnn_setup():
        import jax, jax.numpy as jnp
        import numpy as np
        EPS = 1e-12
        key = jax.random.key(seed)
        k1, k2, k3, k4, k5 = jax.random.split(key, 5)
        N, E, D = (12500, 200000, 128)
        x = jax.random.normal(k1, (N, D), dtype=jnp.float32)
        edge_index = jax.random.randint(k2, (2, E), 0, N, dtype=jnp.int64)
        W_l = jax.random.normal(k3, (D, D), dtype=jnp.float32) * 0.05
        b_l = jax.random.normal(k4, (D,), dtype=jnp.float32) * 0.05
        W_r = jax.random.normal(k5, (D, D), dtype=jnp.float32) * 0.05
        return {'x': x, 'edge_index': edge_index, 'W_l': W_l, 'b_l': b_l, 'W_r': W_r}
    _L3_gnn_all = _L3_gnn_setup()
    _L3_gnn_in = {k: v for k, v in _L3_gnn_all.items() if k in ('W_l', 'b_l', 'W_r')}
    del _L3_gnn_all
    return {'x': x, 'src': src, 'dst': dst, 'edge_attr_128': edge_attr_128, 'edge_weight': edge_weight, 'edge_weight1': edge_weight1, 'L0_gnn_W0': _L0_gnn_in['W0'], 'L0_gnn_b0': _L0_gnn_in['b0'], 'L0_gnn_W1': _L0_gnn_in['W1'], 'L0_gnn_b1': _L0_gnn_in['b1'], 'L0_gnn_W2': _L0_gnn_in['W2'], 'L0_gnn_b2': _L0_gnn_in['b2'], 'L1_gnn_W1': _L1_gnn_in['W1'], 'L1_gnn_b1': _L1_gnn_in['b1'], 'L1_gnn_W2': _L1_gnn_in['W2'], 'L1_gnn_b2': _L1_gnn_in['b2'], 'L2_gnn_Wq': _L2_gnn_in['Wq'], 'L2_gnn_bq': _L2_gnn_in['bq'], 'L2_gnn_Wk': _L2_gnn_in['Wk'], 'L2_gnn_bk': _L2_gnn_in['bk'], 'L2_gnn_Wv': _L2_gnn_in['Wv'], 'L2_gnn_bv': _L2_gnn_in['bv'], 'L2_gnn_Wo': _L2_gnn_in['Wo'], 'L2_gnn_bo': _L2_gnn_in['bo'], 'L2_gnn_lam': _L2_gnn_in['lam'], 'L3_gnn_W_l': _L3_gnn_in['W_l'], 'L3_gnn_b_l': _L3_gnn_in['b_l'], 'L3_gnn_W_r': _L3_gnn_in['W_r']}

def reference(x, src, dst, edge_attr_128, edge_weight, edge_weight1, L0_gnn_W0, L0_gnn_b0, L0_gnn_W1, L0_gnn_b1, L0_gnn_W2, L0_gnn_b2, L1_gnn_W1, L1_gnn_b1, L1_gnn_W2, L1_gnn_b2, L2_gnn_Wq, L2_gnn_bq, L2_gnn_Wk, L2_gnn_bk, L2_gnn_Wv, L2_gnn_bv, L2_gnn_Wo, L2_gnn_bo, L2_gnn_lam, L3_gnn_W_l, L3_gnn_b_l, L3_gnn_W_r):
    import jax
    import jax.numpy as jnp

    def _L0_gnn_ref(x, edge_index, edge_weight, W0, b0, W1, b1, W2, b2):
        import jax, jax.numpy as jnp
        import numpy as np
        N = 6250
        E = 100000
        D_IN = 128
        D_HID = 128
        NUM_LAYERS = 3

        def _gcn_layer(h, src, dst, norm, W, b, n):
            h = h @ W
            msg = h[src] * norm[:, None]
            out = jax.ops.segment_sum(msg, dst, num_segments=n)
            return out + b
        n = x.shape[0]
        loop = jnp.arange(n, dtype=edge_index.dtype)
        src = jnp.concatenate([edge_index[0], loop])
        dst = jnp.concatenate([edge_index[1], loop])
        ew = jnp.concatenate([edge_weight, jnp.ones((n,), dtype=edge_weight.dtype)])
        deg = jax.ops.segment_sum(ew, dst, num_segments=n)
        dis = jnp.where(deg > 0, jax.lax.rsqrt(deg), 0.0)
        norm = dis[src] * ew * dis[dst]
        z = x
        for W, b in ((W0, b0), (W1, b1), (W2, b2)):
            z = _gcn_layer(z, src, dst, norm, W, b, n)
            z = jax.nn.relu(z)
        return z

    def _L1_gnn_ref(x, edge_index, edge_weight, W1, b1, W2, b2):
        import jax, jax.numpy as jnp
        import numpy as np
        EPS = 0.0
        N = x.shape[0]
        src, dst = (edge_index[0], edge_index[1])
        msg = edge_weight[:, None] * x[src]
        agg = jax.ops.segment_sum(msg, dst, num_segments=N)
        out = (1.0 + EPS) * x + agg
        h = jax.nn.relu(out @ W1 + b1)
        return h @ W2 + b2

    def _L2_gnn_ref(node_h, edge_h, distance, Wq, bq, Wk, bk, Wv, bv, Wo, bo, lam, src, dst):
        import jax, jax.numpy as jnp
        import numpy as np
        import math
        NUM_HEADS = 8
        HEAD_DIM = 16
        SCALE = 1.0 / math.sqrt(HEAD_DIM)

        def _segment_softmax(logits, seg, num):
            m = jax.ops.segment_max(logits, seg, num_segments=num)
            m = jax.lax.stop_gradient(jnp.where(jnp.isfinite(m), m, 0.0))
            e = jnp.exp(logits - m[seg])
            den = jax.ops.segment_sum(e, seg, num_segments=num)
            den = jnp.where(den == 0, 1.0, den)
            return e / den[seg]
        N = node_h.shape[0]
        q = (node_h @ Wq.T + bq).reshape(N, NUM_HEADS, HEAD_DIM)
        k = (edge_h @ Wk.T + bk).reshape(-1, NUM_HEADS, HEAD_DIM)
        v = (node_h @ Wv.T + bv).reshape(N, NUM_HEADS, HEAD_DIM)
        qs, qd = (q[src], q[dst])
        in_m = jnp.sum(qs * k, axis=-1)
        out_m = jnp.sum(qd * k, axis=-1)
        diag_m = jnp.sum(qs * qd, axis=-1)
        att = jnp.power(distance, lam)
        score = (_segment_softmax(in_m * SCALE, dst, N) + _segment_softmax(out_m * SCALE, dst, N) + _segment_softmax(diag_m * SCALE, dst, N)) * att
        h = jax.ops.segment_sum(score[..., None] * v[dst], dst, num_segments=N)
        h = h.reshape(N, NUM_HEADS * HEAD_DIM)
        out = h @ Wo.T + bo
        return jax.nn.leaky_relu(out, negative_slope=0.1)

    def _L3_gnn_ref(x, edge_index, W_l, b_l, W_r):
        import jax, jax.numpy as jnp
        import numpy as np
        EPS = 1e-12
        N = x.shape[0]
        src, dst = (edge_index[0], edge_index[1])
        msg_sum = jax.ops.segment_sum(x[src], dst, num_segments=N)
        deg = jax.ops.segment_sum(jnp.ones_like(dst, dtype=x.dtype), dst, num_segments=N)
        agg = msg_sum / jnp.maximum(deg, 1.0)[:, None]
        out = agg @ W_l.T + b_l + x @ W_r.T
        norm = jnp.sqrt(jnp.sum(out * out, axis=-1, keepdims=True))
        return out / jnp.maximum(norm, EPS)
    edge_index = jnp.stack([src, dst])
    h = jnp.maximum(_layernorm(x, axis=-1), 0.0)
    x = x + _L0_gnn_ref(h, edge_index, edge_weight, L0_gnn_W0, L0_gnn_b0, L0_gnn_W1, L0_gnn_b1, L0_gnn_W2, L0_gnn_b2)
    h = jnp.maximum(_layernorm(x, axis=-1), 0.0)
    x = x + _L1_gnn_ref(h, edge_index, edge_weight, L1_gnn_W1, L1_gnn_b1, L1_gnn_W2, L1_gnn_b2)
    h = jnp.maximum(_layernorm(x, axis=-1), 0.0)
    x = x + _L2_gnn_ref(h, edge_attr_128, edge_weight1, L2_gnn_Wq, L2_gnn_bq, L2_gnn_Wk, L2_gnn_bk, L2_gnn_Wv, L2_gnn_bv, L2_gnn_Wo, L2_gnn_bo, L2_gnn_lam, src, dst)
    h = jnp.maximum(_layernorm(x, axis=-1), 0.0)
    x = x + _L3_gnn_ref(h, edge_index, L3_gnn_W_l, L3_gnn_b_l, L3_gnn_W_r)
    return x

_drawn_inputs = setup_inputs


def setup_inputs(seed=0):
    import zlib

    import numpy as np

    out = dict(_drawn_inputs(seed))
    spreads = {'L0_gnn_b0': (0.0, 0.1),
     'L0_gnn_b1': (0.0, 0.1),
     'L0_gnn_b2': (0.0, 0.1),
     'L1_gnn_b1': (0.0, 0.516),
     'L1_gnn_b2': (0.0, 0.336)}
    factors = {'edge_attr_128': 4.721,
     'L2_gnn_Wq': 4.61,
     'L2_gnn_bq': 47.143,
     'L2_gnn_Wk': 4.7,
     'L2_gnn_bk': 64.0,
     'L2_gnn_bv': 8.0,
     'L2_gnn_bo': 21.367,
     'L3_gnn_W_l': 23.822,
     'L3_gnn_b_l': 64.0,
     'L3_gnn_W_r': 18.891}
    for name, (base, spread) in spreads.items():
        noise = np.random.default_rng([zlib.crc32(name.encode()), seed]).standard_normal(out[name].shape)
        drawn = base * np.exp(spread * noise) if base else spread * noise
        out[name] = jnp.asarray(drawn.astype(out[name].dtype))
    for name, factor in factors.items():
        out[name] = (out[name] * factor).astype(out[name].dtype)
    return out
```

```python
import math
from contextlib import ExitStack

import concourse.bass as bass
from concourse import mybir

F32 = mybir.dt.float32
BF16 = mybir.dt.bfloat16
I32 = mybir.dt.int32
ALU = mybir.AluOpType
ACT = mybir.ActivationFunctionType
AX = mybir.AxisListType

P = 128
D = 128
HEADS = 8
HEAD_DIM = D // HEADS
SCALE = 1.0 / math.sqrt(HEAD_DIM)
LN_EPS = 1e-5
NORM_EPS = 1e-12
SLOPE = 0.1
BIG = 1e30

PS_BANKS = 8
BANK = 512
GROUP = BANK // P


def ceil_div(a, b):
    return -(-a // b)


def spread(ap, dim, n):
    shape = list(ap.shape)
    shape[dim] = n
    return ap.broadcast_to(shape)


class Engine:

    def __init__(self, name, done):
        self.name, self.done, self.count, self.queue, self.seen = name, done, 0, [], {}

    def do(self, instruction):
        self.count += 1
        self.queue.append(lambda e, f=instruction, s=self.done: f(e).then_inc(s, 1))
        return (self.done, self.count)

    def dma(self, instruction, semaphore):
        semaphore.count += 16
        self.queue.append(lambda e, f=instruction, s=semaphore.handle: f(e).then_inc(s, 16))
        return (semaphore.handle, semaphore.count)

    def wait(self, *tokens):
        for token in tokens:
            if token is None:
                continue
            handle, count = token
            if self.seen.get(id(handle), 0) < count:
                self.seen[id(handle)] = count
                self.queue.append(lambda e, h=handle, c=count: e.wait_ge(h, c))


class Lane:

    def __init__(self, handle):
        self.handle, self.count = handle, 0


def build(nc, x_in, src_in, dst_in, attr_in, ew_in, dist_in, W0, b0, W1, b1, W2, b2,
          G1, c1, G2, c2, Wq, bq, Wk, bk, Wv, bv, Wo, bo, lam, Wl, bl, Wr, out):
    N = x_in.shape[0]
    E = src_in.shape[0]
    NB = ceil_div(N, P)
    NP = NB * P
    LAST = N - (NB - 1) * P
    NT = ceil_div(E, P)
    OVER = NT * P - E
    QUADS = 4
    NS = ceil_div(NT + NB - 1, QUADS * GROUP) * QUADS * GROUP
    SR = ceil_div(NS, P)
    QS = NS // QUADS
    FIELDS = 6
    DST, BEFORE, AFTER, SRC, WEIGHT, DIST = range(FIELDS)

    ctx = ExitStack()
    with ctx:
        def sb(name, shape, dt=F32):
            return ctx.enter_context(nc.sbuf_tensor(name, shape, dt))

        def sem(name):
            return ctx.enter_context(nc.semaphore(name))

        def lane(name):
            return Lane(sem(name))

        VE = Engine("vector", sem("vector_done"))
        AE = Engine("scalar", sem("scalar_done"))
        PE = Engine("tensor", sem("tensor_done"))
        GE = Engine("gpsimd", sem("gpsimd_done"))
        SP = Engine("sync", sem("sync_done"))

        edge_tiles = nc.dram_tensor("edge_tiles", [NT, FIELDS * P], I32).ap()
        plan_rows = nc.dram_tensor("plan_rows", [2, SR * P], I32).ap()
        step_masks = nc.dram_tensor("step_masks", [3, SR * P, P], F32).ap()
        table = [nc.dram_tensor(f"table{i}", [NP, D], F32).ap() for i in range(2)]

        ident = sb("ident", [P, P])
        iota_f = sb("iota_f", [P, P])
        iota_b = sb("iota_b", [P, P], BF16)
        X = sb("X", [P, NB, D])
        V = sb("V", [P, NB, D])
        ACCW = 3 * 3 * HEADS
        SOFT = 3 * HEADS
        work = sb("work", [P, max(QUADS * NB * ACCW, 2 * NB * D)])
        AGG = work[:, 0:NB * D].rearrange("p (b d) -> p b d", b=NB)
        Y = work[:, NB * D:2 * NB * D].rearrange("p (b d) -> p b d", b=NB)
        soft_acc = work[:, 0:QUADS * NB * ACCW].rearrange("p (q b c) -> p q b c", q=QUADS, b=NB)
        rel_col = sb("rel_col", [P, SR * P])
        end_col = sb("end_col", [P, SR * P])
        ew_col = sb("ew_col", [P, SR * P])
        src_col = sb("src_col", [P, SR * P], I32)
        plan_reg = sb("plan_reg", [1, 2, NS], I32)
        dst_col = sb("dst_col", [P, SR * P], I32)
        weights = sb("weights", [P, 12, P])
        WI = {n: i for i, n in enumerate(["W0", "W1", "W2", "G1", "G2", "Wq", "Wk", "Wv", "Wo", "Wl", "Wr"])}
        bias = sb("bias", [P, 9, P])
        BI = {n: i for i, n in enumerate(["b0", "b1", "b2", "c1", "c2", "bq", "bv", "bo", "bl"])}
        bk_col = sb("bk_col", [P, 1])
        head_sum = sb("head_sum", [P, 3, 32])
        dis = sb("dis", [P, NB])
        deg = sb("deg", [P, NB])
        inv_cnt = sb("inv_cnt", [P, NB])
        ln_stat = sb("ln_stat", [P, NB, 6])
        ln_mv = sb("ln_mv", [P, NB, 2])
        ln_rstd = sb("ln_rstd", [P, NB])
        ln_shift = sb("ln_shift", [P, NB])

        SLOTS = 12
        HOTS = 4
        gath = sb("gath", [P, SLOTS, D])
        hot = sb("hot", [P, HOTS, P])
        NX = 14088
        pool = sb("pool", [P, NX])

        psum = ctx.enter_context(nc.psum_tensor("psum", [P, PS_BANKS, BANK], F32))

        slot_lane = [lane(f"slot{i}") for i in range(SLOTS)]
        setup_lane = [lane(f"setup{i}") for i in range(24)]
        table_lane = [lane(f"table_lane{i}") for i in range(4)]
        out_lane = [lane(f"out_lane{i}") for i in range(4)]

        iota_tok = GE.do(lambda e: e.iota(iota_f[:, :], pattern=[[1, P]], base=0, channel_multiplier=0,
                                          allow_small_or_imprecise_dtypes=True))
        step_no = sb("step_no", [P, SR])
        step_no_tok = GE.do(lambda e: e.iota(step_no[:, :], pattern=[[P, SR]], base=0, channel_multiplier=1,
                                             allow_small_or_imprecise_dtypes=True))
        part_no = sb("part_no", [P, 1])
        part_tok = GE.do(lambda e: e.iota(part_no[:, :], pattern=[[0, 1]], base=0, channel_multiplier=1,
                                          allow_small_or_imprecise_dtypes=True))
        VE.wait(iota_tok, part_tok)
        ident_tok = VE.do(lambda e: e.tensor_scalar(ident[:, :], iota_f[:, :], part_no[:, 0:1], None, ALU.is_equal))
        iota_b_tok = VE.do(lambda e: e.tensor_copy(iota_b[:, :], iota_f[:, :]))
        ones_row = sb("ones_row", [1, P])
        ones_tok = VE.do(lambda e: e.memset(ones_row[:, :], 1.0))
        minus_row = sb("minus_row", [1, P], I32)
        minus_tok = VE.do(lambda e: e.memset(minus_row[:, :], -1))

        hs_tok = GE.do(lambda e: e.memset(head_sum[:, :, :], 0.0))
        for k in range(3):
            part = head_sum[:, k, HEADS * k:HEADS * (k + 1)]
            GE.wait(hs_tok)
            hs_tok = GE.do(lambda e, part=part: e.memset(part, SCALE))
            for base, mult, step in ((0, 1, -HEAD_DIM), (HEAD_DIM - 1, -1, HEAD_DIM)):
                GE.wait(hs_tok)
                hs_tok = GE.do(lambda e, part=part, base=base, mult=mult, step=step: e.affine_select(
                    out=part, in_=part, compare_op=ALU.is_ge, fill=0.0, base=base, pattern=[[step, HEADS]],
                    channel_multiplier=mult))
        head_sum_tok = hs_tok

        setup = iter(setup_lane)
        raw = {DST: dst_in, SRC: src_in, WEIGHT: ew_in.bitcast(I32),
               DIST: dist_in.rearrange("e a -> (e a)").bitcast(I32)}
        WHOLE = (NT - 1) * P
        first_last = pool[0:1, 0:2 * NT].bitcast(I32).rearrange("a (k t) -> a k t", k=2)
        fl_lane = next(setup)
        SP.dma(lambda e: e.dma_start(first_last[:, 0, 0:NT], dst_in.rearrange("(a e) -> a e", a=1)[:, 0:WHOLE + 1:P],
                                     allow_slow_non_contiguous=True), fl_lane)
        SP.dma(lambda e: e.dma_start(first_last[:, 1, 0:NT - 1], dst_in.rearrange("(a e) -> a e", a=1)[:, P - 1:WHOLE:P],
                                     allow_slow_non_contiguous=True), fl_lane)
        fl_tok = SP.dma(lambda e: e.dma_start(first_last[:, 1, NT - 1:NT], dst_in[E - 1:E].rearrange("(a e) -> a e", a=1)),
                        fl_lane)
        tiles_lane = next(setup)
        tile_fields = edge_tiles.rearrange("t (f e) -> t f e", f=FIELDS)
        for field in (DST, SRC, WEIGHT, DIST):
            flat = raw[field]
            SP.dma(lambda e, field=field, flat=flat: e.dma_start(
                tile_fields[0:NT - 1, field, :], flat[0:WHOLE].rearrange("(t e) -> t e", e=P)), tiles_lane)
            skip = OVER if field == DST else 0
            SP.dma(lambda e, field=field, flat=flat, skip=skip: e.dma_start(
                tile_fields[NT - 1:NT, field, skip:P], flat[E - P + skip:E].rearrange("(t e) -> t e", t=1)), tiles_lane)
        before = edge_tiles.rearrange("t (f e) -> t f e", f=FIELDS)[:, BEFORE, :]
        after = edge_tiles.rearrange("t (f e) -> t f e", f=FIELDS)[:, AFTER, :]
        SP.dma(lambda e: e.dma_start(before[1:NT - 1, :], dst_in[P - 1:WHOLE - 1].rearrange("(t e) -> t e", e=P)), tiles_lane)
        SP.dma(lambda e: e.dma_start(before[0:1, 1:P], dst_in[0:P - 1].rearrange("(t e) -> t e", t=1)), tiles_lane)
        SP.dma(lambda e: e.dma_start(before[NT - 1:NT, :], dst_in[E - P - 1:E - 1].rearrange("(t e) -> t e", t=1)), tiles_lane)
        SP.dma(lambda e: e.dma_start(after[0:NT - 1, :], dst_in[1:WHOLE + 1].rearrange("(t e) -> t e", e=P)), tiles_lane)
        SP.dma(lambda e: e.dma_start(after[NT - 1:NT, 0:P - 1], dst_in[E - P + 1:E].rearrange("(t e) -> t e", t=1)), tiles_lane)
        SP.wait(minus_tok)
        if OVER:
            SP.dma(lambda e: e.dma_start(tile_fields[NT - 1:NT, DST, 0:OVER], minus_row[:, 0:OVER]), tiles_lane)
        SP.dma(lambda e: e.dma_start(before[0:1, 0:1], minus_row[:, 0:1]), tiles_lane)
        tiles_tok = SP.dma(lambda e: e.dma_start(after[NT - 1:NT, P - 1:P], minus_row[:, 0:1]), tiles_lane)

        x_lane = next(setup)
        VE_x0 = VE.do(lambda e: e.memset(X[:, NB - 1, :], 0.0))
        SP.dma(lambda e: e.dma_start(X[:, 0:NB - 1, :], x_in[0:(NB - 1) * P, :].rearrange("(b p) d -> p b d", p=P)), x_lane)
        SP.wait(VE_x0)
        x_tok = SP.dma(lambda e: e.dma_start(X[0:LAST, NB - 1, :], x_in[(NB - 1) * P:N, :]), x_lane)
        w_lane = next(setup)
        for name, w in dict(W0=W0, W1=W1, W2=W2, G1=G1, G2=G2, Wq=Wq, Wk=Wk, Wv=Wv, Wo=Wo, Wl=Wl, Wr=Wr).items():
            AE.dma(lambda e, name=name, w=w: e.dma_start(weights[:, WI[name], :], w), w_lane)
        for name, b in dict(b0=b0, b1=b1, b2=b2, c1=c1, c2=c2, bq=bq, bv=bv, bo=bo, bl=bl).items():
            AE.dma(lambda e, name=name, b=b: e.dma_start(
                bias[:, BI[name], :], spread(b.rearrange("(a d) -> a d", a=1), 0, P)), w_lane)
        lam_col = sb("lam_col", [P, 1])
        AE.dma(lambda e: e.dma_start(lam_col[:, :], spread(lam.rearrange("(a d) -> a d", a=1), 0, P)), w_lane)
        w_tok = AE.dma(lambda e: e.dma_start(bk_col[:, :], bk.rearrange("(d a) -> d a", a=1)), w_lane)

        o = 2 * NT
        row = {}
        for name in ("fb", "lb", "spread", "off", "gap", "dgap", "ones"):
            row[name] = pool[0:1, o:o + NT]
            o += NT
        fl_block = pool[0:1, o:o + 2 * NT].bitcast(I32).rearrange("a (k t) -> a k t", k=2)
        o += 2 * NT
        ones_nt = VE.do(lambda e: e.memset(row["ones"], 1.0))
        VE.wait(fl_tok)
        t = VE.do(lambda e: e.tensor_scalar(fl_block, first_last, P.bit_length() - 1, None, ALU.arith_shift_right))
        VE.wait(t)
        VE.do(lambda e: e.tensor_copy(row["fb"], fl_block[:, 0, :]))
        t = VE.do(lambda e: e.tensor_copy(row["lb"], fl_block[:, 1, :]))
        VE.wait(t)
        t = VE.do(lambda e: e.tensor_tensor(row["spread"], row["lb"], row["fb"], ALU.subtract))
        VE.wait(t)
        t = VE.do(lambda e: e.tensor_scalar(row["spread"], row["spread"], 1.0, None, ALU.add))
        VE.wait(t, ones_nt)
        t = VE.do(lambda e: e.tensor_tensor_scan(row["off"], row["ones"], row["spread"], 0.0, ALU.mult, ALU.add))
        VE.wait(t)
        t = VE.do(lambda e: e.tensor_tensor(row["off"], row["off"], row["spread"], ALU.subtract))
        VE.wait(t)
        t = VE.do(lambda e: e.tensor_tensor(row["gap"], row["fb"], row["off"], ALU.subtract))
        VE.wait(t)
        VE.do(lambda e: e.tensor_copy(row["dgap"][:, 0:1], row["gap"][:, 0:1]))
        plan_tok = VE.do(lambda e: e.tensor_tensor(row["dgap"][:, 1:NT], row["gap"][:, 1:NT], row["gap"][:, 0:NT - 1],
                                                   ALU.subtract))
        off_all = pool[:, o:o + NT]
        dgap_all = pool[:, o + NT:o + 2 * NT]
        step_junk = pool[:, o + 2 * NT:o + 3 * NT]
        ROWS = o + 3 * NT
        assert ROWS <= NX
        PE.wait(plan_tok)
        copies = []
        bank = 0
        for name, dest in (("off", off_all), ("dgap", dgap_all)):
            for lo in range(0, NT, BANK):
                hi = min(NT, lo + BANK)
                t = PE.do(lambda e, name=name, lo=lo, hi=hi, bank=bank: e.matmul(
                    psum[:, bank, 0:hi - lo], ones_row[:, 0:P], row[name][:, lo:hi], start=True, stop=True))
                VE.wait(t)
                copies.append(VE.do(lambda e, dest=dest, lo=lo, hi=hi, bank=bank: e.tensor_copy(
                    dest[:, lo:hi], psum[:, bank, 0:hi - lo])))
                bank += 1
        VE.wait(copies[-1], step_no_tok)
        tile_of = sb("tile_of", [P, SR])
        block_of = sb("block_of", [P, SR])
        t = None
        for i in range(SR):
            t = VE.do(lambda e, i=i: e.tensor_scalar(step_junk, off_all, step_no[:, i:i + 1], None, ALU.is_le, ALU.add,
                                                     accum_out=tile_of[:, i:i + 1]))
            VE.wait(t)
            t = VE.do(lambda e, i=i: e.scalar_tensor_tensor(step_junk, off_all, step_no[:, i:i + 1], dgap_all, ALU.is_le,
                                                            ALU.mult, accum_out=block_of[:, i:i + 1]))
            VE.wait(t)
        t = VE.do(lambda e: e.tensor_scalar(tile_of[:, :], tile_of[:, :], -1.0, None, ALU.add))
        t = VE.do(lambda e: e.tensor_tensor(block_of[:, :], block_of[:, :], step_no[:, :], ALU.add))
        VE.wait(t)
        tile_idx = sb("tile_idx", [P, SR], I32)
        plan_cols = sb("plan_cols", [P, 2, SR])
        tile_tok = VE.do(lambda e: e.tensor_copy(tile_idx[:, :], tile_of[:, :]))
        VE.do(lambda e: e.tensor_scalar(plan_cols[:, 0, :], block_of[:, :], float(NB - 1), None, ALU.min))
        t = VE.do(lambda e: e.tensor_scalar(plan_cols[:, 1, :], tile_of[:, :], float(P), float(E - P), ALU.mult, ALU.min))
        base_of = sb("base_of", [P, SR])
        base_tok = VE.do(lambda e: e.tensor_scalar(base_of[:, :], block_of[:, :], float(P), None, ALU.mult))
        PE.wait(t, ident_tok)
        bank = 4
        t = PE.do(lambda e: e.transpose(psum[0:2 * SR, bank, 0:P], plan_cols[:, :, :].rearrange("p k s -> p (k s)"),
                                        ident[:, :]))
        VE.wait(t)
        plan_t = sb("plan_t", [2 * SR, P], I32)
        t = VE.do(lambda e: e.tensor_copy(plan_t[:, :], psum[0:2 * SR, 4, 0:P]))
        SP.wait(t)
        pl = next(setup)
        t = SP.dma(lambda e: e.dma_start(plan_rows.rearrange("k (s p) -> (k s) p", p=P), plan_t[:, :]), pl)
        SP.wait(t)
        plan_reg_tok = SP.dma(lambda e: e.dma_start(plan_reg[:, :, :], plan_rows.rearrange("(a k) s -> a k s", a=1)[:, :, 0:NS]), next(setup))

        step_rows = work[:, 0:SR * FIELDS * P].bitcast(I32).rearrange("p (s f) -> p s f", s=SR)
        GE.wait(tile_tok, tiles_tok)
        rows_tok = []
        for i in range(SR):
            rows_tok.append(GE.dma(lambda e, i=i: e.indirect_dma_start(
                out=step_rows[:, i, :], out_offset=None, in_=edge_tiles[:, :],
                in_offset=bass.IndirectOffsetOnAxis(ap=tile_idx[:, i:i + 1], axis=0),
                bounds_check=NT - 1, oob_is_err=False), slot_lane[i]))
        o = ROWS - 3 * NT
        def rows_f(k):
            return pool[:, k * SR * P:(k + 1) * SR * P].rearrange("p (s e) -> p s e", s=SR)
        rel, valid, start, endr, lmask, srcf, tmp = (rows_f(k) for k in range(7))
        raw_field = step_rows.rearrange("p s (f e) -> p s f e", f=FIELDS)
        VE.wait(*rows_tok)
        VE.wait(base_tok)
        t = VE.do(lambda e: e.tensor_copy(tmp, raw_field[:, :, DST, :]))
        VE.do(lambda e: e.tensor_copy(srcf, raw_field[:, :, SRC, :]))
        for i in range(SR):
            VE.wait(t)
            t2 = VE.do(lambda e, i=i: e.tensor_scalar(rel[:, i, :], tmp[:, i, :], base_of[:, i:i + 1], None, ALU.subtract))
        VE.wait(t2)
        t = VE.do(lambda e: e.tensor_scalar(rel, rel, -1.0, float(P), ALU.max, ALU.min))
        VE.wait(t)
        t = VE.do(lambda e: e.tensor_scalar(valid, rel, 0.0, None, ALU.is_ge))
        VE.wait(t)
        t = VE.do(lambda e: e.scalar_tensor_tensor(valid, rel, float(P) - 0.5, valid, ALU.is_lt, ALU.mult))
        VE.wait(t)
        VE.do(lambda e: e.tensor_scalar(lmask, valid, -1.0, BIG, ALU.add, ALU.mult))
        t = VE.do(lambda e: e.tensor_copy(start, raw_field[:, :, BEFORE, :]))
        t = VE.do(lambda e: e.tensor_copy(endr, raw_field[:, :, AFTER, :]))
        VE.wait(t)
        VE.do(lambda e: e.tensor_tensor(start, start, tmp, ALU.not_equal))
        t = VE.do(lambda e: e.tensor_tensor(endr, endr, tmp, ALU.not_equal))
        forced = sb("forced", [P, SR])
        f = VE.do(lambda e: e.tensor_scalar(forced[:, :], step_no[:, :], float(QS - 1), None, ALU.is_equal))
        for q in range(1, QUADS):
            VE.wait(f)
            f = VE.do(lambda e, q=q: e.scalar_tensor_tensor(forced[:, :], step_no[:, :], float(QS * (q + 1) - 1), forced[:, :],
                                                            ALU.is_equal, ALU.max))
        VE.wait(f, t)
        t = VE.do(lambda e: e.tensor_tensor(endr[:, :, P - 1], endr[:, :, P - 1], forced[:, :], ALU.max))
        VE.wait(t)
        VE.do(lambda e: e.tensor_tensor(start, start, valid, ALU.mult))
        t = VE.do(lambda e: e.tensor_tensor(endr, endr, valid, ALU.mult))
        VE.wait(t)
        t = VE.do(lambda e: e.tensor_scalar(start, start, -BIG, None, ALU.mult))
        t = VE.do(lambda e: e.scalar_tensor_tensor(endr, rel, 1.0, endr, ALU.add, ALU.mult))
        VE.wait(t)
        VE.do(lambda e: e.tensor_scalar(endr, endr, -1.0, None, ALU.add))
        rows_done = VE.do(lambda e: e.tensor_scalar(tmp, tmp, 0.0, None, ALU.max))
        dist_f = step_rows.bitcast(F32).rearrange("p s (f e) -> p s f e", f=FIELDS)[:, :, DIST, :]
        lam_row = hot[:, 0, :]
        VE.wait(w_tok)
        lt = VE.do(lambda e: e.tensor_scalar(lam_row, iota_f[:, :], 0.0, lam_col[:, 0:1], ALU.mult, ALU.add))
        att = rows_f(7)
        GE.wait(lt)
        for i in range(SR):
            att_tok = GE.do(lambda e, i=i: e.tensor_tensor(att[:, i, :], dist_f[:, i, :], lam_row, ALU.pow))
        SP.wait(rows_done, att_tok)
        masks_lane = next(setup)
        for k, arr in enumerate((lmask, start, att)):
            masks_tok = SP.dma(lambda e, k=k, arr=arr: e.dma_start(
                step_masks[k].rearrange("(s p) e -> p s e", p=P), arr), masks_lane)
        ew_f = step_rows.bitcast(F32).rearrange("p s (f e) -> p s f e", f=FIELDS)[:, :, WEIGHT, :]
        PE.wait(rows_done)
        free = {}
        n = 0
        for arr, dest in ((rel, rel_col), (ew_f, ew_col), (srcf, src_col), (endr, end_col), (tmp, dst_col)):
            for lo in range(0, SR, GROUP):
                hi = min(SR, lo + GROUP)
                b = n % 4
                PE.wait(free.get(b))
                for i in range(lo, hi):
                    t = PE.do(lambda e, arr=arr, i=i, lo=lo, b=b: e.transpose(
                        psum[:, b, (i - lo) * P:(i - lo + 1) * P], arr[:, i, :], ident[:, :]))
                VE.wait(t)
                free[b] = cols_tok = VE.do(lambda e, dest=dest, lo=lo, hi=hi, b=b: e.tensor_copy(
                    dest[:, lo * P:hi * P], psum[:, b, 0:(hi - lo) * P]))
                n += 1

        PARTS = 4
        PER = BANK // PARTS
        SRW = SR * P
        parts = pool[:, 0:SRW * PARTS // 2].bitcast(BF16).rearrange("p (s k) -> p s k", k=PARTS)
        rest = pool[:, SRW * 2:SRW * 3]
        VE.wait(cols_tok, masks_tok)
        t = VE.do(lambda e: e.tensor_copy(parts[:, :, 0], ew_col[:, :]))
        VE.do(lambda e: e.memset(parts[:, :, 3], 1.0))
        VE.wait(t)
        t = VE.do(lambda e: e.tensor_tensor(rest, ew_col[:, :], parts[:, :, 0], ALU.subtract))
        VE.wait(t)
        t = VE.do(lambda e: e.tensor_copy(parts[:, :, 1], rest))
        VE.wait(t)
        t = VE.do(lambda e: e.tensor_tensor(rest, rest, parts[:, :, 1], ALU.subtract))
        VE.wait(t)
        parts_tok = VE.do(lambda e: e.tensor_copy(parts[:, :, 2], rest))
        hot_b = pool[:, SRW * 3:SRW * 3 + 8 * P // 2].bitcast(BF16).rearrange("p (k n) -> p k n", k=8)
        deg_of = pool[:, SRW * 4:SRW * 6].rearrange("p (k s) -> p k s", k=2)
        HB = 8
        PE.wait(parts_tok)
        VE.wait(iota_b_tok)
        pe_tok = []
        z = VE.do(lambda e: e.memset(deg_of[:, :, NS:SRW], 0.0))
        PE.wait(*free.values())
        for s in range(NS):
            if s >= HB:
                VE.wait(pe_tok[s - HB])
            t = VE.do(lambda e, s=s: e.tensor_scalar(hot_b[:, s % HB, :], iota_b[:, :], rel_col[:, s:s + 1], None,
                                                     ALU.is_equal))
            PE.wait(t)
            pe_tok.append(PE.do(lambda e, s=s: e.matmul(
                psum[:, s // PER, (s % PER) * PARTS:(s % PER + 1) * PARTS], hot_b[:, s % HB, :], parts[:, s, :],
                start=True, stop=True)))
        VE.wait(pe_tok[-1])
        for lo in range(0, NS, PER):
            n = min(PER, NS - lo)
            view = psum[:, lo // PER, 0:n * PARTS].rearrange("p (s k) -> p s k", k=PARTS)
            VE.do(lambda e, lo=lo, n=n, view=view: e.tensor_reduce(deg_of[:, 0, lo:lo + n], view[:, :, 0:3], AX.X, ALU.add))
            deg_tok = VE.do(lambda e, lo=lo, n=n, view=view: e.tensor_copy(deg_of[:, 1, lo:lo + n], view[:, :, 3]))
        block_hot = pool[:, SRW * 6:SRW * 6 + SR * NB].rearrange("p (s b) -> p s b", s=SR)
        for i in range(SR):
            bh_tok = VE.do(lambda e, i=i: e.tensor_scalar(block_hot[:, i, :], iota_f[:, 0:NB], block_of[:, i:i + 1], None,
                                                          ALU.is_equal))
        deg_t = pool[:, SRW * 3:SRW * 4].rearrange("p (s n) -> p s n", s=SR)
        PE.wait(deg_tok, bh_tok)
        for k in range(2):
            for lo in range(0, SR, GROUP):
                hi = min(SR, lo + GROUP)
                for i in range(lo, hi):
                    t = PE.do(lambda e, i=i, lo=lo, k=k: e.transpose(
                        psum[:, lo // GROUP, (i - lo) * P:(i - lo + 1) * P], deg_of[:, k, i * P:(i + 1) * P], ident[:, :]))
                VE.wait(t)
                t = VE.do(lambda e, lo=lo, hi=hi: e.tensor_copy(
                    deg_t[:, lo:hi, :], psum[:, lo // GROUP, 0:(hi - lo) * P].rearrange("p (s n) -> p s n", n=P)))
            PE.wait(t)
            for i in range(SR):
                t = PE.do(lambda e, i=i, k=k: e.matmul(psum[:, 2 + k, 0:NB], deg_t[:, i, :], block_hot[:, i, :],
                                                       start=(i == 0), stop=(i == SR - 1)))
            VE.wait(t)
            PE.wait(t)
        cnt_tok = VE.do(lambda e: e.tensor_scalar(inv_cnt[:, :], psum[:, 3, 0:NB], 1.0, None, ALU.max))
        t = VE.do(lambda e: e.tensor_scalar(deg[:, :], psum[:, 2, 0:NB], 1.0, None, ALU.add))
        VE.wait(t, cnt_tok)
        VE.do(lambda e: e.reciprocal(inv_cnt[:, :], inv_cnt[:, :]))
        t = VE.do(lambda e: e.tensor_scalar(dis[:, :], deg[:, :], 1e-30, None, ALU.max))
        AE.wait(t)
        t = AE.do(lambda e: e.activation(dis[:, :], dis[:, :], ACT.Sqrt))
        VE.wait(t)
        t = VE.do(lambda e: e.reciprocal(dis[:, :], dis[:, :]))
        VE.wait(t)
        dis_tok = VE.do(lambda e: e.scalar_tensor_tensor(dis[:, :], deg[:, :], 0.0, dis[:, :], ALU.is_gt, ALU.mult))

        PE.wait(w_tok, dis_tok)
        for k, name in enumerate(["Wq", "Wk", "Wv", "Wo", "Wl", "Wr"]):
            t = PE.do(lambda e, name=name, k=k: e.transpose(psum[:, k % 4, 0:P], weights[:, WI[name], :], ident[:, :]))
            AE.wait(t)
            t = AE.do(lambda e, name=name, k=k: e.activation(weights[:, WI[name], :], psum[:, k % 4, 0:P], ACT.Copy))
            PE.wait(t)
        wt_tok = t

        groups = [(lo, min(NB, lo + GROUP)) for lo in range(0, NB, GROUP)]
        tr = pool[:, 0:4 * BANK].rearrange("p (k n) -> p k n", k=4)
        stage = pool[:, 4 * BANK:8 * BANK].rearrange("p (k n) -> p k n", k=4)
        stage_free = [None] * 4
        tr_free = [None] * 4
        bank_free = [None] * PS_BANKS

        def layer_norm(dest, ready):
            VE.wait(*ready)
            for b in range(NB):
                t = VE.do(lambda e, b=b: e.bn_stats(ln_stat[:, b, :], X[:, b, :]))
            VE.wait(t)
            for b in range(NB):
                t = VE.do(lambda e, b=b: e.bn_aggr(ln_mv[:, b, :], ln_stat[:, b, :]))
            VE.wait(t)
            t = VE.do(lambda e: e.tensor_scalar(ln_rstd[:, :], ln_mv[:, :, 1], LN_EPS, None, ALU.add))
            AE.wait(t)
            t = AE.do(lambda e: e.activation(ln_rstd[:, :], ln_rstd[:, :], ACT.Sqrt))
            VE.wait(t)
            t = VE.do(lambda e: e.reciprocal(ln_rstd[:, :], ln_rstd[:, :]))
            VE.wait(t)
            t = VE.do(lambda e: e.scalar_tensor_tensor(ln_shift[:, :], ln_mv[:, :, 0], -1.0, ln_rstd[:, :], ALU.mult, ALU.mult))
            AE.wait(t)
            for b in range(NB):
                t = AE.do(lambda e, b=b: e.activation(dest[:, b, :], X[:, b, :], ACT.Relu, bias=ln_shift[:, b:b + 1],
                                                      scale=ln_rstd[:, b:b + 1]))
            return t

        def dense(products, ready, post):
            PE.wait(*ready)
            for g, (lo, hi) in enumerate(groups):
                n = hi - lo
                moved = []
                for k, (source, _) in enumerate(products):
                    b = 2 * k + g % 2
                    PE.wait(bank_free[b])
                    for i in range(n):
                        t = PE.do(lambda e, source=source, i=i, b=b, lo=lo: e.transpose(
                            psum[:, b, i * P:(i + 1) * P], source[:, lo + i, :], ident[:, :]))
                    AE.wait(t, tr_free[b])
                    bank_free[b] = AE.do(lambda e, b=b, n=n: e.activation(tr[:, b, 0:n * P], psum[:, b, 0:n * P], ACT.Copy))
                    moved.append(bank_free[b])
                PE.wait(bank_free[4 + g % 2], *moved)
                for i in range(n):
                    for k, (_, w) in enumerate(products):
                        b = 2 * k + g % 2
                        t = PE.do(lambda e, i=i, k=k, b=b, w=w, g=g: e.matmul(
                            psum[:, 4 + g % 2, i * P:(i + 1) * P], tr[:, b, i * P:(i + 1) * P], weights[:, WI[w], :],
                            start=(k == 0), stop=(k == len(products) - 1)))
                for k in range(len(products)):
                    tr_free[2 * k + g % 2] = t
                view = psum[:, 4 + g % 2, 0:n * P].rearrange("p (b d) -> p b d", b=n)
                bank_free[4 + g % 2] = post(g, lo, hi, view, t)

        def bias_of(name, n):
            return spread(bias[:, BI[name], :].rearrange("p (a d) -> p a d", a=1), 1, n)

        def store_table(dest, source, g, lo, hi, ready):
            SP.wait(ready)
            return SP.dma(lambda e: e.dma_start(dest[lo * P:hi * P, :].rearrange("(b p) d -> p b d", p=P), source),
                          table_lane[g % 4])

        def col_bc(col, lo, hi):
            return spread(col[:, lo:hi].rearrange("p (b a) -> p b a", a=1), 2, D)

        plan_ready = plan_reg_tok

        def aggregate(source, stored, weighted, agg_free):
            VE.wait(plan_ready, *agg_free)
            acc_tok = VE.do(lambda e: e.memset(AGG, 0.0))
            GE.wait(*stored)
            PE.wait(*agg_free)
            mm = []

            def gather(s):
                if s >= SLOTS:
                    GE.wait(mm[s - SLOTS])
                return GE.dma(lambda e: e.indirect_dma_start(
                    out=gath[:, s % SLOTS, :], out_offset=None, in_=source[:, :],
                    in_offset=bass.IndirectOffsetOnAxis(ap=src_col[:, s:s + 1], axis=0),
                    bounds_check=NP - 1, oob_is_err=False), slot_lane[s % SLOTS])

            def one_hot(s):
                if s >= HOTS:
                    VE.wait(mm[s - HOTS])
                return VE.do(lambda e: e.tensor_scalar(
                    hot[:, s % HOTS, :], iota_f[:, :], rel_col[:, s:s + 1], ew_col[:, s:s + 1] if weighted else None,
                    ALU.is_equal, ALU.mult if weighted else ALU.bypass))

            gathered = []
            hots = []
            for s in range(NS + 2):
                if s < NS:
                    gathered.append(gather(s))
                    hots.append(one_hot(s))
                    PE.wait(hots[s], gathered[s])
                    PE.wait(bank_free[s % 4])
                    mm.append(PE.do(lambda e, s=s: e.matmul(psum[:, s % 4, 0:D], hot[:, s % HOTS, :], gath[:, s % SLOTS, :],
                                                            start=True, stop=True)))
                if s >= 2:
                    a = s - 2
                    VE.wait(mm[a], acc_tok)

                    def add(e, a=a):
                        b = e.value_load(plan_reg[0:1, 0, a:a + 1], min_val=0, max_val=NB - 1)
                        return e.tensor_tensor(AGG[:, bass.ds(b, 1), :], AGG[:, bass.ds(b, 1), :],
                                               psum[:, a % 4, 0:D].rearrange("p (a d) -> p a d", a=1), ALU.add)
                    acc_tok = VE.do(add)
                    bank_free[a % 4] = acc_tok
            return acc_tok

        tok = layer_norm(AGG, [x_tok, cols_tok, att_tok, dis_tok])

        def gcn_table(which):
            def post(g, lo, hi, view, t):
                VE.wait(t, dis_tok)
                t = VE.do(lambda e: e.tensor_tensor(Y[:, lo:hi, :], view, col_bc(dis, lo, hi), ALU.mult))
                stored.append(store_table(table[which], Y[:, lo:hi, :], g, lo, hi, t))
                return t
            return post

        for layer, (w, b) in enumerate((("W0", "b0"), ("W1", "b1"), ("W2", "b2"))):
            stored = []
            dense([(AGG, w)], [tok, wt_tok], gcn_table(layer % 2))
            end = aggregate(table[layer % 2], stored[-4:], True, [(PE.done, PE.count)])
            for lo, hi in groups:
                VE.wait(end)
                t = VE.do(lambda e, lo=lo, hi=hi: e.tensor_tensor(AGG[:, lo:hi, :], AGG[:, lo:hi, :], Y[:, lo:hi, :], ALU.add))
                VE.wait(t)
                t = VE.do(lambda e, lo=lo, hi=hi: e.tensor_tensor(AGG[:, lo:hi, :], AGG[:, lo:hi, :], col_bc(dis, lo, hi), ALU.mult))
                VE.wait(t)
                t = VE.do(lambda e, lo=lo, hi=hi, b=b: e.tensor_tensor(AGG[:, lo:hi, :], AGG[:, lo:hi, :], bias_of(b, hi - lo), ALU.add))
                VE.wait(t)
                if layer < 2:
                    tok = VE.do(lambda e, lo=lo, hi=hi: e.tensor_scalar(AGG[:, lo:hi, :], AGG[:, lo:hi, :], 0.0, None, ALU.max))
                else:
                    tok = VE.do(lambda e, lo=lo, hi=hi: e.scalar_tensor_tensor(X[:, lo:hi, :], AGG[:, lo:hi, :], 0.0, X[:, lo:hi, :],
                                                                               ALU.max, ALU.add))

        tok = layer_norm(Y, [tok])
        stored = [store_table(table[1], Y[:, lo:hi, :], g, lo, hi, tok) for g, (lo, hi) in enumerate(groups)]
        end = aggregate(table[1], stored[-4:], True, [tok])
        VE.wait(end)
        for lo, hi in groups:
            tok = VE.do(lambda e, lo=lo, hi=hi: e.tensor_tensor(AGG[:, lo:hi, :], AGG[:, lo:hi, :], Y[:, lo:hi, :], ALU.add))

        def gin_hidden(g, lo, hi, view, t):
            VE.wait(t)
            t = VE.do(lambda e: e.tensor_tensor(Y[:, lo:hi, :], view, bias_of("c1", hi - lo), ALU.add))
            VE.wait(t)
            hidden.append(VE.do(lambda e: e.tensor_scalar(Y[:, lo:hi, :], Y[:, lo:hi, :], 0.0, None, ALU.max)))
            return t

        def gin_out(g, lo, hi, view, t):
            VE.wait(t)
            free = VE.do(lambda e: e.tensor_tensor(AGG[:, lo:hi, :], view, bias_of("c2", hi - lo), ALU.add))
            VE.wait(free)
            hidden.append(VE.do(lambda e: e.tensor_tensor(X[:, lo:hi, :], X[:, lo:hi, :], AGG[:, lo:hi, :], ALU.add)))
            return free

        hidden = []
        dense([(AGG, "G1")], [tok], gin_hidden)
        dense([(Y, "G2")], [hidden[-1]], gin_out)
        tok = hidden[-1]

        tok = layer_norm(AGG, [tok])
        stored = []

        def q_table(g, lo, hi, view, t):
            VE.wait(t, stage_free[g % 4])
            n = hi - lo
            t = VE.do(lambda e: e.tensor_tensor(stage[:, g % 4, 0:n * P].rearrange("p (b d) -> p b d", b=n), view,
                                                bias_of("bq", n), ALU.add))
            stage_free[g % 4] = store_table(table[0], stage[:, g % 4, 0:n * P].rearrange("p (b d) -> p b d", b=n), g, lo, hi, t)
            stored.append(stage_free[g % 4])
            return t

        def v_nodes(g, lo, hi, view, t):
            VE.wait(t)
            v_tok.append(VE.do(lambda e: e.tensor_tensor(V[:, lo:hi, :], view, bias_of("bv", hi - lo), ALU.add)))
            return v_tok[-1]

        v_tok = []
        dense([(AGG, "Wq")], [tok], q_table)
        dense([(AGG, "Wv")], [tok], v_nodes)
        qv_done = [(PE.done, PE.count), (AE.done, AE.count), (VE.done, VE.count)] + stored[-4:]

        o = 0

        def take(n, *shape):
            nonlocal o
            view = pool[:, o:o + n * math.prod(shape)]
            o += n * math.prod(shape)
            names = [f"a{i}" for i in range(len(shape) + 1)]
            return view.rearrange(f"p ({' '.join(names)}) -> p {' '.join(names)}",
                                  **{k: s for k, s in zip(names, (n,) + shape)})

        q_src = gath
        SLOT2 = 8
        q_dst = take(SLOT2, D)
        attr = take(SLOT2, D)
        attr_t = take(2, BANK)
        qsrc_t = take(2, BANK)
        qdst_t = take(2, BANK)
        prod = take(3, BANK)
        masks = take(2, 3, BANK)
        m_run = take(2, BANK + 1)
        den_run = take(2, BANK)
        num_run = take(2, BANK)
        expo = take(1, BANK)
        ends = take(2, 3 * P)
        assert o <= NX, o

        ROUNDS = QS // GROUP
        qd_lane = [lane(f"qdst{i}") for i in range(SLOT2)]
        at_lane = [lane(f"attr{i}") for i in range(SLOT2)]
        mask_lane = [lane(f"mask{i}") for i in range(2)]
        B_ATTR, B_QS, B_QD, B_K, B_LOGIT, B_END, B_SUM = range(7)

        VE.wait(*qv_done)
        VE.do(lambda e: e.memset(soft_acc, 0.0))
        VE.do(lambda e: e.memset(m_run[:, 1, BANK:BANK + 1], -BIG))
        VE.do(lambda e: e.memset(den_run[:, 1, BANK - 1:BANK], 0.0))
        acc_tok = init_tok = VE.do(lambda e: e.memset(num_run[:, 1, BANK - 1:BANK], 0.0))
        for eng in (GE, SP, PE, AE):
            eng.wait(*qv_done)
            eng.wait(init_tok)
        SP.wait(plan_reg_tok, masks_tok)

        free = {}
        gs_free = [None] * SLOTS
        qd_free = [None] * SLOT2
        at_free = [None] * SLOT2
        count = 0
        hot_free = [None] * HOTS
        hots_used = 0

        def load(r):
            tokens = []
            mslot = r % 2
            SP.wait(free.get(("masks", mslot)))
            for k in range(3):
                for q in range(QUADS):
                    s0 = q * QS + r * GROUP
                    mt = SP.dma(lambda e, k=k, q=q, s0=s0: e.dma_start(
                        masks[32 * q:32 * (q + 1), mslot, k, :],
                        spread(step_masks[k, s0:s0 + GROUP, :].rearrange("(a s) e -> a (s e)", a=1), 0, 32)), mask_lane[mslot])
            return mt

        def fetch(r, q, n0):
            toks = []
            for j in range(GROUP):
                s = q * QS + r * GROUP + j
                n = n0 + j
                GE.wait(gs_free[n % SLOTS])
                a = GE.dma(lambda e, s=s, n=n: e.indirect_dma_start(
                    out=q_src[:, n % SLOTS, :], out_offset=None, in_=table[0][:, :],
                    in_offset=bass.IndirectOffsetOnAxis(ap=src_col[:, s:s + 1], axis=0),
                    bounds_check=NP - 1, oob_is_err=False), slot_lane[n % SLOTS])
                GE.wait(qd_free[n % SLOT2])
                b = GE.dma(lambda e, s=s, n=n: e.indirect_dma_start(
                    out=q_dst[:, n % SLOT2, :], out_offset=None, in_=table[0][:, :],
                    in_offset=bass.IndirectOffsetOnAxis(ap=dst_col[:, s:s + 1], axis=0),
                    bounds_check=NP - 1, oob_is_err=False), qd_lane[n % SLOT2])
                SP.wait(at_free[n % SLOT2])

                def load_attr(e, s=s, n=n):
                    r0 = e.value_load(plan_reg[0:1, 1, s:s + 1], min_val=0, max_val=E - P)
                    return e.dma_start(attr[:, n % SLOT2, :], attr_in[bass.ds(r0, P), :])
                c = SP.dma(load_attr, at_lane[n % SLOT2])
                toks.append((a, b, c))
            return toks

        n = 0
        for r in range(ROUNDS):
            mslot = r % 2
            mask_tok = load(r)
            for q in range(QUADS):
                toks = fetch(r, q, n)
                g = n // GROUP
                two = g % 2
                PE.wait(free.get("b_attr"))
                for j in range(GROUP):
                    PE.wait(toks[j][2])
                    at_free[(n + j) % SLOT2] = ta = PE.do(lambda e, j=j, m=n + j: e.transpose(
                        psum[:, B_ATTR, j * P:(j + 1) * P], attr[:, m % SLOT2, :], ident[:, :]))
                PE.wait(free.get("b_qs"))
                for j in range(GROUP):
                    PE.wait(toks[j][0])
                    gs_free[(n + j) % SLOTS] = ts = PE.do(lambda e, j=j, m=n + j: e.transpose(
                        psum[:, B_QS, j * P:(j + 1) * P], q_src[:, m % SLOTS, :], ident[:, :]))
                PE.wait(free.get("b_qd"))
                for j in range(GROUP):
                    PE.wait(toks[j][1])
                    qd_free[(n + j) % SLOT2] = td = PE.do(lambda e, j=j, m=n + j: e.transpose(
                        psum[:, B_QD, j * P:(j + 1) * P], q_dst[:, m % SLOT2, :], ident[:, :]))
                AE.wait(ta, free.get(("attr_t", two)))
                ca = free["b_attr"] = AE.do(lambda e, two=two: e.activation(attr_t[:, two, :], psum[:, B_ATTR, :], ACT.Copy))
                AE.wait(ts, free.get(("qsrc_t", two)))
                cs = AE.do(lambda e, two=two: e.activation(qsrc_t[:, two, :], psum[:, B_QS, :], ACT.Copy))
                AE.wait(td, free.get(("qdst_t", two)))
                cd = free["b_qd"] = AE.do(lambda e, two=two: e.activation(qdst_t[:, two, :], psum[:, B_QD, :], ACT.Copy))
                PE.wait(ca, free.get("b_k"))
                tk = free[("attr_t", two)] = PE.do(lambda e, two=two: e.matmul(psum[:, B_K, :], weights[:, WI["Wk"], :],
                                                                               attr_t[:, two, :], start=True, stop=True))
                VE.wait(tk, cs, cd, free.get("prod"))
                p0 = VE.do(lambda e, two=two: e.scalar_tensor_tensor(prod[:, 0, :], psum[:, B_K, :], bk_col[:, 0:1],
                                                                     qsrc_t[:, two, :], ALU.add, ALU.mult))
                p1 = free["b_k"] = VE.do(lambda e, two=two: e.scalar_tensor_tensor(
                    prod[:, 1, :], psum[:, B_K, :], bk_col[:, 0:1], qdst_t[:, two, :], ALU.add, ALU.mult))
                p2 = VE.do(lambda e, two=two: e.tensor_tensor(prod[:, 2, :], psum[:, B_QS, :], qdst_t[:, two, :], ALU.mult))
                free["b_qs"] = free[("qsrc_t", two)] = free[("qdst_t", two)] = p2
                if q == 0:
                    PE.wait(free.get("b_logit"))
                for k, tk in enumerate((p0, p1, p2)):
                    PE.wait(tk)
                    th = PE.do(lambda e, k=k, q=q: e.matmul(psum[32 * q:32 * (q + 1), B_LOGIT, :], head_sum[:, k, :],
                                                            prod[:, k, :], start=(k == 0), stop=(k == 2),
                                                            tile_position=(0, 32 * q)))
                free["prod"] = th
                n += GROUP
            cur, old = r % 2, 1 - r % 2
            VE.wait(th, mask_tok)
            lt = free["b_logit"] = VE.do(lambda e, cur=cur: e.tensor_tensor(masks[:, cur, 0, :], psum[:, B_LOGIT, :],
                                                                             masks[:, cur, 0, :], ALU.add))
            VE.wait(free.get(("runs", cur)))
            t = VE.do(lambda e, cur=cur, old=old: e.tensor_copy(m_run[:, cur, 0:1], m_run[:, old, BANK:BANK + 1]))
            VE.wait(t, lt)
            t = VE.do(lambda e, cur=cur: e.tensor_tensor_scan(
                m_run[:, cur, 1:BANK + 1], masks[:, cur, 1, :], masks[:, cur, 0, :], m_run[:, cur, 0:1], ALU.add, ALU.max))
            VE.wait(t, free.get("expo"))
            t = VE.do(lambda e, cur=cur: e.tensor_tensor(masks[:, cur, 1, :], m_run[:, cur, 0:BANK], masks[:, cur, 1, :], ALU.add))
            te = VE.do(lambda e, cur=cur: e.tensor_tensor(expo[:, 0, :], masks[:, cur, 0, :], m_run[:, cur, 1:BANK + 1], ALU.subtract))
            VE.wait(t)
            t = VE.do(lambda e, cur=cur: e.tensor_tensor(masks[:, cur, 1, :], masks[:, cur, 1, :], m_run[:, cur, 1:BANK + 1], ALU.subtract))
            AE.wait(te)
            te = AE.do(lambda e: e.activation(expo[:, 0, :], expo[:, 0, :], ACT.Exp))
            AE.wait(t)
            tc = AE.do(lambda e, cur=cur: e.activation(masks[:, cur, 1, :], masks[:, cur, 1, :], ACT.Exp))
            VE.wait(te)
            tw = VE.do(lambda e, cur=cur: e.tensor_tensor(masks[:, cur, 2, :], expo[:, 0, :], masks[:, cur, 2, :], ALU.mult))
            VE.wait(tc)
            VE.do(lambda e, cur=cur, old=old: e.tensor_tensor_scan(den_run[:, cur, :], masks[:, cur, 1, :], expo[:, 0, :],
                                                                   den_run[:, old, BANK - 1:BANK], ALU.mult, ALU.add))
            VE.wait(tw)
            tn = VE.do(lambda e, cur=cur, old=old: e.tensor_tensor_scan(num_run[:, cur, :], masks[:, cur, 1, :], masks[:, cur, 2, :],
                                                                        num_run[:, old, BANK - 1:BANK], ALU.mult, ALU.add))
            free[("masks", mslot)] = free["expo"] = tn
            for j in range(GROUP):
                two = j % 2
                PE.wait(tn, free.get("b_end"))
                for k, run in enumerate((m_run[:, cur, 1:BANK + 1], den_run[:, cur, :], num_run[:, cur, :])):
                    tt = PE.do(lambda e, k=k, run=run, j=j: e.transpose(psum[:, B_END, k * P:(k + 1) * P],
                                                                        run[:, j * P:(j + 1) * P], ident[:, :]))
                AE.wait(tt, free.get(("ends", two)))
                tx = free["b_end"] = AE.do(lambda e, two=two: e.activation(ends[:, two, :], psum[:, B_END, 0:3 * P], ACT.Copy))
                values = ends[:, two, :].rearrange("p (k q c) -> p k q c", k=3, q=QUADS)
                for q in range(QUADS):
                    s = q * QS + r * GROUP + j
                    h = hots_used % HOTS
                    hots_used += 1
                    VE.wait(hot_free[h])
                    t = VE.do(lambda e, s=s, h=h: e.tensor_scalar(hot[:, h, :], iota_f[:, :], end_col[:, s:s + 1], None, ALU.is_equal))
                    if q == 0:
                        PE.wait(free.get("b_sum"))
                    PE.wait(t, tx)
                    ts = hot_free[h] = PE.do(lambda e, q=q, h=h, values=values: e.matmul(
                        psum[:, B_SUM, q * ACCW:(q + 1) * ACCW].rearrange("p (k c) -> p k c", k=3), hot[:, h, :],
                        values[:, :, q, 0:SOFT], start=True, stop=True))
                free[("ends", two)] = ts
                VE.wait(ts)
                for q in range(QUADS):
                    s = q * QS + r * GROUP + j
                    VE.wait(acc_tok)

                    def add(e, s=s, q=q):
                        b = e.value_load(plan_reg[0:1, 0, s:s + 1], min_val=0, max_val=NB - 1)
                        return e.tensor_tensor(soft_acc[:, q, bass.ds(b, 1), :], soft_acc[:, q, bass.ds(b, 1), :],
                                               psum[:, B_SUM, q * ACCW:(q + 1) * ACCW].rearrange("p (a c) -> p a c", a=1), ALU.add)
                    acc_tok = VE.do(add)
                free["b_sum"] = acc_tok
            free[("runs", cur)] = tt

        VE.wait(acc_tok)
        NC = NB * SOFT
        assert 4 * NC <= NX
        big_m = pool[:, 0:NC].rearrange("p (b c) -> p b c", b=NB)
        sum_d = pool[:, NC:2 * NC].rearrange("p (b c) -> p b c", b=NB)
        sum_n = pool[:, 2 * NC:3 * NC].rearrange("p (b c) -> p b c", b=NB)
        tmp3 = pool[:, 3 * NC:4 * NC].rearrange("p (b c) -> p b c", b=NB)

        def part(q, k):
            return soft_acc[:, q, :, k * SOFT:(k + 1) * SOFT]

        PE_end = (PE.done, PE.count)
        AE_end = (AE.done, AE.count)
        VE.wait(PE_end, AE_end)
        for q in range(QUADS):
            t = VE.do(lambda e, q=q: e.tensor_scalar(tmp3, part(q, 1), 0.5, -BIG, ALU.is_lt, ALU.mult))
            VE.wait(t)
            t = VE.do(lambda e, q=q: e.tensor_tensor(part(q, 0), part(q, 0), tmp3, ALU.add))
            VE.wait(t)
            if q == 0:
                t = VE.do(lambda e: e.tensor_copy(big_m, part(0, 0)))
            else:
                t = VE.do(lambda e, q=q: e.tensor_tensor(big_m, big_m, part(q, 0), ALU.max))
            VE.wait(t)
        for q in range(QUADS):
            t = VE.do(lambda e, q=q: e.tensor_tensor(part(q, 0), part(q, 0), big_m, ALU.subtract))
            AE.wait(t)
            t = AE.do(lambda e, q=q: e.activation(part(q, 0), part(q, 0), ACT.Exp))
            VE.wait(t)
            for k, total in ((1, sum_d), (2, sum_n)):
                if q == 0:
                    t = VE.do(lambda e, k=k, total=total: e.tensor_tensor(total, part(0, k), part(0, 0), ALU.mult))
                else:
                    t = VE.do(lambda e, q=q, k=k: e.tensor_tensor(tmp3, part(q, k), part(q, 0), ALU.mult))
                    VE.wait(t)
                    t = VE.do(lambda e, total=total: e.tensor_tensor(total, total, tmp3, ALU.add))
                VE.wait(t)
        t = VE.do(lambda e: e.scalar_tensor_tensor(sum_d, sum_d, 0.0, sum_d, ALU.is_equal, ALU.add))
        VE.wait(t)
        t = VE.do(lambda e: e.reciprocal(sum_d, sum_d))
        VE.wait(t)
        t = VE.do(lambda e: e.tensor_tensor(sum_n, sum_n, sum_d, ALU.mult))
        VE.wait(t)
        score = tmp3[:, :, 0:HEADS]
        t = VE.do(lambda e: e.tensor_tensor(score, sum_n[:, :, 0:HEADS], sum_n[:, :, HEADS:2 * HEADS], ALU.add))
        VE.wait(t)
        t = VE.do(lambda e: e.tensor_tensor(score, score, sum_n[:, :, 2 * HEADS:3 * HEADS], ALU.add))
        VE.wait(t)
        for lo, hi in groups:
            for b in range(lo, hi):
                tok = VE.do(lambda e, b=b: e.tensor_tensor(
                    V[:, b, :].rearrange("p (h d) -> p h d", h=HEADS), V[:, b, :].rearrange("p (h d) -> p h d", h=HEADS),
                    spread(score[:, b, :].rearrange("p (h a) -> p h a", a=1), 2, HEAD_DIM), ALU.mult))

        def attention_out(g, lo, hi, view, t):
            VE.wait(t)
            n = hi - lo
            st = stage[:, g % 4, 0:n * P].rearrange("p (b d) -> p b d", b=n)
            free = VE.do(lambda e: e.tensor_tensor(st, view, bias_of("bo", n), ALU.add))
            VE.wait(free)
            t = VE.do(lambda e: e.scalar_tensor_tensor(st, st, SLOPE, st, ALU.mult, ALU.max))
            VE.wait(t)
            hidden.append(VE.do(lambda e: e.tensor_tensor(X[:, lo:hi, :], X[:, lo:hi, :], st, ALU.add)))
            return free

        hidden = []
        bank_free = [(VE.done, VE.count)] * PS_BANKS
        dense([(V, "Wo")], [tok], attention_out)
        tok = hidden[-1]

        tok = layer_norm(Y, [tok])
        stored = [store_table(table[1], Y[:, lo:hi, :], g, lo, hi, tok) for g, (lo, hi) in enumerate(groups)]
        end = aggregate(table[1], stored[-4:], False, [tok])
        VE.wait(end)
        for lo, hi in groups:
            tok = VE.do(lambda e, lo=lo, hi=hi: e.tensor_tensor(AGG[:, lo:hi, :], AGG[:, lo:hi, :], col_bc(inv_cnt, lo, hi), ALU.mult))
        nrm = ln_shift
        square = pool[:, 8 * BANK:9 * BANK]

        def sage_out(g, lo, hi, view, t):
            VE.wait(t)
            n = hi - lo
            st = stage[:, g % 4, 0:n * P].rearrange("p (b d) -> p b d", b=n)
            sq = square[:, 0:n * P].rearrange("p (b d) -> p b d", b=n)
            free = VE.do(lambda e: e.tensor_tensor(st, view, bias_of("bl", n), ALU.add))
            VE.wait(free)
            t = VE.do(lambda e: e.tensor_tensor(sq, st, st, ALU.mult))
            VE.wait(t)
            t = VE.do(lambda e: e.tensor_reduce(nrm[:, lo:hi], sq, AX.X, ALU.add))
            VE.wait(t)
            t = VE.do(lambda e: e.tensor_scalar(nrm[:, lo:hi], nrm[:, lo:hi], NORM_EPS * NORM_EPS, None, ALU.max))
            AE.wait(t)
            t = AE.do(lambda e: e.activation(nrm[:, lo:hi], nrm[:, lo:hi], ACT.Sqrt))
            VE.wait(t)
            t = VE.do(lambda e: e.reciprocal(nrm[:, lo:hi], nrm[:, lo:hi]))
            VE.wait(t)
            t = VE.do(lambda e: e.tensor_tensor(st, st, col_bc(nrm, lo, hi), ALU.mult))
            VE.wait(t)
            t = VE.do(lambda e: e.tensor_tensor(X[:, lo:hi, :], X[:, lo:hi, :], st, ALU.add))
            SP.wait(t)
            whole = min(hi, NB - 1)
            if whole > lo:
                SP.dma(lambda e: e.dma_start(out[lo * P:whole * P, :].rearrange("(b p) d -> p b d", p=P),
                                                         X[:, lo:whole, :]), out_lane[g % 4])
            if hi == NB:
                SP.dma(lambda e: e.dma_start(out[(NB - 1) * P:N, :], X[0:LAST, NB - 1, :]), out_lane[g % 4])
            return free

        dense([(AGG, "Wl"), (Y, "Wr")], [tok], sage_out)
        SP.wait(*[(lane.handle, lane.count) for lane in out_lane])

        block = ctx.enter_context(nc.Block())
        for engine in (VE, AE, PE, GE, SP):
            def emit(e, engine=engine):
                for instruction in engine.queue:
                    instruction(e)
            {"vector": block.vector, "scalar": block.scalar, "tensor": block.tensor, "gpsimd": block.gpsimd,
             "sync": block.sync}[engine.name](emit)


_NAMES = ["x", "src", "dst", "edge_attr_128", "edge_weight", "edge_weight1", "L0_gnn_W0", "L0_gnn_b0", "L0_gnn_W1",
          "L0_gnn_b1", "L0_gnn_W2", "L0_gnn_b2", "L1_gnn_W1", "L1_gnn_b1", "L1_gnn_W2", "L1_gnn_b2", "L2_gnn_Wq",
          "L2_gnn_bq", "L2_gnn_Wk", "L2_gnn_bk", "L2_gnn_Wv", "L2_gnn_bv", "L2_gnn_Wo", "L2_gnn_bo", "L2_gnn_lam",
          "L3_gnn_W_l", "L3_gnn_b_l", "L3_gnn_W_r"]


def kernel(**inputs):
    import numpy as np
    import concourse.bacc as bacc
    from concourse.bass_utils import run_bass_kernel_spmd

    nc = bacc.Bacc("TRN2", target_bir_lowering=False, num_devices=1)
    arrays, args = {}, []
    for name in _NAMES:
        a = np.ascontiguousarray(inputs[name])
        if a.ndim == 0:
            a = a.reshape(1)
        arrays[name] = a
        args.append(nc.dram_tensor(name, a.shape, mybir.dt.from_np(a.dtype), kind="ExternalInput").ap())
    out = nc.dram_tensor("out", arrays["x"].shape, F32, kind="ExternalOutput").ap()
    build(nc, *args, out)
    result = run_bass_kernel_spmd(nc, [arrays], core_ids=[0])
    return result.results[0]["out"]
```

```python
import math
from contextlib import ExitStack

import concourse.bass as bass
from concourse import mybir

F32 = mybir.dt.float32
BF16 = mybir.dt.bfloat16
I32 = mybir.dt.int32
ALU = mybir.AluOpType
ACT = mybir.ActivationFunctionType
AX = mybir.AxisListType

P = 128
D = 128
HEADS = 8
HEAD_DIM = D // HEADS
SCALE = 1.0 / math.sqrt(HEAD_DIM)
LN_EPS = 1e-5
NORM_EPS = 1e-12
SLOPE = 0.1
BIG = 1e30

PS_BANKS = 8
BANK = 512
GROUP = BANK // P


def ceil_div(a, b):
    return -(-a // b)


def spread(ap, dim, n):
    shape = list(ap.shape)
    shape[dim] = n
    return ap.broadcast_to(shape)


class Engine:

    def __init__(self, name, done):
        self.name, self.done, self.count, self.queue, self.seen = name, done, 0, [], {}

    def do(self, instruction):
        self.count += 1
        self.queue.append(lambda e, f=instruction, s=self.done: f(e).then_inc(s, 1))
        return (self.done, self.count)

    def dma(self, instruction, semaphore):
        semaphore.count += 16
        self.queue.append(lambda e, f=instruction, s=semaphore.handle: f(e).then_inc(s, 16))
        return (semaphore.handle, semaphore.count)

    def wait(self, *tokens):
        for token in tokens:
            if token is None:
                continue
            handle, count = token
            if self.seen.get(id(handle), 0) < count:
                self.seen[id(handle)] = count
                self.queue.append(lambda e, h=handle, c=count: e.wait_ge(h, c))


class Lane:

    def __init__(self, handle):
        self.handle, self.count = handle, 0


def build(nc, x_in, src_in, dst_in, attr_in, ew_in, dist_in, W0, b0, W1, b1, W2, b2,
          G1, c1, G2, c2, Wq, bq, Wk, bk, Wv, bv, Wo, bo, lam, Wl, bl, Wr, out):
    N = x_in.shape[0]
    E = src_in.shape[0]
    NB = ceil_div(N, P)
    NP = NB * P
    LAST = N - (NB - 1) * P
    NT = ceil_div(E, P)
    OVER = NT * P - E
    QUADS = 4
    NS = ceil_div(NT + NB - 1, QUADS * GROUP) * QUADS * GROUP
    SR = ceil_div(NS, P)
    QS = NS // QUADS
    FIELDS = 5
    DST, BEFORE, AFTER, SRC, WEIGHT = range(FIELDS)

    ctx = ExitStack()
    with ctx:
        def sb(name, shape, dt=F32):
            return ctx.enter_context(nc.sbuf_tensor(name, shape, dt))

        def sem(name):
            return ctx.enter_context(nc.semaphore(name))

        def lane(name):
            return Lane(sem(name))

        VE = Engine("vector", sem("vector_done"))
        AE = Engine("scalar", sem("scalar_done"))
        PE = Engine("tensor", sem("tensor_done"))
        GE = Engine("gpsimd", sem("gpsimd_done"))
        SP = Engine("sync", sem("sync_done"))

        edge_tiles = nc.dram_tensor("edge_tiles", [NT, FIELDS * P], I32).ap()
        plan_rows = nc.dram_tensor("plan_rows", [2, SR * P], I32).ap()
        att_flat = nc.dram_tensor("att_flat", [E], F32).ap()
        att_tiles = nc.dram_tensor("att_tiles", [NT, P], F32).ap()
        step_masks = nc.dram_tensor("step_masks", [3, SR * P, P], F32).ap()
        table = [nc.dram_tensor(f"table{i}", [NP, D], F32).ap() for i in range(2)]

        ident = sb("ident", [P, P])
        iota_f = sb("iota_f", [P, P])
        iota_b = sb("iota_b", [P, P], BF16)
        X = sb("X", [P, NB, D])
        V = sb("V", [P, NB, D])
        ACCW = 3 * 3 * HEADS
        SOFT = 3 * HEADS
        work = sb("work", [P, max(QUADS * NB * ACCW, 2 * NB * D)])
        AGG = work[:, 0:NB * D].rearrange("p (b d) -> p b d", b=NB)
        Y = work[:, NB * D:2 * NB * D].rearrange("p (b d) -> p b d", b=NB)
        soft_acc = work[:, 0:QUADS * NB * ACCW].rearrange("p (q b c) -> p q b c", q=QUADS, b=NB)
        rel_col = sb("rel_col", [P, SR * P])
        end_col = sb("end_col", [P, SR * P])
        ew_col = sb("ew_col", [P, SR * P])
        src_col = sb("src_col", [P, SR * P], I32)
        plan_reg = sb("plan_reg", [1, 2, NS], I32)
        dst_col = sb("dst_col", [P, SR * P], I32)
        weights = sb("weights", [P, 12, P])
        WI = {n: i for i, n in enumerate(["W0", "W1", "W2", "G1", "G2", "Wq", "Wk", "Wv", "Wo", "Wl", "Wr"])}
        bias = sb("bias", [P, 9, P])
        BI = {n: i for i, n in enumerate(["b0", "b1", "b2", "c1", "c2", "bq", "bv", "bo", "bl"])}
        bk_col = sb("bk_col", [P, 1])
        head_sum = sb("head_sum", [P, 3, 32])
        dis = sb("dis", [P, NB])
        deg = sb("deg", [P, NB])
        inv_cnt = sb("inv_cnt", [P, NB])
        ln_stat = sb("ln_stat", [P, NB, 6])
        ln_mv = sb("ln_mv", [P, NB, 2])
        ln_rstd = sb("ln_rstd", [P, NB])
        ln_shift = sb("ln_shift", [P, NB])

        SLOTS = 12
        HOTS = 4
        gath = sb("gath", [P, SLOTS, D])
        hot = sb("hot", [P, HOTS, P])
        NX = 14088
        pool = sb("pool", [P, NX])

        psum = ctx.enter_context(nc.psum_tensor("psum", [P, PS_BANKS, BANK], F32))

        slot_lane = [lane(f"slot{i}") for i in range(SLOTS)]
        setup_lane = [lane(f"setup{i}") for i in range(24)]
        table_lane = [lane(f"table_lane{i}") for i in range(4)]
        out_lane = [lane(f"out_lane{i}") for i in range(4)]

        iota_tok = GE.do(lambda e: e.iota(iota_f[:, :], pattern=[[1, P]], base=0, channel_multiplier=0,
                                          allow_small_or_imprecise_dtypes=True))
        step_no = sb("step_no", [P, SR])
        step_no_tok = GE.do(lambda e: e.iota(step_no[:, :], pattern=[[P, SR]], base=0, channel_multiplier=1,
                                             allow_small_or_imprecise_dtypes=True))
        part_no = sb("part_no", [P, 1])
        part_tok = GE.do(lambda e: e.iota(part_no[:, :], pattern=[[0, 1]], base=0, channel_multiplier=1,
                                          allow_small_or_imprecise_dtypes=True))
        VE.wait(iota_tok, part_tok)
        ident_tok = VE.do(lambda e: e.tensor_scalar(ident[:, :], iota_f[:, :], part_no[:, 0:1], None, ALU.is_equal))
        iota_b_tok = VE.do(lambda e: e.tensor_copy(iota_b[:, :], iota_f[:, :]))
        ones_row = sb("ones_row", [1, P])
        ones_tok = VE.do(lambda e: e.memset(ones_row[:, :], 1.0))
        minus_row = sb("minus_row", [1, P], I32)
        minus_tok = VE.do(lambda e: e.memset(minus_row[:, :], -1))

        hs_tok = GE.do(lambda e: e.memset(head_sum[:, :, :], 0.0))
        for k in range(3):
            part = head_sum[:, k, HEADS * k:HEADS * (k + 1)]
            GE.wait(hs_tok)
            hs_tok = GE.do(lambda e, part=part: e.memset(part, SCALE))
            for base, mult, step in ((0, 1, -HEAD_DIM), (HEAD_DIM - 1, -1, HEAD_DIM)):
                GE.wait(hs_tok)
                hs_tok = GE.do(lambda e, part=part, base=base, mult=mult, step=step: e.affine_select(
                    out=part, in_=part, compare_op=ALU.is_ge, fill=0.0, base=base, pattern=[[step, HEADS]],
                    channel_multiplier=mult))
        head_sum_tok = hs_tok

        setup = iter(setup_lane)
        raw = {DST: dst_in, SRC: src_in, WEIGHT: ew_in.bitcast(I32)}
        WHOLE = (NT - 1) * P
        first_last = pool[0:1, 0:2 * NT].bitcast(I32).rearrange("a (k t) -> a k t", k=2)
        fl_lane = next(setup)
        SP.dma(lambda e: e.dma_start(first_last[:, 0, 0:NT], dst_in.rearrange("(a e) -> a e", a=1)[:, 0:WHOLE + 1:P],
                                     allow_slow_non_contiguous=True), fl_lane)
        SP.dma(lambda e: e.dma_start(first_last[:, 1, 0:NT - 1], dst_in.rearrange("(a e) -> a e", a=1)[:, P - 1:WHOLE:P],
                                     allow_slow_non_contiguous=True), fl_lane)
        fl_tok = SP.dma(lambda e: e.dma_start(first_last[:, 1, NT - 1:NT], dst_in[E - 1:E].rearrange("(a e) -> a e", a=1)),
                        fl_lane)
        tiles_lane = next(setup)
        tile_fields = edge_tiles.rearrange("t (f e) -> t f e", f=FIELDS)
        for field in (DST, SRC, WEIGHT):
            flat = raw[field]
            SP.dma(lambda e, field=field, flat=flat: e.dma_start(
                tile_fields[0:NT - 1, field, :], flat[0:WHOLE].rearrange("(t e) -> t e", e=P)), tiles_lane)
            skip = OVER if field == DST else 0
            SP.dma(lambda e, field=field, flat=flat, skip=skip: e.dma_start(
                tile_fields[NT - 1:NT, field, skip:P], flat[E - P + skip:E].rearrange("(t e) -> t e", t=1)), tiles_lane)
        before = edge_tiles.rearrange("t (f e) -> t f e", f=FIELDS)[:, BEFORE, :]
        after = edge_tiles.rearrange("t (f e) -> t f e", f=FIELDS)[:, AFTER, :]
        SP.dma(lambda e: e.dma_start(before[1:NT - 1, :], dst_in[P - 1:WHOLE - 1].rearrange("(t e) -> t e", e=P)), tiles_lane)
        SP.dma(lambda e: e.dma_start(before[0:1, 1:P], dst_in[0:P - 1].rearrange("(t e) -> t e", t=1)), tiles_lane)
        SP.dma(lambda e: e.dma_start(before[NT - 1:NT, :], dst_in[E - P - 1:E - 1].rearrange("(t e) -> t e", t=1)), tiles_lane)
        SP.dma(lambda e: e.dma_start(after[0:NT - 1, :], dst_in[1:WHOLE + 1].rearrange("(t e) -> t e", e=P)), tiles_lane)
        SP.dma(lambda e: e.dma_start(after[NT - 1:NT, 0:P - 1], dst_in[E - P + 1:E].rearrange("(t e) -> t e", t=1)), tiles_lane)
        SP.wait(minus_tok)
        if OVER:
            SP.dma(lambda e: e.dma_start(tile_fields[NT - 1:NT, DST, 0:OVER], minus_row[:, 0:OVER]), tiles_lane)
        SP.dma(lambda e: e.dma_start(before[0:1, 0:1], minus_row[:, 0:1]), tiles_lane)
        tiles_tok = SP.dma(lambda e: e.dma_start(after[NT - 1:NT, P - 1:P], minus_row[:, 0:1]), tiles_lane)

        x_lane = next(setup)
        VE_x0 = VE.do(lambda e: e.memset(X[:, NB - 1, :], 0.0))
        SP.dma(lambda e: e.dma_start(X[:, 0:NB - 1, :], x_in[0:(NB - 1) * P, :].rearrange("(b p) d -> p b d", p=P)), x_lane)
        SP.wait(VE_x0)
        x_tok = SP.dma(lambda e: e.dma_start(X[0:LAST, NB - 1, :], x_in[(NB - 1) * P:N, :]), x_lane)
        w_lane = next(setup)
        for name, w in dict(W0=W0, W1=W1, W2=W2, G1=G1, G2=G2, Wq=Wq, Wk=Wk, Wv=Wv, Wo=Wo, Wl=Wl, Wr=Wr).items():
            AE.dma(lambda e, name=name, w=w: e.dma_start(weights[:, WI[name], :], w), w_lane)
        for name, b in dict(b0=b0, b1=b1, b2=b2, c1=c1, c2=c2, bq=bq, bv=bv, bo=bo, bl=bl).items():
            AE.dma(lambda e, name=name, b=b: e.dma_start(
                bias[:, BI[name], :], spread(b.rearrange("(a d) -> a d", a=1), 0, P)), w_lane)
        lam_col = sb("lam_col", [P, 1])
        AE.dma(lambda e: e.dma_start(lam_col[:, :], spread(lam.rearrange("(a d) -> a d", a=1), 0, P)), w_lane)
        w_tok = AE.dma(lambda e: e.dma_start(bk_col[:, :], bk.rearrange("(d a) -> d a", a=1)), w_lane)

        DR = max(d for d in range(1, P + 1) if E % d == 0)
        DC = E // DR
        dist_sb = V[0:DR, :, :].rearrange("p b d -> p (b d)")[:, 0:DC]
        lam_row = V[0:DR, :, :].rearrange("p b d -> p (b d)")[:, DC:2 * DC]
        dist_tok = SP.dma(lambda e: e.dma_start(dist_sb, dist_in.rearrange("(p c) a -> p (c a)", p=DR)), next(setup))
        VE.wait(w_tok)
        t = VE.do(lambda e: e.memset(lam_row, 0.0))
        VE.wait(t)
        lam_tok = VE.do(lambda e: e.tensor_scalar(lam_row, lam_row, lam_col[0:DR, 0:1], None, ALU.add))

        o = 2 * NT
        row = {}
        for name in ("fb", "lb", "spread", "off", "gap", "dgap", "ones"):
            row[name] = pool[0:1, o:o + NT]
            o += NT
        fl_block = pool[0:1, o:o + 2 * NT].bitcast(I32).rearrange("a (k t) -> a k t", k=2)
        o += 2 * NT
        ones_nt = VE.do(lambda e: e.memset(row["ones"], 1.0))
        VE.wait(fl_tok)
        t = VE.do(lambda e: e.tensor_scalar(fl_block, first_last, P.bit_length() - 1, None, ALU.arith_shift_right))
        VE.wait(t)
        VE.do(lambda e: e.tensor_copy(row["fb"], fl_block[:, 0, :]))
        t = VE.do(lambda e: e.tensor_copy(row["lb"], fl_block[:, 1, :]))
        VE.wait(t)
        t = VE.do(lambda e: e.tensor_tensor(row["spread"], row["lb"], row["fb"], ALU.subtract))
        VE.wait(t)
        t = VE.do(lambda e: e.tensor_scalar(row["spread"], row["spread"], 1.0, None, ALU.add))
        VE.wait(t, ones_nt)
        t = VE.do(lambda e: e.tensor_tensor_scan(row["off"], row["ones"], row["spread"], 0.0, ALU.mult, ALU.add))
        VE.wait(t)
        t = VE.do(lambda e: e.tensor_tensor(row["off"], row["off"], row["spread"], ALU.subtract))
        VE.wait(t)
        t = VE.do(lambda e: e.tensor_tensor(row["gap"], row["fb"], row["off"], ALU.subtract))
        VE.wait(t)
        VE.do(lambda e: e.tensor_copy(row["dgap"][:, 0:1], row["gap"][:, 0:1]))
        plan_tok = VE.do(lambda e: e.tensor_tensor(row["dgap"][:, 1:NT], row["gap"][:, 1:NT], row["gap"][:, 0:NT - 1],
                                                   ALU.subtract))
        off_all = pool[:, o:o + NT]
        dgap_all = pool[:, o + NT:o + 2 * NT]
        step_junk = pool[:, o + 2 * NT:o + 3 * NT]
        ROWS = o + 3 * NT
        assert ROWS <= NX
        PE.wait(plan_tok)
        copies = []
        bank = 0
        for name, dest in (("off", off_all), ("dgap", dgap_all)):
            for lo in range(0, NT, BANK):
                hi = min(NT, lo + BANK)
                t = PE.do(lambda e, name=name, lo=lo, hi=hi, bank=bank: e.matmul(
                    psum[:, bank, 0:hi - lo], ones_row[:, 0:P], row[name][:, lo:hi], start=True, stop=True))
                VE.wait(t)
                copies.append(VE.do(lambda e, dest=dest, lo=lo, hi=hi, bank=bank: e.tensor_copy(
                    dest[:, lo:hi], psum[:, bank, 0:hi - lo])))
                bank += 1
        VE.wait(copies[-1], step_no_tok)
        tile_of = sb("tile_of", [P, SR])
        block_of = sb("block_of", [P, SR])
        t = None
        for i in range(SR):
            t = VE.do(lambda e, i=i: e.tensor_scalar(step_junk, off_all, step_no[:, i:i + 1], None, ALU.is_le, ALU.add,
                                                     accum_out=tile_of[:, i:i + 1]))
            VE.wait(t)
            t = VE.do(lambda e, i=i: e.scalar_tensor_tensor(step_junk, off_all, step_no[:, i:i + 1], dgap_all, ALU.is_le,
                                                            ALU.mult, accum_out=block_of[:, i:i + 1]))
            VE.wait(t)
        t = VE.do(lambda e: e.tensor_scalar(tile_of[:, :], tile_of[:, :], -1.0, None, ALU.add))
        t = VE.do(lambda e: e.tensor_tensor(block_of[:, :], block_of[:, :], step_no[:, :], ALU.add))
        VE.wait(t)
        tile_idx = sb("tile_idx", [P, SR], I32)
        plan_cols = sb("plan_cols", [P, 2, SR])
        tile_tok = VE.do(lambda e: e.tensor_copy(tile_idx[:, :], tile_of[:, :]))
        VE.do(lambda e: e.tensor_scalar(plan_cols[:, 0, :], block_of[:, :], float(NB - 1), None, ALU.min))
        t = VE.do(lambda e: e.tensor_scalar(plan_cols[:, 1, :], tile_of[:, :], float(P), float(E - P), ALU.mult, ALU.min))
        base_of = sb("base_of", [P, SR])
        base_tok = VE.do(lambda e: e.tensor_scalar(base_of[:, :], block_of[:, :], float(P), None, ALU.mult))
        PE.wait(t, ident_tok)
        bank = 4
        t = PE.do(lambda e: e.transpose(psum[0:2 * SR, bank, 0:P], plan_cols[:, :, :].rearrange("p k s -> p (k s)"),
                                        ident[:, :]))
        VE.wait(t)
        plan_t = sb("plan_t", [2 * SR, P], I32)
        t = VE.do(lambda e: e.tensor_copy(plan_t[:, :], psum[0:2 * SR, 4, 0:P]))
        SP.wait(t)
        pl = next(setup)
        t = SP.dma(lambda e: e.dma_start(plan_rows.rearrange("k (s p) -> (k s) p", p=P), plan_t[:, :]), pl)
        SP.wait(t)
        plan_reg_tok = SP.dma(lambda e: e.dma_start(plan_reg[:, :, :], plan_rows.rearrange("(a k) s -> a k s", a=1)[:, :, 0:NS]), next(setup))

        def power():
            GE.wait(lam_tok, dist_tok)
            p = GE.do(lambda e: e.tensor_tensor(dist_sb, dist_sb, lam_row, ALU.pow))
            SP.wait(p)
            return SP.dma(lambda e: e.dma_start(att_flat.rearrange("(p c) -> p c", p=DR), dist_sb), next(setup))

        step_rows = work[:, 0:SR * FIELDS * P].bitcast(I32).rearrange("p (s f) -> p s f", s=SR)
        GE.wait(tile_tok, tiles_tok)
        rows_tok = []
        for i in range(SR):
            rows_tok.append(GE.dma(lambda e, i=i: e.indirect_dma_start(
                out=step_rows[:, i, :], out_offset=None, in_=edge_tiles[:, :],
                in_offset=bass.IndirectOffsetOnAxis(ap=tile_idx[:, i:i + 1], axis=0),
                bounds_check=NT - 1, oob_is_err=False), slot_lane[i]))
        o = ROWS - 3 * NT
        def rows_f(k):
            return pool[:, k * SR * P:(k + 1) * SR * P].rearrange("p (s e) -> p s e", s=SR)
        rel, valid, start, endr, lmask, srcf, tmp = (rows_f(k) for k in range(7))
        raw_field = step_rows.rearrange("p s (f e) -> p s f e", f=FIELDS)
        VE.wait(*rows_tok)
        VE.wait(base_tok)
        t = VE.do(lambda e: e.tensor_copy(tmp, raw_field[:, :, DST, :]))
        VE.do(lambda e: e.tensor_copy(srcf, raw_field[:, :, SRC, :]))
        for i in range(SR):
            VE.wait(t)
            t2 = VE.do(lambda e, i=i: e.tensor_scalar(rel[:, i, :], tmp[:, i, :], base_of[:, i:i + 1], None, ALU.subtract))
        VE.wait(t2)
        t = VE.do(lambda e: e.tensor_scalar(rel, rel, -1.0, float(P), ALU.max, ALU.min))
        VE.wait(t)
        t = VE.do(lambda e: e.tensor_scalar(valid, rel, 0.0, None, ALU.is_ge))
        VE.wait(t)
        t = VE.do(lambda e: e.scalar_tensor_tensor(valid, rel, float(P) - 0.5, valid, ALU.is_lt, ALU.mult))
        VE.wait(t)
        VE.do(lambda e: e.tensor_scalar(lmask, valid, -1.0, BIG, ALU.add, ALU.mult))
        t = VE.do(lambda e: e.tensor_copy(start, raw_field[:, :, BEFORE, :]))
        t = VE.do(lambda e: e.tensor_copy(endr, raw_field[:, :, AFTER, :]))
        VE.wait(t)
        VE.do(lambda e: e.tensor_tensor(start, start, tmp, ALU.not_equal))
        t = VE.do(lambda e: e.tensor_tensor(endr, endr, tmp, ALU.not_equal))
        forced = sb("forced", [P, SR])
        f = VE.do(lambda e: e.tensor_scalar(forced[:, :], step_no[:, :], float(QS - 1), None, ALU.is_equal))
        for q in range(1, QUADS):
            VE.wait(f)
            f = VE.do(lambda e, q=q: e.scalar_tensor_tensor(forced[:, :], step_no[:, :], float(QS * (q + 1) - 1), forced[:, :],
                                                            ALU.is_equal, ALU.max))
        VE.wait(f, t)
        t = VE.do(lambda e: e.tensor_tensor(endr[:, :, P - 1], endr[:, :, P - 1], forced[:, :], ALU.max))
        VE.wait(t)
        VE.do(lambda e: e.tensor_tensor(start, start, valid, ALU.mult))
        t = VE.do(lambda e: e.tensor_tensor(endr, endr, valid, ALU.mult))
        VE.wait(t)
        t = VE.do(lambda e: e.tensor_scalar(start, start, -BIG, None, ALU.mult))
        t = VE.do(lambda e: e.scalar_tensor_tensor(endr, rel, 1.0, endr, ALU.add, ALU.mult))
        VE.wait(t)
        VE.do(lambda e: e.tensor_scalar(endr, endr, -1.0, None, ALU.add))
        rows_done = VE.do(lambda e: e.tensor_scalar(tmp, tmp, 0.0, None, ALU.max))
        SP.wait(rows_done)
        masks_lane = next(setup)
        for k, arr in enumerate((lmask, start)):
            masks_tok = SP.dma(lambda e, k=k, arr=arr: e.dma_start(
                step_masks[k].rearrange("(s p) e -> p s e", p=P), arr), masks_lane)
        att_tok = power()
        SP.wait(att_tok)
        att_lane = next(setup)
        SP.dma(lambda e: e.dma_start(att_tiles[0:NT - 1, :], att_flat[0:WHOLE].rearrange("(t e) -> t e", e=P)), att_lane)
        t = SP.dma(lambda e: e.dma_start(att_tiles[NT - 1:NT, :], att_flat[E - P:E].rearrange("(t e) -> t e", t=1)), att_lane)
        GE.wait(t)
        att_rows = rows_f(8)
        for i in range(SR):
            t = GE.dma(lambda e, i=i: e.indirect_dma_start(
                out=att_rows[:, i, :], out_offset=None, in_=att_tiles[:, :],
                in_offset=bass.IndirectOffsetOnAxis(ap=tile_idx[:, i:i + 1], axis=0),
                bounds_check=NT - 1, oob_is_err=False), slot_lane[i])
            SP.wait(t)
        att_masks_tok = SP.dma(lambda e: e.dma_start(step_masks[2].rearrange("(s p) e -> p s e", p=P), att_rows), next(setup))
        ew_f = step_rows.bitcast(F32).rearrange("p s (f e) -> p s f e", f=FIELDS)[:, :, WEIGHT, :]
        PE.wait(rows_done)
        free = {}
        n = 0
        for arr, dest in ((rel, rel_col), (ew_f, ew_col), (srcf, src_col), (endr, end_col), (tmp, dst_col)):
            for lo in range(0, SR, GROUP):
                hi = min(SR, lo + GROUP)
                b = n % 4
                PE.wait(free.get(b))
                for i in range(lo, hi):
                    t = PE.do(lambda e, arr=arr, i=i, lo=lo, b=b: e.transpose(
                        psum[:, b, (i - lo) * P:(i - lo + 1) * P], arr[:, i, :], ident[:, :]))
                VE.wait(t)
                free[b] = cols_tok = VE.do(lambda e, dest=dest, lo=lo, hi=hi, b=b: e.tensor_copy(
                    dest[:, lo * P:hi * P], psum[:, b, 0:(hi - lo) * P]))
                n += 1

        PARTS = 4
        PER = BANK // PARTS
        SRW = SR * P
        parts = pool[:, 0:SRW * PARTS // 2].bitcast(BF16).rearrange("p (s k) -> p s k", k=PARTS)
        rest = pool[:, SRW * 2:SRW * 3]
        VE.wait(cols_tok, masks_tok)
        t = VE.do(lambda e: e.tensor_copy(parts[:, :, 0], ew_col[:, :]))
        VE.do(lambda e: e.memset(parts[:, :, 3], 1.0))
        VE.wait(t)
        t = VE.do(lambda e: e.tensor_tensor(rest, ew_col[:, :], parts[:, :, 0], ALU.subtract))
        VE.wait(t)
        t = VE.do(lambda e: e.tensor_copy(parts[:, :, 1], rest))
        VE.wait(t)
        t = VE.do(lambda e: e.tensor_tensor(rest, rest, parts[:, :, 1], ALU.subtract))
        VE.wait(t)
        parts_tok = VE.do(lambda e: e.tensor_copy(parts[:, :, 2], rest))
        hot_b = pool[:, SRW * 3:SRW * 3 + 8 * P // 2].bitcast(BF16).rearrange("p (k n) -> p k n", k=8)
        deg_of = pool[:, SRW * 4:SRW * 6].rearrange("p (k s) -> p k s", k=2)
        HB = 8
        PE.wait(parts_tok)
        VE.wait(iota_b_tok)
        pe_tok = []
        z = VE.do(lambda e: e.memset(deg_of[:, :, NS:SRW], 0.0))
        PE.wait(*free.values())
        for s in range(NS):
            if s >= HB:
                VE.wait(pe_tok[s - HB])
            t = VE.do(lambda e, s=s: e.tensor_scalar(hot_b[:, s % HB, :], iota_b[:, :], rel_col[:, s:s + 1], None,
                                                     ALU.is_equal))
            PE.wait(t)
            pe_tok.append(PE.do(lambda e, s=s: e.matmul(
                psum[:, s // PER, (s % PER) * PARTS:(s % PER + 1) * PARTS], hot_b[:, s % HB, :], parts[:, s, :],
                start=True, stop=True)))
        VE.wait(pe_tok[-1])
        for lo in range(0, NS, PER):
            n = min(PER, NS - lo)
            view = psum[:, lo // PER, 0:n * PARTS].rearrange("p (s k) -> p s k", k=PARTS)
            VE.do(lambda e, lo=lo, n=n, view=view: e.tensor_reduce(deg_of[:, 0, lo:lo + n], view[:, :, 0:3], AX.X, ALU.add))
            deg_tok = VE.do(lambda e, lo=lo, n=n, view=view: e.tensor_copy(deg_of[:, 1, lo:lo + n], view[:, :, 3]))
        block_hot = pool[:, SRW * 6:SRW * 6 + SR * NB].rearrange("p (s b) -> p s b", s=SR)
        for i in range(SR):
            bh_tok = VE.do(lambda e, i=i: e.tensor_scalar(block_hot[:, i, :], iota_f[:, 0:NB], block_of[:, i:i + 1], None,
                                                          ALU.is_equal))
        deg_t = pool[:, SRW * 3:SRW * 4].rearrange("p (s n) -> p s n", s=SR)
        PE.wait(deg_tok, bh_tok)
        for k in range(2):
            for lo in range(0, SR, GROUP):
                hi = min(SR, lo + GROUP)
                for i in range(lo, hi):
                    t = PE.do(lambda e, i=i, lo=lo, k=k: e.transpose(
                        psum[:, lo // GROUP, (i - lo) * P:(i - lo + 1) * P], deg_of[:, k, i * P:(i + 1) * P], ident[:, :]))
                VE.wait(t)
                t = VE.do(lambda e, lo=lo, hi=hi: e.tensor_copy(
                    deg_t[:, lo:hi, :], psum[:, lo // GROUP, 0:(hi - lo) * P].rearrange("p (s n) -> p s n", n=P)))
            PE.wait(t)
            for i in range(SR):
                t = PE.do(lambda e, i=i, k=k: e.matmul(psum[:, 2 + k, 0:NB], deg_t[:, i, :], block_hot[:, i, :],
                                                       start=(i == 0), stop=(i == SR - 1)))
            VE.wait(t)
            PE.wait(t)
        cnt_tok = VE.do(lambda e: e.tensor_scalar(inv_cnt[:, :], psum[:, 3, 0:NB], 1.0, None, ALU.max))
        t = VE.do(lambda e: e.tensor_scalar(deg[:, :], psum[:, 2, 0:NB], 1.0, None, ALU.add))
        VE.wait(t, cnt_tok)
        VE.do(lambda e: e.reciprocal(inv_cnt[:, :], inv_cnt[:, :]))
        t = VE.do(lambda e: e.tensor_scalar(dis[:, :], deg[:, :], 1e-30, None, ALU.max))
        AE.wait(t)
        t = AE.do(lambda e: e.activation(dis[:, :], dis[:, :], ACT.Sqrt))
        VE.wait(t)
        t = VE.do(lambda e: e.reciprocal(dis[:, :], dis[:, :]))
        VE.wait(t)
        dis_tok = VE.do(lambda e: e.scalar_tensor_tensor(dis[:, :], deg[:, :], 0.0, dis[:, :], ALU.is_gt, ALU.mult))

        PE.wait(w_tok, dis_tok)
        for k, name in enumerate(["Wq", "Wk", "Wv", "Wo", "Wl", "Wr"]):
            t = PE.do(lambda e, name=name, k=k: e.transpose(psum[:, k % 4, 0:P], weights[:, WI[name], :], ident[:, :]))
            AE.wait(t)
            t = AE.do(lambda e, name=name, k=k: e.activation(weights[:, WI[name], :], psum[:, k % 4, 0:P], ACT.Copy))
            PE.wait(t)
        wt_tok = t

        groups = [(lo, min(NB, lo + GROUP)) for lo in range(0, NB, GROUP)]
        tr = pool[:, 0:4 * BANK].rearrange("p (k n) -> p k n", k=4)
        stage = pool[:, 4 * BANK:8 * BANK].rearrange("p (k n) -> p k n", k=4)
        stage_free = [None] * 4
        tr_free = [None] * 4
        bank_free = [None] * PS_BANKS

        def layer_norm(dest, ready):
            VE.wait(*ready)
            for b in range(NB):
                t = VE.do(lambda e, b=b: e.bn_stats(ln_stat[:, b, :], X[:, b, :]))
            VE.wait(t)
            for b in range(NB):
                t = VE.do(lambda e, b=b: e.bn_aggr(ln_mv[:, b, :], ln_stat[:, b, :]))
            VE.wait(t)
            t = VE.do(lambda e: e.tensor_scalar(ln_rstd[:, :], ln_mv[:, :, 1], LN_EPS, None, ALU.add))
            AE.wait(t)
            t = AE.do(lambda e: e.activation(ln_rstd[:, :], ln_rstd[:, :], ACT.Sqrt))
            VE.wait(t)
            t = VE.do(lambda e: e.reciprocal(ln_rstd[:, :], ln_rstd[:, :]))
            VE.wait(t)
            t = VE.do(lambda e: e.scalar_tensor_tensor(ln_shift[:, :], ln_mv[:, :, 0], -1.0, ln_rstd[:, :], ALU.mult, ALU.mult))
            AE.wait(t)
            return [AE.do(lambda e, b=b: e.activation(dest[:, b, :], X[:, b, :], ACT.Relu, bias=ln_shift[:, b:b + 1],
                                                      scale=ln_rstd[:, b:b + 1])) for b in range(NB)]

        def dense(products, ready, post, func=ACT.Copy):
            for g, (lo, hi) in enumerate(groups):
                PE.wait(*(ready(g) if callable(ready) else ready))
                n = hi - lo
                moved = []
                for k, (source, _) in enumerate(products):
                    b = 2 * k + g % 2
                    PE.wait(bank_free[b])
                    for i in range(n):
                        t = PE.do(lambda e, source=source, i=i, b=b, lo=lo: e.transpose(
                            psum[:, b, i * P:(i + 1) * P], source[:, lo + i, :], ident[:, :]))
                    AE.wait(t, tr_free[b])
                    bank_free[b] = AE.do(lambda e, b=b, n=n: e.activation(tr[:, b, 0:n * P], psum[:, b, 0:n * P], func))
                    moved.append(bank_free[b])
                PE.wait(bank_free[4 + g % 2], *moved)
                for i in range(n):
                    for k, (_, w) in enumerate(products):
                        b = 2 * k + g % 2
                        t = PE.do(lambda e, i=i, k=k, b=b, w=w, g=g: e.matmul(
                            psum[:, 4 + g % 2, i * P:(i + 1) * P], tr[:, b, i * P:(i + 1) * P], weights[:, WI[w], :],
                            start=(k == 0), stop=(k == len(products) - 1)))
                for k in range(len(products)):
                    tr_free[2 * k + g % 2] = t
                view = psum[:, 4 + g % 2, 0:n * P].rearrange("p (b d) -> p b d", b=n)
                bank_free[4 + g % 2] = post(g, lo, hi, view, t)

        def bias_of(name, n):
            return spread(bias[:, BI[name], :].rearrange("p (a d) -> p a d", a=1), 1, n)

        def store_table(dest, source, g, lo, hi, ready):
            SP.wait(ready)
            return SP.dma(lambda e: e.dma_start(dest[lo * P:hi * P, :].rearrange("(b p) d -> p b d", p=P), source),
                          table_lane[g % 4])

        def col_bc(col, lo, hi):
            return spread(col[:, lo:hi].rearrange("p (b a) -> p b a", a=1), 2, D)

        plan_ready = plan_reg_tok

        def load_blocks(first, n):
            blocks = []
            VE.queue.append(lambda e: blocks.extend(nc.values_load_multi_w_load_instructions(
                plan_reg[0:1, 0, first:first + n], engines=[mybir.EngineType.DVE], min_val=0, max_val=NB - 1,
                skip_runtime_bounds_check_because="the plan takes the smaller of the block and the last block")[1]))
            return blocks

        REGS = 16

        def aggregate(source, stored, weighted, agg_free, start=None):
            VE.wait(plan_ready, *agg_free)
            acc_tok = start or VE.do(lambda e: e.memset(AGG, 0.0))
            GE.wait(*stored)
            PE.wait(*agg_free)
            mm = []

            def gather(s):
                if s >= SLOTS:
                    GE.wait(mm[s - SLOTS])
                return GE.dma(lambda e: e.indirect_dma_start(
                    out=gath[:, s % SLOTS, :], out_offset=None, in_=source[:, :],
                    in_offset=bass.IndirectOffsetOnAxis(ap=src_col[:, s:s + 1], axis=0),
                    bounds_check=NP - 1, oob_is_err=False), slot_lane[s % SLOTS])

            def one_hot(s):
                if s >= HOTS:
                    VE.wait(mm[s - HOTS])
                return VE.do(lambda e: e.tensor_scalar(
                    hot[:, s % HOTS, :], iota_f[:, :], rel_col[:, s:s + 1], ew_col[:, s:s + 1] if weighted else None,
                    ALU.is_equal, ALU.mult if weighted else ALU.bypass))

            gathered = []
            hots = []
            for s in range(NS + 2):
                if s < NS:
                    gathered.append(gather(s))
                    hots.append(one_hot(s))
                    PE.wait(hots[s], gathered[s])
                    PE.wait(bank_free[s % 4])
                    mm.append(PE.do(lambda e, s=s: e.matmul(psum[:, s % 4, 0:D], hot[:, s % HOTS, :], gath[:, s % SLOTS, :],
                                                            start=True, stop=True)))
                if s >= 2:
                    a = s - 2
                    if a % REGS == 0:
                        blocks = load_blocks(a, REGS)
                    VE.wait(mm[a], acc_tok)

                    def add(e, a=a, blocks=blocks):
                        b = blocks[a % REGS]
                        return e.tensor_tensor(AGG[:, bass.ds(b, 1), :], AGG[:, bass.ds(b, 1), :],
                                               psum[:, a % 4, 0:D].rearrange("p (a d) -> p a d", a=1), ALU.add)
                    acc_tok = VE.do(add)
                    bank_free[a % 4] = acc_tok
            return acc_tok

        normed = layer_norm(AGG, [x_tok, cols_tok])

        def gcn_table(which):
            def post(g, lo, hi, view, t):
                VE.wait(t, dis_tok)
                t = VE.do(lambda e: e.tensor_tensor(Y[:, lo:hi, :], view, col_bc(dis, lo, hi), ALU.mult))
                stored.append(store_table(table[which], Y[:, lo:hi, :], g, lo, hi, t))
                AE.wait(t)
                started.append(AE.do(lambda e: e.activation(AGG[:, lo:hi, :], Y[:, lo:hi, :], ACT.Copy)))
                return t
            return post

        for layer, (w, b) in enumerate((("W0", "b0"), ("W1", "b1"), ("W2", "b2"))):
            stored, started = [], []
            dense([(AGG, w)], (lambda g, normed=normed: [normed[groups[g][1] - 1], wt_tok]) if layer == 0 else (lambda g, done=done: [done[g]]),
                  gcn_table(layer % 2), ACT.Copy if layer == 0 else ACT.Relu)
            end = aggregate(table[layer % 2], stored[-4:], True, [(PE.done, PE.count)], started[-1])
            VE.wait(end)
            done = []
            for lo, hi in groups:
                for i in range(lo, hi):
                    t = VE.do(lambda e, i=i, b=b: e.scalar_tensor_tensor(AGG[:, i, :], AGG[:, i, :], dis[:, i:i + 1],
                                                                         bias[:, BI[b], :], ALU.mult, ALU.add))
                done.append(t)
                if layer == 2:
                    VE.wait(t)
                    tok = VE.do(lambda e, lo=lo, hi=hi: e.scalar_tensor_tensor(X[:, lo:hi, :], AGG[:, lo:hi, :], 0.0, X[:, lo:hi, :],
                                                                               ALU.max, ALU.add))

        normed = layer_norm(AGG, [tok])
        stored = [store_table(table[1], AGG[:, lo:hi, :], g, lo, hi, normed[hi - 1]) for g, (lo, hi) in enumerate(groups)]
        tok = aggregate(table[1], stored[-4:], True, stored[-4:], normed[-1])

        def gin_hidden(g, lo, hi, view, t):
            VE.wait(t)
            hidden.append(VE.do(lambda e: e.tensor_tensor(Y[:, lo:hi, :], view, bias_of("c1", hi - lo), ALU.add)))
            return hidden[-1]

        def gin_out(g, lo, hi, view, t):
            VE.wait(t)
            free = VE.do(lambda e: e.tensor_tensor(AGG[:, lo:hi, :], view, bias_of("c2", hi - lo), ALU.add))
            VE.wait(free)
            hidden.append(VE.do(lambda e: e.tensor_tensor(X[:, lo:hi, :], X[:, lo:hi, :], AGG[:, lo:hi, :], ALU.add)))
            return free

        hidden = []
        dense([(AGG, "G1")], [tok], gin_hidden)
        hid = list(hidden)
        dense([(Y, "G2")], lambda g: [hid[g]], gin_out, ACT.Relu)
        tok = hidden[-1]

        normed = layer_norm(AGG, [tok])
        stored = []

        def q_table(g, lo, hi, view, t):
            VE.wait(t, stage_free[g % 4])
            n = hi - lo
            t = VE.do(lambda e: e.tensor_tensor(stage[:, g % 4, 0:n * P].rearrange("p (b d) -> p b d", b=n), view,
                                                bias_of("bq", n), ALU.add))
            stage_free[g % 4] = store_table(table[0], stage[:, g % 4, 0:n * P].rearrange("p (b d) -> p b d", b=n), g, lo, hi, t)
            stored.append(stage_free[g % 4])
            return t

        def v_nodes(g, lo, hi, view, t):
            VE.wait(t)
            v_tok.append(VE.do(lambda e: e.tensor_tensor(V[:, lo:hi, :], view, bias_of("bv", hi - lo), ALU.add)))
            return v_tok[-1]

        v_tok = []
        dense([(AGG, "Wq")], lambda g: [normed[groups[g][1] - 1]], q_table)
        dense([(AGG, "Wv")], [normed[-1]], v_nodes)
        qv_done = [(PE.done, PE.count), (AE.done, AE.count), (VE.done, VE.count)] + stored[-4:]

        o = 0

        def take(n, *shape):
            nonlocal o
            view = pool[:, o:o + n * math.prod(shape)]
            o += n * math.prod(shape)
            names = [f"a{i}" for i in range(len(shape) + 1)]
            return view.rearrange(f"p ({' '.join(names)}) -> p {' '.join(names)}",
                                  **{k: s for k, s in zip(names, (n,) + shape)})

        q_src = gath
        SLOT2 = 8
        q_dst = take(SLOT2, D)
        attr = take(SLOT2, D)
        attr_t = take(2, BANK)
        qsrc_t = take(2, BANK)
        qdst_t = take(2, BANK)
        prod = take(3, BANK)
        masks = take(2, 3, BANK)
        m_run = take(2, BANK + 1)
        den_run = take(2, BANK)
        num_run = take(2, BANK)
        expo = take(1, BANK)
        ends = take(2, 3 * P)
        assert o <= NX, o

        ROUNDS = QS // GROUP
        qd_lane = [lane(f"qdst{i}") for i in range(SLOT2)]
        at_lane = [lane(f"attr{i}") for i in range(SLOT2)]
        mask_lane = [lane(f"mask{i}") for i in range(2)]
        B_ATTR, B_QS, B_QD, B_K, B_END, B_SUM = range(6)
        B_LOGIT = (6, 7)

        VE.wait(*qv_done)
        VE.do(lambda e: e.memset(soft_acc, 0.0))
        VE.do(lambda e: e.memset(m_run[:, 1, BANK:BANK + 1], -BIG))
        VE.do(lambda e: e.memset(den_run[:, 1, BANK - 1:BANK], 0.0))
        init_tok = VE.do(lambda e: e.memset(num_run[:, 1, BANK - 1:BANK], 0.0))
        for eng in (GE, SP, PE, AE):
            eng.wait(*qv_done)
            eng.wait(init_tok)
        SP.wait(plan_reg_tok, masks_tok, att_masks_tok)

        free = {}
        gs_free = [None] * SLOTS
        qd_free = [None] * SLOT2
        at_free = [None] * SLOT2
        hot_free = [None] * HOTS
        NG = ROUNDS * QUADS

        def group_steps(g):
            first = (g % QUADS) * QS + (g // QUADS) * GROUP
            return range(first, first + GROUP)

        def fetch(g):
            tokens = []
            for j, s in enumerate(group_steps(g)):
                n = g * GROUP + j
                GE.wait(gs_free[n % SLOTS])
                a = GE.dma(lambda e, s=s, n=n: e.indirect_dma_start(
                    out=q_src[:, n % SLOTS, :], out_offset=None, in_=table[0][:, :],
                    in_offset=bass.IndirectOffsetOnAxis(ap=src_col[:, s:s + 1], axis=0),
                    bounds_check=NP - 1, oob_is_err=False), slot_lane[n % SLOTS])
                GE.wait(qd_free[n % SLOT2])
                b = GE.dma(lambda e, s=s, n=n: e.indirect_dma_start(
                    out=q_dst[:, n % SLOT2, :], out_offset=None, in_=table[0][:, :],
                    in_offset=bass.IndirectOffsetOnAxis(ap=dst_col[:, s:s + 1], axis=0),
                    bounds_check=NP - 1, oob_is_err=False), qd_lane[n % SLOT2])
                SP.wait(at_free[n % SLOT2])

                def load_attr(e, s=s, n=n):
                    r0 = e.value_load(plan_reg[0:1, 1, s:s + 1], min_val=0, max_val=E - P)
                    return e.dma_start(attr[:, n % SLOT2, :], attr_in[bass.ds(r0, P), :])
                tokens.append((a, b, SP.dma(load_attr, at_lane[n % SLOT2])))
            return tokens

        def load_masks(r):
            SP.wait(free.get(("masks", r % 2)))
            for k in range(3):
                for q in range(QUADS):
                    s0 = q * QS + r * GROUP
                    t = SP.dma(lambda e, k=k, q=q, s0=s0: e.dma_start(
                        masks[32 * q:32 * (q + 1), r % 2, k, :],
                        spread(step_masks[k, s0:s0 + GROUP, :].rearrange("(a s) e -> a (s e)", a=1), 0, 32)), mask_lane[r % 2])
            return t

        def transpose_group(g, tokens):
            two = g % 2
            copied = []
            for k, (source, bank, dest) in enumerate(((attr, B_ATTR, attr_t), (q_src, B_QS, qsrc_t), (q_dst, B_QD, qdst_t))):
                slots = source.shape[1]
                PE.wait(free.get(bank))
                for j in range(GROUP):
                    n = g * GROUP + j
                    PE.wait(tokens[j][(2, 0, 1)[k]])
                    t = PE.do(lambda e, source=source, bank=bank, j=j, n=n, slots=slots: e.transpose(
                        psum[:, bank, j * P:(j + 1) * P], source[:, n % slots, :], ident[:, :]))
                    (at_free, gs_free, qd_free)[k][n % slots] = t
                AE.wait(t, free.get((bank, two)))
                t = AE.do(lambda e, dest=dest, bank=bank: e.activation(dest[:, two, :], psum[:, bank, :], ACT.Copy))
                if bank != B_QS:
                    free[bank] = t
                copied.append(t)
            return copied

        def keys(g, copied):
            PE.wait(copied[0], free.get(B_K))
            t = PE.do(lambda e: e.matmul(psum[:, B_K, :], weights[:, WI["Wk"], :], attr_t[:, g % 2, :], start=True, stop=True))
            free[(B_ATTR, g % 2)] = t
            return t

        def products(g, copied, key_tok):
            two = g % 2
            VE.wait(copied[2], free.get(("prod", 2)))
            p2 = VE.do(lambda e: e.tensor_tensor(prod[:, 2, :], psum[:, B_QS, :], qdst_t[:, two, :], ALU.mult))
            VE.wait(key_tok, copied[1], free.get(("prod", 0)))
            p0 = VE.do(lambda e: e.scalar_tensor_tensor(prod[:, 0, :], psum[:, B_K, :], bk_col[:, 0:1], qsrc_t[:, two, :],
                                                        ALU.add, ALU.mult))
            VE.wait(free.get(("prod", 1)))
            p1 = VE.do(lambda e: e.scalar_tensor_tensor(prod[:, 1, :], psum[:, B_K, :], bk_col[:, 0:1], qdst_t[:, two, :],
                                                        ALU.add, ALU.mult))
            free[B_QS] = p2
            free[B_K] = free[(B_QS, two)] = free[(B_QD, two)] = p1
            return ((2, p2), (0, p0), (1, p1))

        def logits(g, made):
            r, q = divmod(g, QUADS)
            bank = B_LOGIT[r % 2]
            PE.wait(free.get(bank))
            for n, (k, p) in enumerate(made):
                PE.wait(p)
                t = free[("prod", k)] = PE.do(lambda e, k=k, n=n: e.matmul(
                    psum[32 * q:32 * (q + 1), bank, :], head_sum[:, k, :], prod[:, k, :], start=(n == 0), stop=(n == 2),
                    tile_position=(0, 32 * q)))
            return t

        soft = {}

        def softmax_part(r, part, ready):
            cur, old = r % 2, 1 - r % 2
            m_now, m_before = m_run[:, cur, 1:BANK + 1], m_run[:, cur, 0:BANK]
            invalid, starts, factor = (masks[:, cur, k, :] for k in range(3))
            if part == 0:
                VE.wait(ready, soft["masks", r])
                t = free[B_LOGIT[cur]] = VE.do(lambda e: e.tensor_tensor(invalid, psum[:, B_LOGIT[cur], :], invalid, ALU.add))
                VE.wait(free.get(("runs", cur)))
                c = VE.do(lambda e: e.tensor_copy(m_run[:, cur, 0:1], m_run[:, old, BANK:BANK + 1]))
                VE.wait(t, c)
                soft["m", r] = VE.do(lambda e: e.tensor_tensor_scan(m_now, starts, invalid, m_run[:, cur, 0:1], ALU.add, ALU.max))
            elif part == 1:
                VE.wait(soft["m", r])
                t = VE.do(lambda e: e.tensor_tensor(expo[:, 0, :], invalid, m_now, ALU.subtract))
                c = VE.do(lambda e: e.tensor_tensor(starts, m_before, starts, ALU.add))
                AE.wait(t)
                soft["exp", r] = AE.do(lambda e: e.activation(expo[:, 0, :], expo[:, 0, :], ACT.Exp))
                VE.wait(c)
                t = VE.do(lambda e: e.tensor_tensor(starts, starts, m_now, ALU.subtract))
                AE.wait(t)
                soft["carry", r] = AE.do(lambda e: e.activation(starts, starts, ACT.Exp))
            elif part == 2:
                VE.wait(soft["exp", r])
                soft["weighted", r] = VE.do(lambda e: e.tensor_tensor(factor, expo[:, 0, :], factor, ALU.mult))
                VE.wait(soft["carry", r])
                soft["den", r] = VE.do(lambda e: e.tensor_tensor_scan(den_run[:, cur, :], starts, expo[:, 0, :],
                                                       den_run[:, old, BANK - 1:BANK], ALU.mult, ALU.add))
            else:
                VE.wait(soft["weighted", r])
                soft["num", r] = free[("masks", cur)] = VE.do(lambda e: e.tensor_tensor_scan(
                    num_run[:, cur, :], starts, factor, num_run[:, old, BANK - 1:BANK], ALU.mult, ALU.add))

        def ends_one_hot(r, j):
            made = []
            for q in range(QUADS):
                s = q * QS + r * GROUP + j
                VE.wait(hot_free[q])
                made.append(VE.do(lambda e, s=s, q=q: e.tensor_scalar(hot[:, q, :], iota_f[:, :], end_col[:, s:s + 1], None,
                                                                      ALU.is_equal)))
            return made

        def ends_product(r, j, made):
            cur, two = r % 2, j % 2
            PE.wait(soft["num", r], free.get(B_END))
            for k, run in enumerate((m_run[:, cur, 1:BANK + 1], den_run[:, cur, :], num_run[:, cur, :])):
                t = PE.do(lambda e, k=k, run=run: e.transpose(psum[:, B_END, k * P:(k + 1) * P], run[:, j * P:(j + 1) * P],
                                                              ident[:, :]))
            free[("runs", cur)] = t
            AE.wait(t, free.get(("ends", two)))
            t = free[B_END] = AE.do(lambda e: e.activation(ends[:, two, :], psum[:, B_END, 0:3 * P], ACT.Copy))
            values = ends[:, two, :].rearrange("p (k q c) -> p k q c", k=3, q=QUADS)
            PE.wait(t, free.get(B_SUM))
            for q in range(QUADS):
                PE.wait(made[q])
                t = hot_free[q] = PE.do(lambda e, q=q: e.matmul(
                    psum[:, B_SUM, q * ACCW:(q + 1) * ACCW].rearrange("p (k c) -> p k c", k=3), hot[:, q, :],
                    values[:, :, q, 0:SOFT], start=True, stop=True))
            free[("ends", two)] = t
            return t

        def ends_add(r, j, ready, blocks, tok):
            VE.wait(ready)
            for q in range(QUADS):
                VE.wait(tok[q])

                def add(e, q=q):
                    into = soft_acc[:, q, bass.ds(blocks[q][j], 1), :]
                    return e.tensor_tensor(into, into, psum[:, B_SUM, q * ACCW:(q + 1) * ACCW].rearrange("p (a c) -> p a c", a=1),
                                           ALU.add)
                tok[q] = VE.do(add)
            free[B_SUM] = tok[QUADS - 1]

        acc = [init_tok] * QUADS
        tokens = fetch(0)
        copied = transpose_group(0, tokens)
        for g in range(NG + 2 * QUADS):
            r, q = divmod(g, QUADS)
            if g < NG and q == 0:
                soft["masks", r] = load_masks(r)
            if g + 1 < NG:
                tokens = fetch(g + 1)
            done_round = r - 2
            if done_round >= 0:
                if q == 0:
                    blocks = [load_blocks(k * QS + done_round * GROUP, GROUP) for k in range(QUADS)]
                made = ends_one_hot(done_round, q)
            if g < NG:
                key_tok = keys(g, copied)
                prods = products(g, copied, key_tok)
            if done_round >= 0:
                summed = ends_product(done_round, q, made)
            if g + 1 < NG:
                copied = transpose_group(g + 1, tokens)
            if g < NG:
                last_logit = logits(g, prods)
            if 1 <= r <= ROUNDS:
                softmax_part(r - 1, q, soft.get(("logits", r - 1)))
            if done_round >= 0:
                ends_add(done_round, q, summed, blocks, acc)
            if g < NG and q == QUADS - 1:
                soft["logits", r] = last_logit
        acc_tok = (VE.done, VE.count)

        VE.wait(acc_tok)
        NC = NB * SOFT
        assert 4 * NC <= NX
        big_m = pool[:, 0:NC].rearrange("p (b c) -> p b c", b=NB)
        sum_d = pool[:, NC:2 * NC].rearrange("p (b c) -> p b c", b=NB)
        sum_n = pool[:, 2 * NC:3 * NC].rearrange("p (b c) -> p b c", b=NB)
        tmp3 = pool[:, 3 * NC:4 * NC].rearrange("p (b c) -> p b c", b=NB)

        def part(q, k):
            return soft_acc[:, q, :, k * SOFT:(k + 1) * SOFT]

        PE_end = (PE.done, PE.count)
        AE_end = (AE.done, AE.count)
        VE.wait(PE_end, AE_end)
        for q in range(QUADS):
            t = VE.do(lambda e, q=q: e.tensor_scalar(tmp3, part(q, 1), 0.5, -BIG, ALU.is_lt, ALU.mult))
            VE.wait(t)
            t = VE.do(lambda e, q=q: e.tensor_tensor(part(q, 0), part(q, 0), tmp3, ALU.add))
            VE.wait(t)
            if q == 0:
                t = VE.do(lambda e: e.tensor_copy(big_m, part(0, 0)))
            else:
                t = VE.do(lambda e, q=q: e.tensor_tensor(big_m, big_m, part(q, 0), ALU.max))
            VE.wait(t)
        for q in range(QUADS):
            t = VE.do(lambda e, q=q: e.tensor_tensor(part(q, 0), part(q, 0), big_m, ALU.subtract))
            AE.wait(t)
            t = AE.do(lambda e, q=q: e.activation(part(q, 0), part(q, 0), ACT.Exp))
            VE.wait(t)
            for k, total in ((1, sum_d), (2, sum_n)):
                if q == 0:
                    t = VE.do(lambda e, k=k, total=total: e.tensor_tensor(total, part(0, k), part(0, 0), ALU.mult))
                else:
                    t = VE.do(lambda e, q=q, k=k: e.tensor_tensor(tmp3, part(q, k), part(q, 0), ALU.mult))
                    VE.wait(t)
                    t = VE.do(lambda e, total=total: e.tensor_tensor(total, total, tmp3, ALU.add))
                VE.wait(t)
        t = VE.do(lambda e: e.scalar_tensor_tensor(sum_d, sum_d, 0.0, sum_d, ALU.is_equal, ALU.add))
        VE.wait(t)
        t = VE.do(lambda e: e.reciprocal(sum_d, sum_d))
        VE.wait(t)
        t = VE.do(lambda e: e.tensor_tensor(sum_n, sum_n, sum_d, ALU.mult))
        VE.wait(t)
        score = tmp3[:, :, 0:HEADS]
        t = VE.do(lambda e: e.tensor_tensor(score, sum_n[:, :, 0:HEADS], sum_n[:, :, HEADS:2 * HEADS], ALU.add))
        VE.wait(t)
        t = VE.do(lambda e: e.tensor_tensor(score, score, sum_n[:, :, 2 * HEADS:3 * HEADS], ALU.add))
        VE.wait(t)
        for lo, hi in groups:
            for b in range(lo, hi):
                tok = VE.do(lambda e, b=b: e.tensor_tensor(
                    V[:, b, :].rearrange("p (h d) -> p h d", h=HEADS), V[:, b, :].rearrange("p (h d) -> p h d", h=HEADS),
                    spread(score[:, b, :].rearrange("p (h a) -> p h a", a=1), 2, HEAD_DIM), ALU.mult))

        def attention_out(g, lo, hi, view, t):
            VE.wait(t)
            n = hi - lo
            st = stage[:, g % 4, 0:n * P].rearrange("p (b d) -> p b d", b=n)
            free = VE.do(lambda e: e.tensor_tensor(st, view, bias_of("bo", n), ALU.add))
            VE.wait(free)
            t = VE.do(lambda e: e.scalar_tensor_tensor(st, st, SLOPE, st, ALU.mult, ALU.max))
            VE.wait(t)
            hidden.append(VE.do(lambda e: e.tensor_tensor(X[:, lo:hi, :], X[:, lo:hi, :], st, ALU.add)))
            return free

        hidden = []
        bank_free = [(VE.done, VE.count)] * PS_BANKS
        dense([(V, "Wo")], [tok], attention_out)
        tok = hidden[-1]

        normed = layer_norm(Y, [tok])
        stored = [store_table(table[1], Y[:, lo:hi, :], g, lo, hi, normed[hi - 1]) for g, (lo, hi) in enumerate(groups)]
        end = aggregate(table[1], stored[-4:], False, [])
        VE.wait(end)
        for lo, hi in groups:
            tok = VE.do(lambda e, lo=lo, hi=hi: e.tensor_tensor(AGG[:, lo:hi, :], AGG[:, lo:hi, :], col_bc(inv_cnt, lo, hi), ALU.mult))
        nrm = ln_shift
        square = pool[:, 8 * BANK:9 * BANK]

        def sage_out(g, lo, hi, view, t):
            VE.wait(t)
            n = hi - lo
            st = stage[:, g % 4, 0:n * P].rearrange("p (b d) -> p b d", b=n)
            sq = square[:, 0:n * P].rearrange("p (b d) -> p b d", b=n)
            free = VE.do(lambda e: e.tensor_tensor(st, view, bias_of("bl", n), ALU.add))
            VE.wait(free)
            t = VE.do(lambda e: e.tensor_tensor(sq, st, st, ALU.mult))
            VE.wait(t)
            t = VE.do(lambda e: e.tensor_reduce(nrm[:, lo:hi], sq, AX.X, ALU.add))
            VE.wait(t)
            t = VE.do(lambda e: e.tensor_scalar(nrm[:, lo:hi], nrm[:, lo:hi], NORM_EPS * NORM_EPS, None, ALU.max))
            AE.wait(t)
            t = AE.do(lambda e: e.activation(nrm[:, lo:hi], nrm[:, lo:hi], ACT.Sqrt))
            VE.wait(t)
            t = VE.do(lambda e: e.reciprocal(nrm[:, lo:hi], nrm[:, lo:hi]))
            VE.wait(t)
            t = VE.do(lambda e: e.tensor_tensor(st, st, col_bc(nrm, lo, hi), ALU.mult))
            VE.wait(t)
            t = VE.do(lambda e: e.tensor_tensor(X[:, lo:hi, :], X[:, lo:hi, :], st, ALU.add))
            SP.wait(t)
            whole = min(hi, NB - 1)
            if whole > lo:
                SP.dma(lambda e: e.dma_start(out[lo * P:whole * P, :].rearrange("(b p) d -> p b d", p=P),
                                                         X[:, lo:whole, :]), out_lane[g % 4])
            if hi == NB:
                SP.dma(lambda e: e.dma_start(out[(NB - 1) * P:N, :], X[0:LAST, NB - 1, :]), out_lane[g % 4])
            return free

        dense([(AGG, "Wl"), (Y, "Wr")], [tok], sage_out)
        SP.wait(*[(lane.handle, lane.count) for lane in out_lane])

        block = ctx.enter_context(nc.Block())
        for engine in (VE, AE, PE, GE, SP):
            def emit(e, engine=engine):
                for instruction in engine.queue:
                    instruction(e)
            {"vector": block.vector, "scalar": block.scalar, "tensor": block.tensor, "gpsimd": block.gpsimd,
             "sync": block.sync}[engine.name](emit)


_NAMES = ["x", "src", "dst", "edge_attr_128", "edge_weight", "edge_weight1", "L0_gnn_W0", "L0_gnn_b0", "L0_gnn_W1",
          "L0_gnn_b1", "L0_gnn_W2", "L0_gnn_b2", "L1_gnn_W1", "L1_gnn_b1", "L1_gnn_W2", "L1_gnn_b2", "L2_gnn_Wq",
          "L2_gnn_bq", "L2_gnn_Wk", "L2_gnn_bk", "L2_gnn_Wv", "L2_gnn_bv", "L2_gnn_Wo", "L2_gnn_bo", "L2_gnn_lam",
          "L3_gnn_W_l", "L3_gnn_b_l", "L3_gnn_W_r"]


def kernel(**inputs):
    import numpy as np
    import concourse.bacc as bacc
    from concourse.bass_utils import run_bass_kernel_spmd

    nc = bacc.Bacc("TRN2", target_bir_lowering=False, num_devices=1)
    arrays, args = {}, []
    for name in _NAMES:
        a = np.ascontiguousarray(inputs[name])
        if a.ndim == 0:
            a = a.reshape(1)
        arrays[name] = a
        args.append(nc.dram_tensor(name, a.shape, mybir.dt.from_np(a.dtype), kind="ExternalInput").ap())
    out = nc.dram_tensor("out", arrays["x"].shape, F32, kind="ExternalOutput").ap()
    build(nc, *args, out)
    result = run_bass_kernel_spmd(nc, [arrays], core_ids=[0])
    return result.results[0]["out"]
```

```python
import math
from contextlib import ExitStack

import concourse.bass as bass
from concourse import mybir

F32 = mybir.dt.float32
BF16 = mybir.dt.bfloat16
I32 = mybir.dt.int32
ALU = mybir.AluOpType
ACT = mybir.ActivationFunctionType
AX = mybir.AxisListType

P = 128
D = 128
HEADS = 8
HEAD_DIM = D // HEADS
SCALE = 1.0 / math.sqrt(HEAD_DIM)
LN_EPS = 1e-5
NORM_EPS = 1e-12
SLOPE = 0.1
BIG = 1e30

PS_BANKS = 8
BANK = 512
GROUP = BANK // P


def ceil_div(a, b):
    return -(-a // b)


def spread(ap, dim, n):
    shape = list(ap.shape)
    shape[dim] = n
    return ap.broadcast_to(shape)


class Engine:

    def __init__(self, name, done):
        self.name, self.done, self.count, self.queue, self.seen = name, done, 0, [], {}

    def do(self, instruction):
        self.count += 1
        self.queue.append(lambda e, f=instruction, s=self.done: f(e).then_inc(s, 1))
        return (self.done, self.count)

    def dma(self, instruction, semaphore):
        semaphore.count += 16
        self.queue.append(lambda e, f=instruction, s=semaphore.handle: f(e).then_inc(s, 16))
        return (semaphore.handle, semaphore.count)

    def wait(self, *tokens):
        for token in tokens:
            if token is None:
                continue
            handle, count = token
            if self.seen.get(id(handle), 0) < count:
                self.seen[id(handle)] = count
                self.queue.append(lambda e, h=handle, c=count: e.wait_ge(h, c))


class Lane:

    def __init__(self, handle):
        self.handle, self.count = handle, 0


def build(nc, x_in, src_in, dst_in, attr_in, ew_in, dist_in, W0, b0, W1, b1, W2, b2,
          G1, c1, G2, c2, Wq, bq, Wk, bk, Wv, bv, Wo, bo, lam, Wl, bl, Wr, out):
    N = x_in.shape[0]
    E = src_in.shape[0]
    NB = ceil_div(N, P)
    NP = NB * P
    LAST = N - (NB - 1) * P
    NT = ceil_div(E, P)
    OVER = NT * P - E
    QUADS = 4
    NS = ceil_div(NT + NB - 1, QUADS * GROUP) * QUADS * GROUP
    SR = ceil_div(NS, P)
    QS = NS // QUADS
    FIELDS = 5
    DST, BEFORE, AFTER, SRC, WEIGHT = range(FIELDS)

    ctx = ExitStack()
    with ctx:
        def sb(name, shape, dt=F32):
            return ctx.enter_context(nc.sbuf_tensor(name, shape, dt))

        def sem(name):
            return ctx.enter_context(nc.semaphore(name))

        def lane(name):
            return Lane(sem(name))

        VE = Engine("vector", sem("vector_done"))
        AE = Engine("scalar", sem("scalar_done"))
        PE = Engine("tensor", sem("tensor_done"))
        GE = Engine("gpsimd", sem("gpsimd_done"))
        SP = Engine("sync", sem("sync_done"))

        edge_tiles = nc.dram_tensor("edge_tiles", [NT, FIELDS * P], I32).ap()
        PLAN = 2
        plan_rows = nc.dram_tensor("plan_rows", [PLAN, SR * P], I32).ap()
        rel_rows = nc.dram_tensor("rel_rows", [SR * P, P], BF16).ap()
        att_flat = nc.dram_tensor("att_flat", [E], F32).ap()
        att_tiles = nc.dram_tensor("att_tiles", [NT, P], F32).ap()
        step_masks = nc.dram_tensor("step_masks", [3, SR * P, P], F32).ap()
        table = [nc.dram_tensor(f"table{i}", [NP, D], F32).ap() for i in range(2)]

        ident = sb("ident", [P, P])
        iota_f = sb("iota_f", [P, P])
        iota_b = sb("iota_b", [P, P], BF16)
        X = sb("X", [P, NB, D])
        QV = sb("QV", [P, NB, D])
        ACCW = 3 * 3 * HEADS
        SOFT = 3 * HEADS
        work = sb("work", [P, max(QUADS * NB * ACCW, 2 * NB * D)])
        AGG = work[:, 0:NB * D].rearrange("p (b d) -> p b d", b=NB)
        Y = work[:, NB * D:2 * NB * D].rearrange("p (b d) -> p b d", b=NB)
        soft_acc = work[:, 0:QUADS * NB * ACCW].rearrange("p (q b c) -> p q b c", q=QUADS, b=NB)
        rel_col = sb("rel_col", [P, SR * P])
        end_col = sb("end_col", [P, SR * P])
        ew_col = sb("ew_col", [P, SR * P])
        src_col = sb("src_col", [P, SR * P], I32)
        plan_reg = sb("plan_reg", [PLAN, NS], I32)
        weights = sb("weights", [P, 12, P])
        WI = {n: i for i, n in enumerate(["W0", "W1", "W2", "G1", "G2", "Wq", "Wk", "Wv", "Wo", "Wl", "Wr"])}
        bias = sb("bias", [P, 9, P])
        BI = {n: i for i, n in enumerate(["b0", "b1", "b2", "c1", "c2", "bq", "bv", "bo", "bl"])}
        bk_col = sb("bk_col", [P, 1])
        head_sum = sb("head_sum", [P, 3, 32])
        dis = sb("dis", [P, NB])
        deg = sb("deg", [P, NB])
        inv_cnt = sb("inv_cnt", [P, NB])
        ln_mv = sb("ln_mv", [P, NB, 2])
        ln_rstd = sb("ln_rstd", [P, NB])
        ln_shift = sb("ln_shift", [P, NB])

        SLOTS = 10
        HOTS = 4
        gath = sb("gath", [P, SLOTS, D])
        hot = sb("hot", [P, 2 * HOTS, P])
        ln_stat = hot[:, HOTS:, :].rearrange("p a b -> p (a b)")[:, 0:NB * 6].rearrange("p (b k) -> p b k", k=6)
        NX = 15880
        pool = sb("pool", [P, NX])

        psum = ctx.enter_context(nc.psum_tensor("psum", [P, PS_BANKS, BANK], F32))

        slot_lane = [lane(f"slot{i}") for i in range(SLOTS)]
        setup_lane = [lane(f"setup{i}") for i in range(24)]
        table_lane = [lane(f"table_lane{i}") for i in range(4)]
        out_lane = [lane(f"out_lane{i}") for i in range(4)]

        iota_tok = GE.do(lambda e: e.iota(iota_f[:, :], pattern=[[1, P]], base=0, channel_multiplier=0,
                                          allow_small_or_imprecise_dtypes=True))
        step_no = sb("step_no", [P, SR])
        step_no_tok = GE.do(lambda e: e.iota(step_no[:, :], pattern=[[P, SR]], base=0, channel_multiplier=1,
                                             allow_small_or_imprecise_dtypes=True))
        part_no = sb("part_no", [P, 1])
        part_tok = GE.do(lambda e: e.iota(part_no[:, :], pattern=[[0, 1]], base=0, channel_multiplier=1,
                                          allow_small_or_imprecise_dtypes=True))
        VE.wait(iota_tok, part_tok)
        ident_tok = VE.do(lambda e: e.tensor_scalar(ident[:, :], iota_f[:, :], part_no[:, 0:1], None, ALU.is_equal))
        iota_b_tok = VE.do(lambda e: e.tensor_copy(iota_b[:, :], iota_f[:, :]))
        ones_row = sb("ones_row", [1, P])
        ones_tok = VE.do(lambda e: e.memset(ones_row[:, :], 1.0))
        minus_row = sb("minus_row", [1, P], I32)
        minus_tok = VE.do(lambda e: e.memset(minus_row[:, :], -1))

        hs_tok = GE.do(lambda e: e.memset(head_sum[:, :, :], 0.0))
        for k in range(3):
            part = head_sum[:, k, HEADS * k:HEADS * (k + 1)]
            GE.wait(hs_tok)
            hs_tok = GE.do(lambda e, part=part: e.memset(part, SCALE))
            for base, mult, step in ((0, 1, -HEAD_DIM), (HEAD_DIM - 1, -1, HEAD_DIM)):
                GE.wait(hs_tok)
                hs_tok = GE.do(lambda e, part=part, base=base, mult=mult, step=step: e.affine_select(
                    out=part, in_=part, compare_op=ALU.is_ge, fill=0.0, base=base, pattern=[[step, HEADS]],
                    channel_multiplier=mult))
        head_sum_tok = hs_tok

        setup = iter(setup_lane)
        raw = {DST: dst_in, SRC: src_in, WEIGHT: ew_in.bitcast(I32)}
        WHOLE = (NT - 1) * P
        first_last = pool[0:1, 0:2 * NT].bitcast(I32).rearrange("a (k t) -> a k t", k=2)
        fl_lane = next(setup)
        SP.dma(lambda e: e.dma_start(first_last[:, 0, 0:NT], dst_in.rearrange("(a e) -> a e", a=1)[:, 0:WHOLE + 1:P],
                                     allow_slow_non_contiguous=True), fl_lane)
        SP.dma(lambda e: e.dma_start(first_last[:, 1, 0:NT - 1], dst_in.rearrange("(a e) -> a e", a=1)[:, P - 1:WHOLE:P],
                                     allow_slow_non_contiguous=True), fl_lane)
        fl_tok = SP.dma(lambda e: e.dma_start(first_last[:, 1, NT - 1:NT], dst_in[E - 1:E].rearrange("(a e) -> a e", a=1)),
                        fl_lane)
        tiles_lane = next(setup)
        tile_fields = edge_tiles.rearrange("t (f e) -> t f e", f=FIELDS)
        for field in (DST, SRC, WEIGHT):
            flat = raw[field]
            SP.dma(lambda e, field=field, flat=flat: e.dma_start(
                tile_fields[0:NT - 1, field, :], flat[0:WHOLE].rearrange("(t e) -> t e", e=P)), tiles_lane)
            skip = OVER if field == DST else 0
            SP.dma(lambda e, field=field, flat=flat, skip=skip: e.dma_start(
                tile_fields[NT - 1:NT, field, skip:P], flat[E - P + skip:E].rearrange("(t e) -> t e", t=1)), tiles_lane)
        before = edge_tiles.rearrange("t (f e) -> t f e", f=FIELDS)[:, BEFORE, :]
        after = edge_tiles.rearrange("t (f e) -> t f e", f=FIELDS)[:, AFTER, :]
        SP.dma(lambda e: e.dma_start(before[1:NT - 1, :], dst_in[P - 1:WHOLE - 1].rearrange("(t e) -> t e", e=P)), tiles_lane)
        SP.dma(lambda e: e.dma_start(before[0:1, 1:P], dst_in[0:P - 1].rearrange("(t e) -> t e", t=1)), tiles_lane)
        SP.dma(lambda e: e.dma_start(before[NT - 1:NT, :], dst_in[E - P - 1:E - 1].rearrange("(t e) -> t e", t=1)), tiles_lane)
        SP.dma(lambda e: e.dma_start(after[0:NT - 1, :], dst_in[1:WHOLE + 1].rearrange("(t e) -> t e", e=P)), tiles_lane)
        SP.dma(lambda e: e.dma_start(after[NT - 1:NT, 0:P - 1], dst_in[E - P + 1:E].rearrange("(t e) -> t e", t=1)), tiles_lane)
        SP.wait(minus_tok)
        if OVER:
            SP.dma(lambda e: e.dma_start(tile_fields[NT - 1:NT, DST, 0:OVER], minus_row[:, 0:OVER]), tiles_lane)
        SP.dma(lambda e: e.dma_start(before[0:1, 0:1], minus_row[:, 0:1]), tiles_lane)
        tiles_tok = SP.dma(lambda e: e.dma_start(after[NT - 1:NT, P - 1:P], minus_row[:, 0:1]), tiles_lane)

        x_lane = next(setup)
        VE_x0 = VE.do(lambda e: e.memset(X[:, NB - 1, :], 0.0))
        SP.dma(lambda e: e.dma_start(X[:, 0:NB - 1, :], x_in[0:(NB - 1) * P, :].rearrange("(b p) d -> p b d", p=P)), x_lane)
        SP.wait(VE_x0)
        x_tok = SP.dma(lambda e: e.dma_start(X[0:LAST, NB - 1, :], x_in[(NB - 1) * P:N, :]), x_lane)
        w_lane = next(setup)
        for name, w in dict(W0=W0, W1=W1, W2=W2, G1=G1, G2=G2, Wq=Wq, Wk=Wk, Wv=Wv, Wo=Wo, Wl=Wl, Wr=Wr).items():
            AE.dma(lambda e, name=name, w=w: e.dma_start(weights[:, WI[name], :], w), w_lane)
        for name, b in dict(b0=b0, b1=b1, b2=b2, c1=c1, c2=c2, bq=bq, bv=bv, bo=bo, bl=bl).items():
            AE.dma(lambda e, name=name, b=b: e.dma_start(
                bias[:, BI[name], :], spread(b.rearrange("(a d) -> a d", a=1), 0, P)), w_lane)
        lam_col = sb("lam_col", [P, 1])
        AE.dma(lambda e: e.dma_start(lam_col[:, :], spread(lam.rearrange("(a d) -> a d", a=1), 0, P)), w_lane)
        w_tok = AE.dma(lambda e: e.dma_start(bk_col[:, :], bk.rearrange("(d a) -> d a", a=1)), w_lane)

        DR = max(d for d in range(1, P + 1) if E % d == 0)
        DC = E // DR
        dist_sb = QV[0:DR, :, :].rearrange("p b d -> p (b d)")[:, 0:DC]
        lam_row = QV[0:DR, :, :].rearrange("p b d -> p (b d)")[:, DC:2 * DC]
        dist_tok = SP.dma(lambda e: e.dma_start(dist_sb, dist_in.rearrange("(p c) a -> p (c a)", p=DR)), next(setup))
        VE.wait(w_tok)
        t = VE.do(lambda e: e.memset(lam_row, 0.0))
        VE.wait(t)
        lam_tok = VE.do(lambda e: e.tensor_scalar(lam_row, lam_row, lam_col[0:DR, 0:1], None, ALU.add))

        o = 2 * NT
        row = {}
        for name in ("fb", "lb", "spread", "off", "gap", "dgap", "ones"):
            row[name] = pool[0:1, o:o + NT]
            o += NT
        fl_block = pool[0:1, o:o + 2 * NT].bitcast(I32).rearrange("a (k t) -> a k t", k=2)
        o += 2 * NT
        ones_nt = VE.do(lambda e: e.memset(row["ones"], 1.0))
        VE.wait(fl_tok)
        t = VE.do(lambda e: e.tensor_scalar(fl_block, first_last, P.bit_length() - 1, None, ALU.arith_shift_right))
        VE.wait(t)
        VE.do(lambda e: e.tensor_copy(row["fb"], fl_block[:, 0, :]))
        t = VE.do(lambda e: e.tensor_copy(row["lb"], fl_block[:, 1, :]))
        VE.wait(t)
        t = VE.do(lambda e: e.tensor_tensor(row["spread"], row["lb"], row["fb"], ALU.subtract))
        VE.wait(t)
        t = VE.do(lambda e: e.tensor_scalar(row["spread"], row["spread"], 1.0, None, ALU.add))
        VE.wait(t, ones_nt)
        t = VE.do(lambda e: e.tensor_tensor_scan(row["off"], row["ones"], row["spread"], 0.0, ALU.mult, ALU.add))
        VE.wait(t)
        t = VE.do(lambda e: e.tensor_tensor(row["off"], row["off"], row["spread"], ALU.subtract))
        VE.wait(t)
        t = VE.do(lambda e: e.tensor_tensor(row["gap"], row["fb"], row["off"], ALU.subtract))
        VE.wait(t)
        VE.do(lambda e: e.tensor_copy(row["dgap"][:, 0:1], row["gap"][:, 0:1]))
        plan_tok = VE.do(lambda e: e.tensor_tensor(row["dgap"][:, 1:NT], row["gap"][:, 1:NT], row["gap"][:, 0:NT - 1],
                                                   ALU.subtract))
        off_all = pool[:, o:o + NT]
        dgap_all = pool[:, o + NT:o + 2 * NT]
        step_junk = pool[:, o + 2 * NT:o + 3 * NT]
        ROWS = o + 3 * NT
        assert ROWS <= NX
        PE.wait(plan_tok)
        copies = []
        bank = 0
        for name, dest in (("off", off_all), ("dgap", dgap_all)):
            for lo in range(0, NT, BANK):
                hi = min(NT, lo + BANK)
                t = PE.do(lambda e, name=name, lo=lo, hi=hi, bank=bank: e.matmul(
                    psum[:, bank, 0:hi - lo], ones_row[:, 0:P], row[name][:, lo:hi], start=True, stop=True))
                VE.wait(t)
                copies.append(VE.do(lambda e, dest=dest, lo=lo, hi=hi, bank=bank: e.tensor_copy(
                    dest[:, lo:hi], psum[:, bank, 0:hi - lo])))
                bank += 1
        VE.wait(copies[-1], step_no_tok)
        tile_of = sb("tile_of", [P, SR])
        block_of = sb("block_of", [P, SR])
        t = None
        for i in range(SR):
            t = VE.do(lambda e, i=i: e.tensor_scalar(step_junk, off_all, step_no[:, i:i + 1], None, ALU.is_le, ALU.add,
                                                     accum_out=tile_of[:, i:i + 1]))
            VE.wait(t)
            t = VE.do(lambda e, i=i: e.scalar_tensor_tensor(step_junk, off_all, step_no[:, i:i + 1], dgap_all, ALU.is_le,
                                                            ALU.mult, accum_out=block_of[:, i:i + 1]))
            VE.wait(t)
        t = VE.do(lambda e: e.tensor_scalar(tile_of[:, :], tile_of[:, :], -1.0, None, ALU.add))
        t = VE.do(lambda e: e.tensor_tensor(block_of[:, :], block_of[:, :], step_no[:, :], ALU.add))
        VE.wait(t)
        tile_idx = sb("tile_idx", [P, SR], I32)
        plan_cols = sb("plan_cols", [P, PLAN, SR])
        tile_tok = VE.do(lambda e: e.tensor_copy(tile_idx[:, :], tile_of[:, :]))
        VE.do(lambda e: e.tensor_scalar(plan_cols[:, 0, :], block_of[:, :], float(NB - 1), None, ALU.min))
        t = VE.do(lambda e: e.tensor_scalar(plan_cols[:, 1, :], tile_of[:, :], float(P), float(E - P), ALU.mult, ALU.min))
        base_of = sb("base_of", [P, SR])
        base_tok = VE.do(lambda e: e.tensor_scalar(base_of[:, :], block_of[:, :], float(P), None, ALU.mult))
        PE.wait(t, ident_tok)
        bank = 4
        t = PE.do(lambda e: e.transpose(psum[0:PLAN * SR, bank, 0:P], plan_cols[:, :, :].rearrange("p k s -> p (k s)"),
                                        ident[:, :]))
        VE.wait(t)
        plan_t = hot[0:PLAN * SR, 0, :].bitcast(I32)
        t = VE.do(lambda e: e.tensor_copy(plan_t[:, :], psum[0:PLAN * SR, 4, 0:P]))
        SP.wait(t)
        pl = next(setup)
        t = SP.dma(lambda e: e.dma_start(plan_rows.rearrange("k (s p) -> (k s) p", p=P), plan_t[:, :]), pl)
        SP.wait(t)
        plan_reg_tok = SP.dma(lambda e: e.dma_start(plan_reg[:, :], plan_rows[:, 0:NS]), next(setup))

        def power():
            GE.wait(lam_tok, dist_tok)
            p = GE.do(lambda e: e.tensor_tensor(dist_sb, dist_sb, lam_row, ALU.pow))
            SP.wait(p)
            return SP.dma(lambda e: e.dma_start(att_flat.rearrange("(p c) -> p c", p=DR), dist_sb), next(setup))

        step_rows = work[:, 0:SR * FIELDS * P].bitcast(I32).rearrange("p (s f) -> p s f", s=SR)
        GE.wait(tile_tok, tiles_tok)
        rows_tok = []
        for i in range(SR):
            rows_tok.append(GE.dma(lambda e, i=i: e.indirect_dma_start(
                out=step_rows[:, i, :], out_offset=None, in_=edge_tiles[:, :],
                in_offset=bass.IndirectOffsetOnAxis(ap=tile_idx[:, i:i + 1], axis=0),
                bounds_check=NT - 1, oob_is_err=False), slot_lane[i]))
        o = ROWS - 3 * NT
        def rows_f(k):
            return pool[:, k * SR * P:(k + 1) * SR * P].rearrange("p (s e) -> p s e", s=SR)
        rel, valid, start, endr, lmask, srcf, tmp = (rows_f(k) for k in range(7))
        raw_field = step_rows.rearrange("p s (f e) -> p s f e", f=FIELDS)
        VE.wait(*rows_tok)
        VE.wait(base_tok)
        t = VE.do(lambda e: e.tensor_copy(tmp, raw_field[:, :, DST, :]))
        VE.do(lambda e: e.tensor_copy(srcf, raw_field[:, :, SRC, :]))
        for i in range(SR):
            VE.wait(t)
            t2 = VE.do(lambda e, i=i: e.tensor_scalar(rel[:, i, :], tmp[:, i, :], base_of[:, i:i + 1], None, ALU.subtract))
        VE.wait(t2)
        t = VE.do(lambda e: e.tensor_scalar(rel, rel, -1.0, float(P), ALU.max, ALU.min))
        VE.wait(t)
        t = VE.do(lambda e: e.tensor_scalar(valid, rel, 0.0, None, ALU.is_ge))
        VE.wait(t)
        t = VE.do(lambda e: e.scalar_tensor_tensor(valid, rel, float(P) - 0.5, valid, ALU.is_lt, ALU.mult))
        VE.wait(t)
        VE.do(lambda e: e.tensor_scalar(lmask, valid, -1.0, BIG, ALU.add, ALU.mult))
        t = VE.do(lambda e: e.tensor_copy(start, raw_field[:, :, BEFORE, :]))
        t = VE.do(lambda e: e.tensor_copy(endr, raw_field[:, :, AFTER, :]))
        VE.wait(t)
        VE.do(lambda e: e.tensor_tensor(start, start, tmp, ALU.not_equal))
        t = VE.do(lambda e: e.tensor_tensor(endr, endr, tmp, ALU.not_equal))
        forced = sb("forced", [P, SR])
        f = VE.do(lambda e: e.tensor_scalar(forced[:, :], step_no[:, :], float(QS - 1), None, ALU.is_equal))
        for q in range(1, QUADS):
            VE.wait(f)
            f = VE.do(lambda e, q=q: e.scalar_tensor_tensor(forced[:, :], step_no[:, :], float(QS * (q + 1) - 1), forced[:, :],
                                                            ALU.is_equal, ALU.max))
        VE.wait(f, t)
        t = VE.do(lambda e: e.tensor_tensor(endr[:, :, P - 1], endr[:, :, P - 1], forced[:, :], ALU.max))
        VE.wait(t)
        VE.do(lambda e: e.tensor_tensor(start, start, valid, ALU.mult))
        t = VE.do(lambda e: e.tensor_tensor(endr, endr, valid, ALU.mult))
        VE.wait(t)
        t = VE.do(lambda e: e.tensor_scalar(start, start, -BIG, None, ALU.mult))
        t = VE.do(lambda e: e.scalar_tensor_tensor(endr, rel, 1.0, endr, ALU.add, ALU.mult))
        VE.wait(t)
        VE.do(lambda e: e.tensor_scalar(endr, endr, -1.0, None, ALU.add))
        rel_b = pool[:, 9 * SR * P:9 * SR * P + SR * P // 2].bitcast(BF16).rearrange("p (s e) -> p s e", s=SR)
        rows_done = VE.do(lambda e: e.tensor_copy(rel_b, rel))
        SP.wait(rows_done)
        masks_lane = next(setup)
        for k, arr in enumerate((lmask, start)):
            masks_tok = SP.dma(lambda e, k=k, arr=arr: e.dma_start(
                step_masks[k].rearrange("(s p) e -> p s e", p=P), arr), masks_lane)
        masks_tok = SP.dma(lambda e: e.dma_start(rel_rows.rearrange("(s p) e -> p s e", p=P), rel_b), masks_lane)
        att_tok = power()
        SP.wait(att_tok)
        att_lane = next(setup)
        SP.dma(lambda e: e.dma_start(att_tiles[0:NT - 1, :], att_flat[0:WHOLE].rearrange("(t e) -> t e", e=P)), att_lane)
        t = SP.dma(lambda e: e.dma_start(att_tiles[NT - 1:NT, :], att_flat[E - P:E].rearrange("(t e) -> t e", t=1)), att_lane)
        GE.wait(t)
        att_rows = rows_f(8)
        for i in range(SR):
            t = GE.dma(lambda e, i=i: e.indirect_dma_start(
                out=att_rows[:, i, :], out_offset=None, in_=att_tiles[:, :],
                in_offset=bass.IndirectOffsetOnAxis(ap=tile_idx[:, i:i + 1], axis=0),
                bounds_check=NT - 1, oob_is_err=False), slot_lane[i])
            SP.wait(t)
        att_masks_tok = SP.dma(lambda e: e.dma_start(step_masks[2].rearrange("(s p) e -> p s e", p=P), att_rows), next(setup))
        ew_f = step_rows.bitcast(F32).rearrange("p s (f e) -> p s f e", f=FIELDS)[:, :, WEIGHT, :]
        PE.wait(rows_done)
        free = {}
        n = 0
        for arr, dest in ((rel, rel_col), (ew_f, ew_col), (srcf, src_col), (endr, end_col)):
            for lo in range(0, SR, GROUP):
                hi = min(SR, lo + GROUP)
                b = n % 4
                PE.wait(free.get(b))
                for i in range(lo, hi):
                    t = PE.do(lambda e, arr=arr, i=i, lo=lo, b=b: e.transpose(
                        psum[:, b, (i - lo) * P:(i - lo + 1) * P], arr[:, i, :], ident[:, :]))
                VE.wait(t)
                free[b] = cols_tok = VE.do(lambda e, dest=dest, lo=lo, hi=hi, b=b: e.tensor_copy(
                    dest[:, lo * P:hi * P], psum[:, b, 0:(hi - lo) * P]))
                n += 1

        groups = [(lo, min(NB, lo + GROUP)) for lo in range(0, NB, GROUP)]

        def norm_begin(g):
            lo, hi = groups[g]
            for b in range(lo, hi):
                t = VE.do(lambda e, b=b: e.bn_stats(ln_stat[:, b, :], X[:, b, :]))
            VE.wait(t)
            for b in range(lo, hi):
                t = VE.do(lambda e, b=b: e.bn_aggr(ln_mv[:, b, :], ln_stat[:, b, :]))
            VE.wait(t)
            t = VE.do(lambda e: e.tensor_scalar(ln_rstd[:, lo:hi], ln_mv[:, lo:hi, 1], LN_EPS, None, ALU.add))
            AE.wait(t)
            return AE.do(lambda e: e.activation(ln_rstd[:, lo:hi], ln_rstd[:, lo:hi], ACT.Sqrt))

        def norm_end(g, root):
            lo, hi = groups[g]
            VE.wait(root)
            t = VE.do(lambda e: e.reciprocal(ln_rstd[:, lo:hi], ln_rstd[:, lo:hi]))
            VE.wait(t)
            return VE.do(lambda e: e.scalar_tensor_tensor(ln_shift[:, lo:hi], ln_mv[:, lo:hi, 0], -1.0, ln_rstd[:, lo:hi],
                                                          ALU.mult, ALU.mult))

        def normalise(dest, g, shift):
            AE.wait(shift)
            for b in range(*groups[g]):
                t = AE.do(lambda e, b=b: e.activation(dest[:, b, :], X[:, b, :], ACT.Relu, bias=ln_shift[:, b:b + 1],
                                                      scale=ln_rstd[:, b:b + 1]))
            return t

        def layer_norm(dest):
            roots, done = [], []

            def feed(g):
                roots.append(norm_begin(g))
                for k in ([g - 1] if g > 0 else []) + ([g] if g == len(groups) - 1 else []):
                    done.append(normalise(dest, k, norm_end(k, roots[k])))
            return feed, done

        PARTS = 4
        PER = BANK // PARTS
        SRW = SR * P
        parts = pool[:, 0:SRW * PARTS // 2].bitcast(BF16).rearrange("p (s k) -> p s k", k=PARTS)
        rest = pool[:, SRW * 2:SRW * 3]
        VE.wait(cols_tok, masks_tok)
        t = VE.do(lambda e: e.tensor_copy(parts[:, :, 0], ew_col[:, :]))
        VE.do(lambda e: e.memset(parts[:, :, 3], 1.0))
        VE.wait(t)
        t = VE.do(lambda e: e.tensor_tensor(rest, ew_col[:, :], parts[:, :, 0], ALU.subtract))
        VE.wait(t)
        t = VE.do(lambda e: e.tensor_copy(parts[:, :, 1], rest))
        VE.wait(t)
        t = VE.do(lambda e: e.tensor_tensor(rest, rest, parts[:, :, 1], ALU.subtract))
        VE.wait(t)
        parts_tok = VE.do(lambda e: e.tensor_copy(parts[:, :, 2], rest))
        BY_VECTOR, BY_SCALAR = 9, 3
        HB = 6
        HALL = HB + 2 * BY_SCALAR
        assert HALL * P // 2 <= SRW
        hot_b = pool[:, SRW * 3:SRW * 3 + HALL * P // 2].bitcast(BF16).rearrange("p (k n) -> p k n", k=HALL)
        deg_of = pool[:, SRW * 4:SRW * 6].rearrange("p (k s) -> p k s", k=2)
        PE.wait(parts_tok)
        VE.wait(x_tok)
        roots = [norm_begin(g) for g in range(len(groups))]
        shifts = [norm_end(g, root) for g, root in enumerate(roots)]
        VE.wait(iota_b_tok)
        AE.wait(iota_b_tok, cols_tok)
        pe_tok = []
        z = VE.do(lambda e: e.memset(deg_of[:, :, NS:SRW], 0.0))
        PE.wait(*free.values())
        half_free = [None, None]

        def degree_product(s, slot, ready):
            PE.wait(ready)
            return PE.do(lambda e: e.matmul(psum[:, s // PER, (s % PER) * PARTS:(s % PER + 1) * PARTS], hot_b[:, slot, :],
                                            parts[:, s, :], start=True, stop=True))

        for n, lo in enumerate(range(0, NS, BY_VECTOR + BY_SCALAR)):
            whole = lo + BY_VECTOR + BY_SCALAR <= NS
            mid, hi = (lo + BY_VECTOR, lo + BY_VECTOR + BY_SCALAR) if whole else (NS, NS)
            first = HB + (n % 2) * BY_SCALAR
            AE.wait(half_free[n % 2])
            for s in range(mid, hi):
                t = AE.do(lambda e, s=s, slot=first + s - mid: e.activation(hot_b[:, slot, :], iota_b[:, :], ACT.Abs, scale=-1.0,
                                                                            bias=rel_col[:, s:s + 1]))
            if whole:
                AE.wait(t)
                half = hot_b[:, first:first + BY_SCALAR, :]
                on_scalar = AE.do(lambda e, half=half: e.activation(half, half, ACT.Relu, scale=-1.0, bias=1.0))
            for s in range(lo, mid):
                if len(pe_tok) >= HB:
                    VE.wait(pe_tok[-HB])
                slot = len(pe_tok) % HB
                t = VE.do(lambda e, s=s, slot=slot: e.tensor_scalar(hot_b[:, slot, :], iota_b[:, :], rel_col[:, s:s + 1], None,
                                                                    ALU.is_equal))
                pe_tok.append(degree_product(s, slot, t))
            for s in range(mid, hi):
                half_free[n % 2] = degree_product(s, first + s - mid, on_scalar)
        normed = [normalise(AGG, g, shifts[g]) for g in range(len(groups))]
        VE.wait((PE.done, PE.count))
        for lo in range(0, NS, PER):
            n = min(PER, NS - lo)
            view = psum[:, lo // PER, 0:n * PARTS].rearrange("p (s k) -> p s k", k=PARTS)
            VE.do(lambda e, lo=lo, n=n, view=view: e.tensor_reduce(deg_of[:, 0, lo:lo + n], view[:, :, 0:3], AX.X, ALU.add))
            deg_tok = VE.do(lambda e, lo=lo, n=n, view=view: e.tensor_copy(deg_of[:, 1, lo:lo + n], view[:, :, 3]))
        block_hot = pool[:, SRW * 6:SRW * 6 + SR * NB].rearrange("p (s b) -> p s b", s=SR)
        for i in range(SR):
            bh_tok = VE.do(lambda e, i=i: e.tensor_scalar(block_hot[:, i, :], iota_f[:, 0:NB], block_of[:, i:i + 1], None,
                                                          ALU.is_equal))
        deg_t = pool[:, SRW * 3:SRW * 4].rearrange("p (s n) -> p s n", s=SR)
        PE.wait(deg_tok, bh_tok)
        for k in range(2):
            for lo in range(0, SR, GROUP):
                hi = min(SR, lo + GROUP)
                for i in range(lo, hi):
                    t = PE.do(lambda e, i=i, lo=lo, k=k: e.transpose(
                        psum[:, lo // GROUP, (i - lo) * P:(i - lo + 1) * P], deg_of[:, k, i * P:(i + 1) * P], ident[:, :]))
                VE.wait(t)
                t = VE.do(lambda e, lo=lo, hi=hi: e.tensor_copy(
                    deg_t[:, lo:hi, :], psum[:, lo // GROUP, 0:(hi - lo) * P].rearrange("p (s n) -> p s n", n=P)))
            PE.wait(t)
            for i in range(SR):
                t = PE.do(lambda e, i=i, k=k: e.matmul(psum[:, 2 + k, 0:NB], deg_t[:, i, :], block_hot[:, i, :],
                                                       start=(i == 0), stop=(i == SR - 1)))
            VE.wait(t)
            PE.wait(t)
        cnt_tok = VE.do(lambda e: e.tensor_scalar(inv_cnt[:, :], psum[:, 3, 0:NB], 1.0, None, ALU.max))
        t = VE.do(lambda e: e.tensor_scalar(deg[:, :], psum[:, 2, 0:NB], 1.0, None, ALU.add))
        VE.wait(t, cnt_tok)
        VE.do(lambda e: e.reciprocal(inv_cnt[:, :], inv_cnt[:, :]))
        t = VE.do(lambda e: e.tensor_scalar(dis[:, :], deg[:, :], 1e-30, None, ALU.max))
        AE.wait(t)
        t = AE.do(lambda e: e.activation(dis[:, :], dis[:, :], ACT.Sqrt))
        VE.wait(t)
        t = VE.do(lambda e: e.reciprocal(dis[:, :], dis[:, :]))
        VE.wait(t)
        dis_tok = VE.do(lambda e: e.scalar_tensor_tensor(dis[:, :], deg[:, :], 0.0, dis[:, :], ALU.is_gt, ALU.mult))

        PE.wait(w_tok, dis_tok)
        for k, name in enumerate(["Wq", "Wk", "Wv", "Wo", "Wl", "Wr"]):
            t = PE.do(lambda e, name=name, k=k: e.transpose(psum[:, k % 4, 0:P], weights[:, WI[name], :], ident[:, :]))
            AE.wait(t)
            t = AE.do(lambda e, name=name, k=k: e.activation(weights[:, WI[name], :], psum[:, k % 4, 0:P], ACT.Copy))
            PE.wait(t)
        wt_tok = t

        tr = pool[:, 0:4 * BANK].rearrange("p (k n) -> p k n", k=4)
        stage = pool[:, 4 * BANK:8 * BANK].rearrange("p (k n) -> p k n", k=4)
        stage_free = [None] * 4
        tr_free = [None] * 4
        bank_free = [None] * PS_BANKS

        def dense(sources, outputs, ready, post, func=ACT.Copy):
            def turn(g):
                lo, hi = groups[g]
                n = hi - lo
                PE.wait(*given[g])
                moved = []
                for k, source in enumerate(sources):
                    b = 2 * k + g % 2
                    PE.wait(bank_free[b])
                    for i in range(n):
                        t = PE.do(lambda e, source=source, i=i, b=b: e.transpose(
                            psum[:, b, i * P:(i + 1) * P], source[:, lo + i, :], ident[:, :]))
                    AE.wait(t, tr_free[b])
                    bank_free[b] = AE.do(lambda e, b=b: e.activation(tr[:, b, 0:n * P], psum[:, b, 0:n * P], func))
                    moved.append(bank_free[b])
                return moved

            given = [ready(0), ready(1)]
            moved = turn(0)
            for g, (lo, hi) in enumerate(groups):
                n = hi - lo
                ahead = turn(g + 1) if g + 1 < len(groups) else None
                if g + 2 < len(groups):
                    given.append(ready(g + 2))
                PE.wait(*moved)
                views = []
                for m, output in enumerate(outputs):
                    bank = 4 + 2 * m + g % 2
                    PE.wait(bank_free[bank])
                    for i in range(n):
                        for at, (k, w) in enumerate(output):
                            t = PE.do(lambda e, i=i, k=k, w=w, at=at, bank=bank, output=output, g=g: e.matmul(
                                psum[:, bank, i * P:(i + 1) * P], tr[:, 2 * k + g % 2, i * P:(i + 1) * P],
                                weights[:, WI[w], :], start=(at == 0), stop=(at == len(output) - 1)))
                    views.append(psum[:, bank, 0:n * P].rearrange("p (b d) -> p b d", b=n))
                for k in range(len(sources)):
                    tr_free[2 * k + g % 2] = t
                t = post(g, lo, hi, views, t)
                for m in range(len(outputs)):
                    bank_free[4 + 2 * m + g % 2] = t
                moved = ahead

        def bias_of(name, n):
            return spread(bias[:, BI[name], :].rearrange("p (a d) -> p a d", a=1), 1, n)

        def store_table(dest, source, g, lo, hi, ready):
            SP.wait(ready)
            return SP.dma(lambda e: e.dma_start(dest[lo * P:hi * P, :].rearrange("(b p) d -> p b d", p=P), source),
                          table_lane[g % 4])

        def col_bc(col, lo, hi):
            return spread(col[:, lo:hi].rearrange("p (b a) -> p b a", a=1), 2, D)

        plan_ready = plan_reg_tok

        def load_plan(engine, row, first, n, top, reason):
            values = []
            kind = {"vector": mybir.EngineType.DVE, "scalar": mybir.EngineType.Activation, "sync": mybir.EngineType.SP}[engine.name]
            engine.queue.append(lambda e: values.extend(nc.values_load_multi_w_load_instructions(
                plan_reg[row:row + 1, first:first + n], engines=[kind], min_val=0, max_val=top,
                skip_runtime_bounds_check_because=reason)[1]))
            return values

        def load_blocks(engine, first, n):
            return load_plan(engine, 0, first, n, NB - 1, "the plan takes the smaller of the block and the last block")

        REGS = 16

        def aggregate(source, stored, weighted, agg_free, start=None):
            VE.wait(plan_ready, *agg_free)
            acc_tok = start or VE.do(lambda e: e.memset(AGG, 0.0))
            GE.wait(*stored)
            PE.wait(*agg_free)
            mm = []

            def gather(s):
                if s >= SLOTS:
                    GE.wait(mm[s - SLOTS])
                return GE.dma(lambda e: e.indirect_dma_start(
                    out=gath[:, s % SLOTS, :], out_offset=None, in_=source[:, :],
                    in_offset=bass.IndirectOffsetOnAxis(ap=src_col[:, s:s + 1], axis=0),
                    bounds_check=NP - 1, oob_is_err=False), slot_lane[s % SLOTS])

            def one_hot(s):
                if s >= HOTS:
                    VE.wait(mm[s - HOTS])
                return VE.do(lambda e: e.tensor_scalar(
                    hot[:, s % HOTS, :], iota_f[:, :], rel_col[:, s:s + 1], ew_col[:, s:s + 1] if weighted else None,
                    ALU.is_equal, ALU.mult if weighted else ALU.bypass))

            gathered = []
            hots = []
            for s in range(NS + 2):
                if s < NS:
                    gathered.append(gather(s))
                    hots.append(one_hot(s))
                    PE.wait(hots[s], gathered[s])
                    PE.wait(bank_free[s % 4])
                    mm.append(PE.do(lambda e, s=s: e.matmul(psum[:, s % 4, 0:D], hot[:, s % HOTS, :], gath[:, s % SLOTS, :],
                                                            start=True, stop=True)))
                if s >= 2:
                    a = s - 2
                    if a % REGS == 0:
                        blocks = load_blocks(VE, a, REGS)
                    VE.wait(mm[a], acc_tok)

                    def add(e, a=a, blocks=blocks):
                        b = blocks[a % REGS]
                        return e.tensor_tensor(AGG[:, bass.ds(b, 1), :], AGG[:, bass.ds(b, 1), :],
                                               psum[:, a % 4, 0:D].rearrange("p (a d) -> p a d", a=1), ALU.add)
                    acc_tok = VE.do(add)
                    bank_free[a % 4] = acc_tok
            return acc_tok

        def gcn_table(which):
            def post(g, lo, hi, views, t):
                VE.wait(t, dis_tok)
                t = VE.do(lambda e: e.tensor_tensor(Y[:, lo:hi, :], views[0], col_bc(dis, lo, hi), ALU.mult))
                stored.append(store_table(table[which], Y[:, lo:hi, :], g, lo, hi, t))
                GE.wait(t)
                started.append(GE.do(lambda e: e.tensor_copy(AGG[:, lo:hi, :], Y[:, lo:hi, :])))
                return t
            return post

        for layer, (w, b) in enumerate((("W0", "b0"), ("W1", "b1"), ("W2", "b2"))):
            stored, started = [], []
            dense([AGG], [[(0, w)]], (lambda g: [normed[g], wt_tok]) if layer == 0 else (lambda g: [bias_add(g)]),
                  gcn_table(layer % 2), ACT.Copy if layer == 0 else ACT.Relu)
            end = aggregate(table[layer % 2], stored[-4:], True, [(PE.done, PE.count)], started[-1])

            def bias_add(g, b=b, end=end):
                VE.wait(end)
                for i in range(*groups[g]):
                    t = VE.do(lambda e, i=i: e.scalar_tensor_tensor(AGG[:, i, :], AGG[:, i, :], dis[:, i:i + 1],
                                                                    bias[:, BI[b], :], ALU.mult, ALU.add))
                return t

        feed, normed = layer_norm(AGG)
        for g, (lo, hi) in enumerate(groups):
            VE.wait(bias_add(g))
            t = VE.do(lambda e, lo=lo, hi=hi: e.scalar_tensor_tensor(X[:, lo:hi, :], AGG[:, lo:hi, :], 0.0, X[:, lo:hi, :],
                                                                     ALU.max, ALU.add))
            VE.wait(t)
            feed(g)

        stored = [store_table(table[1], AGG[:, lo:hi, :], g, lo, hi, normed[g]) for g, (lo, hi) in enumerate(groups)]
        tok = aggregate(table[1], stored[-4:], True, stored[-4:], normed[-1])

        hidden = []
        feed, normed = layer_norm(AGG)

        def gin_hidden(g, lo, hi, views, t):
            VE.wait(t)
            hidden.append(VE.do(lambda e: e.tensor_tensor(Y[:, lo:hi, :], views[0], bias_of("c1", hi - lo), ALU.add)))
            return hidden[-1]

        def gin_out(g, lo, hi, views, t):
            VE.wait(t)
            free = VE.do(lambda e: e.tensor_tensor(AGG[:, lo:hi, :], views[0], bias_of("c2", hi - lo), ALU.add))
            VE.wait(free)
            t = VE.do(lambda e: e.tensor_tensor(X[:, lo:hi, :], X[:, lo:hi, :], AGG[:, lo:hi, :], ALU.add))
            VE.wait(t)
            feed(g)
            return free

        dense([AGG], [[(0, "G1")]], lambda g: [tok], gin_hidden)
        dense([Y], [[(0, "G2")]], lambda g: [hidden[g]], gin_out, ACT.Relu)

        stored = []

        def q_nodes(g, lo, hi, views, t):
            VE.wait(t)
            t = VE.do(lambda e: e.tensor_tensor(QV[:, lo:hi, :], views[0], bias_of("bq", hi - lo), ALU.add))
            stored.append(store_table(table[0], QV[:, lo:hi, :], g, lo, hi, t))
            return t

        GE.wait((PE.done, PE.count), (VE.done, VE.count))
        GE.do(lambda e: e.memset(work[:, NB * D:], 0.0))
        dense([AGG], [[(0, "Wq")]], lambda g: [normed[g]], q_nodes)
        q_done = [(PE.done, PE.count), (AE.done, AE.count), (VE.done, VE.count)] + stored[-4:]

        o = 0

        def take(n, *shape):
            nonlocal o
            view = pool[:, o:o + n * math.prod(shape)]
            o += n * math.prod(shape)
            names = [f"a{i}" for i in range(len(shape) + 1)]
            return view.rearrange(f"p ({' '.join(names)}) -> p {' '.join(names)}",
                                  **{k: s for k, s in zip(names, (n,) + shape)})

        q_src = gath
        SLOT2 = 8
        q_block = take(SLOT2, D)
        rel_all = take(3, BANK // 2)
        expand = take(2, BANK)
        attr = take(SLOT2, D)
        attr_t = take(2, BANK)
        qsrc_t = take(2, BANK)
        qdst_t = take(2, BANK)
        prod = take(3, BANK)
        masks = take(2, 3, BANK)
        m_run = take(2, BANK + 1)
        den_run = take(2, BANK)
        num_run = take(2, BANK)
        expo = take(1, BANK)
        ends = take(2, 3 * P)
        assert o <= NX, o

        ROUNDS = QS // GROUP
        rel_lane = [lane(f"rel{i}") for i in range(3)]
        at_lane = [lane(f"attr{i}") for i in range(SLOT2)]
        mask_lane = [lane(f"mask{i}") for i in range(2)]
        B_ATTR, B_QS, B_QD, B_K, B_END, B_SUM = range(6)
        B_LOGIT = (6, 7)

        VE.wait(*q_done)
        GE.wait(*q_done)
        half_tok = GE.do(lambda e: e.memset(work[:, NB * D // 2:NB * D], 0.0))
        VE.do(lambda e: e.memset(work[:, 0:NB * D // 2], 0.0))
        VE.do(lambda e: e.memset(m_run[:, 1, BANK:BANK + 1], -BIG))
        VE.do(lambda e: e.memset(den_run[:, 1, BANK - 1:BANK], 0.0))
        init_tok = VE.do(lambda e: e.memset(num_run[:, 1, BANK - 1:BANK], 0.0))
        for eng in (GE, SP, PE, AE):
            eng.wait(*q_done)
            eng.wait(init_tok)
        VE.wait(half_tok)
        SP.wait(plan_reg_tok, masks_tok, att_masks_tok)

        free = {}
        gs_free = [None] * SLOTS
        qb_free = [None] * SLOT2
        at_free = [None] * SLOT2
        hot_free = [None] * HOTS
        NG = ROUNDS * QUADS

        def group_steps(g):
            first = (g % QUADS) * QS + (g // QUADS) * GROUP
            return range(first, first + GROUP)

        def fetch_places(g):
            if g >= NG:
                return None
            steps = group_steps(g)
            SP.wait(free.get(("rel", g % 3)))
            rel_tok = SP.dma(lambda e: e.dma_start(
                rel_all[:, g % 3, :].bitcast(BF16),
                spread(rel_rows[steps[0]:steps[0] + GROUP, :].rearrange("(a s) e -> a (s e)", a=1), 0, P)), rel_lane[g % 3])
            return rel_tok

        def fetch(g):
            steps = group_steps(g)
            regs = load_plan(SP, 1, steps[0], GROUP, E - P, "the plan takes the smaller of the tile's first edge and E - P")
            tokens = []
            for j, s in enumerate(steps):
                n = g * GROUP + j
                GE.wait(gs_free[n % SLOTS])
                a = GE.dma(lambda e, s=s, n=n: e.indirect_dma_start(
                    out=q_src[:, n % SLOTS, :], out_offset=None, in_=table[0][:, :],
                    in_offset=bass.IndirectOffsetOnAxis(ap=src_col[:, s:s + 1], axis=0),
                    bounds_check=NP - 1, oob_is_err=False), slot_lane[n % SLOTS])
                SP.wait(at_free[n % SLOT2])
                c = SP.dma(lambda e, j=j, n=n: e.dma_start(attr[:, n % SLOT2, :], attr_in[bass.ds(regs[j], P), :]),
                           at_lane[n % SLOT2])
                tokens.append((a, c))
            return tokens

        def block_rows(g):
            if g >= NG:
                return None
            blocks = load_blocks(AE, group_steps(g)[0], GROUP)
            for j in range(GROUP):
                slot = (g * GROUP + j) % SLOT2
                AE.wait(qb_free[slot])
                t = AE.do(lambda e, j=j, slot=slot: e.activation(q_block[:, slot:slot + 1, :], QV[:, bass.ds(blocks[j], 1), :],
                                                                 ACT.Copy))
            return t

        def expand_one_hot(g, rel_tok):
            VE.wait(rel_tok, free.get(("expand", g % 2)))
            t = free[("rel", g % 3)] = VE.do(lambda e: e.tensor_scalar(expand[:, g % 2, :], rel_all[:, g % 3, :].bitcast(BF16),
                                                                       part_no[:, 0:1], None, ALU.is_equal))
            return t

        def load_masks(r):
            SP.wait(free.get(("masks", r % 2)))
            for q in range(QUADS):
                s0 = q * QS + r * GROUP
                t = SP.dma(lambda e, q=q, s0=s0: e.dma_start(
                    masks[32 * q:32 * (q + 1), r % 2, :, :],
                    spread(step_masks[:, s0:s0 + GROUP, :].rearrange("k (a s) e -> a k (s e)", a=1), 0, 32)), mask_lane[r % 2])
            return t

        def transpose_group(g, tokens, expand_tok, block_tok):
            two = g % 2
            copied = []
            for k, (source, slot_free, which, bank, dest) in enumerate((
                    (attr, at_free, 1, B_ATTR, attr_t), (q_src, gs_free, 0, B_QS, qsrc_t), (q_block, qb_free, None, B_QD, qdst_t))):
                slots = source.shape[1]
                PE.wait(free.get(bank))
                if bank == B_QD:
                    PE.wait(expand_tok, block_tok)
                for j in range(GROUP):
                    n = g * GROUP + j
                    PE.wait(None if which is None else tokens[j][which])
                    into = psum[:, bank, j * P:(j + 1) * P]
                    if bank == B_QD:
                        t = PE.do(lambda e, n=n, j=j, into=into: e.matmul(
                            into, q_block[:, n % SLOT2, :], expand[:, two, j * P:(j + 1) * P], start=True, stop=True))
                    else:
                        t = PE.do(lambda e, source=source, n=n, slots=slots, into=into: e.transpose(
                            into, source[:, n % slots, :], ident[:, :]))
                    slot_free[n % slots] = t
                if bank == B_QD:
                    free[("expand", two)] = t
                AE.wait(t, free.get((bank, two)))
                t = AE.do(lambda e, dest=dest, bank=bank: e.activation(dest[:, two, :], psum[:, bank, :], ACT.Copy))
                if bank != B_QS:
                    free[bank] = t
                copied.append(t)
            return copied

        def keys(g, copied):
            PE.wait(copied[0], free.get(B_K))
            t = PE.do(lambda e: e.matmul(psum[:, B_K, :], weights[:, WI["Wk"], :], attr_t[:, g % 2, :], start=True, stop=True))
            free[(B_ATTR, g % 2)] = t
            return t

        def products(g, copied, key_tok):
            two = g % 2
            VE.wait(copied[2], free.get(("prod", 2)))
            p2 = VE.do(lambda e: e.tensor_tensor(prod[:, 2, :], psum[:, B_QS, :], qdst_t[:, two, :], ALU.mult))
            VE.wait(key_tok, copied[1], free.get(("prod", 0)))
            p0 = VE.do(lambda e: e.scalar_tensor_tensor(prod[:, 0, :], psum[:, B_K, :], bk_col[:, 0:1], qsrc_t[:, two, :],
                                                        ALU.add, ALU.mult))
            VE.wait(free.get(("prod", 1)))
            p1 = VE.do(lambda e: e.scalar_tensor_tensor(prod[:, 1, :], psum[:, B_K, :], bk_col[:, 0:1], qdst_t[:, two, :],
                                                        ALU.add, ALU.mult))
            free[B_QS] = p2
            free[B_K] = free[(B_QS, two)] = free[(B_QD, two)] = p1
            return ((2, p2), (0, p0), (1, p1))

        def logits(g, made, copied):
            r, q = divmod(g, QUADS)
            key_tok = None
            bank = B_LOGIT[r % 2]
            PE.wait(free.get(bank))
            for n, (k, p) in enumerate(made):
                if n == 2 and g + 1 < NG:
                    key_tok = keys(g + 1, copied)
                PE.wait(p)
                t = free[("prod", k)] = PE.do(lambda e, k=k, n=n: e.matmul(
                    psum[32 * q:32 * (q + 1), bank, :], head_sum[:, k, :], prod[:, k, :], start=(n == 0), stop=(n == 2),
                    tile_position=(0, 32 * q)))
            return t, key_tok

        soft = {}

        def softmax_part(r, part, ready):
            cur, old = r % 2, 1 - r % 2
            m_now, m_before = m_run[:, cur, 1:BANK + 1], m_run[:, cur, 0:BANK]
            invalid, starts, factor = (masks[:, cur, k, :] for k in range(3))
            if part == 0:
                VE.wait(ready, soft["masks", r])
                t = free[B_LOGIT[cur]] = VE.do(lambda e: e.tensor_tensor(invalid, psum[:, B_LOGIT[cur], :], invalid, ALU.add))
                VE.wait(free.get(("runs", cur)))
                c = VE.do(lambda e: e.tensor_copy(m_run[:, cur, 0:1], m_run[:, old, BANK:BANK + 1]))
                VE.wait(t, c)
                soft["m", r] = VE.do(lambda e: e.tensor_tensor_scan(m_now, starts, invalid, m_run[:, cur, 0:1], ALU.add, ALU.max))
            elif part == 1:
                VE.wait(soft["m", r])
                soft["below", r] = VE.do(lambda e: e.tensor_tensor(expo[:, 0, :], invalid, m_now, ALU.subtract))
                soft["restart", r] = VE.do(lambda e: e.tensor_tensor(starts, m_before, starts, ALU.add))
            elif part == 2:
                VE.wait(soft["restart", r])
                soft["drop", r] = VE.do(lambda e: e.tensor_tensor(starts, starts, m_now, ALU.subtract))
                VE.wait(soft["exp", r])
                soft["weighted", r] = VE.do(lambda e: e.tensor_tensor(factor, expo[:, 0, :], factor, ALU.mult))
            else:
                VE.wait(soft["carry", r])
                soft["den", r] = VE.do(lambda e: e.tensor_tensor_scan(den_run[:, cur, :], starts, expo[:, 0, :],
                                                       den_run[:, old, BANK - 1:BANK], ALU.mult, ALU.add))
                VE.wait(soft["weighted", r])
                soft["num", r] = free[("masks", cur)] = VE.do(lambda e: e.tensor_tensor_scan(
                    num_run[:, cur, :], starts, factor, num_run[:, old, BANK - 1:BANK], ALU.mult, ALU.add))

        def softmax_exp(r, part):
            starts = masks[:, r % 2, 1, :]
            if part == 1:
                AE.wait(soft["below", r])
                soft["exp", r] = AE.do(lambda e: e.activation(expo[:, 0, :], expo[:, 0, :], ACT.Exp))
            else:
                AE.wait(soft["drop", r])
                soft["carry", r] = AE.do(lambda e: e.activation(starts, starts, ACT.Exp))

        def chunk_of(g):
            r, q = divmod(g - 1, QUADS)
            return (r - 2, q) if 0 <= r - 2 < ROUNDS else None

        ON_VECTOR = 2

        def ends_one_hot(r, j):
            half = j % 2
            here = hot[:, half * QUADS:(half + 1) * QUADS, :]
            AE.wait(free.get(("hot", half)))
            VE.wait(free.get(("hot", half)))
            for q in range(QUADS):
                s = q * QS + r * GROUP + j
                if q < ON_VECTOR:
                    on_vector = VE.do(lambda e, s=s, q=q: e.tensor_scalar(here[:, q, :], iota_f[:, :], end_col[:, s:s + 1], None,
                                                                          ALU.is_equal))
                else:
                    t = AE.do(lambda e, s=s, q=q: e.activation(here[:, q, :], iota_f[:, :], ACT.Abs, scale=-1.0,
                                                               bias=end_col[:, s:s + 1]))
            AE.wait(t)
            part = here[:, ON_VECTOR:QUADS, :]
            return on_vector, AE.do(lambda e: e.activation(part, part, ACT.Relu, scale=-1.0, bias=1.0))

        def ends_transpose(r, j):
            cur, two = r % 2, j % 2
            PE.wait(soft["num", r], free.get(B_END))
            for k, run in enumerate((m_run[:, cur, 1:BANK + 1], den_run[:, cur, :], num_run[:, cur, :])):
                t = PE.do(lambda e, k=k, run=run: e.transpose(psum[:, B_END, k * P:(k + 1) * P], run[:, j * P:(j + 1) * P],
                                                              ident[:, :]))
            free[("runs", cur)] = t
            AE.wait(t, free.get(("ends", two)))
            t = free[B_END] = AE.do(lambda e: e.activation(ends[:, two, :], psum[:, B_END, 0:3 * P], ACT.Copy))
            return t

        def ends_product(r, j, values_tok, one_hot_tok):
            two = j % 2
            values = ends[:, two, :].rearrange("p (k q c) -> p k q c", k=3, q=QUADS)
            PE.wait(values_tok, *one_hot_tok, free.get(B_SUM))
            for q in range(QUADS):
                t = PE.do(lambda e, q=q: e.matmul(
                    psum[:, B_SUM, q * ACCW:(q + 1) * ACCW].rearrange("p (k c) -> p k c", k=3), hot[:, two * QUADS + q, :],
                    values[:, :, q, 0:SOFT], start=True, stop=True))
            free[("ends", two)] = free[("hot", two)] = t
            return t

        def ends_add(r, j, ready, blocks, tok):
            VE.wait(ready)
            for q in range(QUADS):
                VE.wait(tok[q])

                def add(e, q=q):
                    into = soft_acc[:, q, bass.ds(blocks[q][j], 1), :]
                    return e.tensor_tensor(into, into, psum[:, B_SUM, q * ACCW:(q + 1) * ACCW].rearrange("p (a c) -> p a c", a=1),
                                           ALU.add)
                tok[q] = VE.do(add)
            free[B_SUM] = tok[QUADS - 1]

        acc = [init_tok] * QUADS
        places = {i: fetch_places(i) for i in range(3)}
        expanded = {0: expand_one_hot(0, places[0]), 1: expand_one_hot(1, places[1])}
        block_toks = {0: block_rows(0), 1: block_rows(1)}
        copied = transpose_group(0, fetch(0), expanded[0], block_toks[0])
        key_tok = keys(0, copied)
        summed = one_hot_tok = None
        for g in range(NG + 2 * QUADS + 2):
            r, q = divmod(g, QUADS)
            chunk, chunk_before, chunk_next = chunk_of(g), chunk_of(g - 1), chunk_of(g + 1)
            if chunk_before:
                if chunk_before[1] == 0:
                    blocks = [load_blocks(VE, k * QS + chunk_before[0] * GROUP, GROUP) for k in range(QUADS)]
            if g < NG:
                prods = products(g, copied, key_tok)
            part_round, part = divmod(g - 1, QUADS)
            if 1 <= part_round <= ROUNDS:
                softmax_part(part_round - 1, part, soft["logits", part_round - 1])
            if chunk_before:
                ends_add(*chunk_before, summed, blocks, acc)
            if chunk:
                values_tok = ends_transpose(*chunk)
            if g + 1 < NG:
                copied = transpose_group(g + 1, fetch(g + 1), expanded[g + 1], block_toks[g + 1])
            one_hot_now = one_hot_tok
            if chunk_next:
                one_hot_tok = ends_one_hot(*chunk_next)
            if g + 2 < NG:
                places[g + 3] = fetch_places(g + 3)
                expanded[g + 2] = expand_one_hot(g + 2, places[g + 2])
                block_toks[g + 2] = block_rows(g + 2)
            if g < NG:
                last_logit, key_tok = logits(g, prods, copied)
            if chunk:
                summed = ends_product(*chunk, values_tok, one_hot_now)
            if 1 <= part_round <= ROUNDS and part in (1, 2):
                softmax_exp(part_round - 1, part)
            if g < NG and q == 2:
                soft["masks", r] = load_masks(r)
            if g < NG and q == QUADS - 1:
                soft["logits", r] = last_logit
        acc_tok = (VE.done, VE.count)

        VE.wait(acc_tok)
        NC = NB * SOFT
        JOIN = 8 * BANK
        assert JOIN + 4 * NC + QUADS * NB <= NX
        big_m, sum_d, sum_n, tmp3 = (pool[:, JOIN + k * NC:JOIN + (k + 1) * NC].rearrange("p (b c) -> p b c", b=NB)
                                     for k in range(4))
        absent = pool[:, JOIN + 4 * NC:JOIN + 4 * NC + QUADS * NB]
        by_node = work[:, 0:QUADS * NB * ACCW].rearrange("p (n c) -> p n c", c=ACCW)
        m_all, den_all, num_all = (by_node[:, :, k * SOFT:(k + 1) * SOFT] for k in range(3))

        VE.wait((PE.done, PE.count), (AE.done, AE.count))
        GE.wait((PE.done, PE.count))
        t = VE.do(lambda e: e.tensor_scalar(absent, den_all[:, :, 0], 0.5, -BIG, ALU.is_lt, ALU.mult))
        VE.wait(t)
        t = VE.do(lambda e: e.tensor_tensor(m_all, m_all, spread(absent.rearrange("p (n a) -> p n a", a=1), 2, SOFT), ALU.add))
        VE.wait(t)
        t = VE.do(lambda e: e.tensor_tensor(big_m, soft_acc[:, 0, :, 0:SOFT], soft_acc[:, 1, :, 0:SOFT], ALU.max))
        for q in range(2, QUADS):
            VE.wait(t)
            t = VE.do(lambda e, q=q: e.tensor_tensor(big_m, big_m, soft_acc[:, q, :, 0:SOFT], ALU.max))
        VE.wait(t)
        for q in range(QUADS):
            t = VE.do(lambda e, q=q: e.tensor_tensor(soft_acc[:, q, :, 0:SOFT], soft_acc[:, q, :, 0:SOFT], big_m, ALU.subtract))
            AE.wait(t)
            scale = AE.do(lambda e, q=q: e.activation(soft_acc[:, q, :, 0:SOFT], soft_acc[:, q, :, 0:SOFT], ACT.Exp))
            GE.wait(scale)
            num_tok = GE.do(lambda e, q=q: e.tensor_tensor(soft_acc[:, q, :, 2 * SOFT:3 * SOFT], soft_acc[:, q, :, 2 * SOFT:3 * SOFT],
                                                           soft_acc[:, q, :, 0:SOFT], ALU.mult))
        VE.wait(scale)
        t = VE.do(lambda e: e.tensor_tensor(den_all, den_all, m_all, ALU.mult))
        VE.wait(t)
        for k, total, ready in ((1, sum_d, None), (2, sum_n, num_tok)):
            VE.wait(ready)
            t = VE.do(lambda e, k=k, total=total: e.tensor_tensor(
                total, soft_acc[:, 0, :, k * SOFT:(k + 1) * SOFT], soft_acc[:, 1, :, k * SOFT:(k + 1) * SOFT], ALU.add))
            for q in range(2, QUADS):
                VE.wait(t)
                t = VE.do(lambda e, k=k, q=q, total=total: e.tensor_tensor(
                    total, total, soft_acc[:, q, :, k * SOFT:(k + 1) * SOFT], ALU.add))
            VE.wait(t)
        t = VE.do(lambda e: e.scalar_tensor_tensor(sum_d, sum_d, 0.0, sum_d, ALU.is_equal, ALU.add))
        VE.wait(t)
        t = VE.do(lambda e: e.reciprocal(sum_d, sum_d))
        VE.wait(t)
        t = VE.do(lambda e: e.tensor_tensor(sum_n, sum_n, sum_d, ALU.mult))
        VE.wait(t)
        score = tmp3[:, :, 0:HEADS]
        t = VE.do(lambda e: e.tensor_tensor(score, sum_n[:, :, 0:HEADS], sum_n[:, :, HEADS:2 * HEADS], ALU.add))
        VE.wait(t)
        t_score = VE.do(lambda e: e.tensor_tensor(score, score, sum_n[:, :, 2 * HEADS:3 * HEADS], ALU.add))
        weighted = []

        def v_score(g, lo, hi, views, t):
            VE.wait(t)
            free = VE.do(lambda e: e.tensor_tensor(QV[:, lo:hi, :], views[0], bias_of("bv", hi - lo), ALU.add))
            VE.wait(free)
            for b in range(lo, hi):
                t = VE.do(lambda e, b=b: e.tensor_tensor(
                    QV[:, b, :].rearrange("p (h d) -> p h d", h=HEADS), QV[:, b, :].rearrange("p (h d) -> p h d", h=HEADS),
                    spread(score[:, b, :].rearrange("p (h a) -> p h a", a=1), 2, HEAD_DIM), ALU.mult))
            weighted.append(t)
            return free

        def attention_out(g, lo, hi, views, t):
            VE.wait(t)
            n = hi - lo
            st = stage[:, g % 4, 0:n * P].rearrange("p (b d) -> p b d", b=n)
            free = VE.do(lambda e: e.tensor_tensor(st, views[0], bias_of("bo", n), ALU.add))
            VE.wait(free)
            t = VE.do(lambda e: e.scalar_tensor_tensor(st, st, SLOPE, st, ALU.mult, ALU.max))
            VE.wait(t)
            t = VE.do(lambda e: e.tensor_tensor(X[:, lo:hi, :], X[:, lo:hi, :], st, ALU.add))
            VE.wait(t)
            feed(g)
            return free

        bank_free = [t_score] * PS_BANKS
        AE.wait(t_score)
        dense([AGG], [[(0, "Wv")]], lambda g: [normalise(AGG, g, None)], v_score)
        feed, normed = layer_norm(Y)
        dense([QV], [[(0, "Wo")]], lambda g: [weighted[g]], attention_out)

        stored = [store_table(table[1], Y[:, lo:hi, :], g, lo, hi, normed[g]) for g, (lo, hi) in enumerate(groups)]
        end = aggregate(table[1], stored[-4:], False, [])

        def mean(g):
            VE.wait(end)
            lo, hi = groups[g]
            return VE.do(lambda e: e.tensor_tensor(AGG[:, lo:hi, :], AGG[:, lo:hi, :], col_bc(inv_cnt, lo, hi), ALU.mult))

        nrm = ln_shift
        square = pool[:, 8 * BANK:9 * BANK]

        squared = []

        def sage_out(g, lo, hi, views, t):
            VE.wait(t)
            n = hi - lo
            st = stage[:, g % 4, 0:n * P].rearrange("p (b d) -> p b d", b=n)
            sq = square[:, 0:n * P].rearrange("p (b d) -> p b d", b=n)
            free = VE.do(lambda e: e.tensor_tensor(st, views[0], bias_of("bl", n), ALU.add))
            VE.wait(free)
            t = VE.do(lambda e: e.tensor_tensor(sq, st, st, ALU.mult))
            VE.wait(t)
            t = VE.do(lambda e: e.tensor_reduce(nrm[:, lo:hi], sq, AX.X, ALU.add))
            VE.wait(t)
            t = VE.do(lambda e: e.tensor_scalar(nrm[:, lo:hi], nrm[:, lo:hi], NORM_EPS * NORM_EPS, None, ALU.max))
            AE.wait(t)
            squared.append((g, lo, hi, st, AE.do(lambda e: e.activation(nrm[:, lo:hi], nrm[:, lo:hi], ACT.Sqrt))))
            if g > 0:
                finish(*squared[g - 1])
            return free

        def finish(g, lo, hi, st, root):
            VE.wait(root)
            t = VE.do(lambda e: e.reciprocal(nrm[:, lo:hi], nrm[:, lo:hi]))
            VE.wait(t)
            t = VE.do(lambda e: e.tensor_tensor(st, st, col_bc(nrm, lo, hi), ALU.mult))
            VE.wait(t)
            t = VE.do(lambda e: e.tensor_tensor(X[:, lo:hi, :], X[:, lo:hi, :], st, ALU.add))
            SP.wait(t)
            whole = min(hi, NB - 1)
            if whole > lo:
                SP.dma(lambda e: e.dma_start(out[lo * P:whole * P, :].rearrange("(b p) d -> p b d", p=P),
                                                         X[:, lo:whole, :]), out_lane[g % 4])
            if hi == NB:
                SP.dma(lambda e: e.dma_start(out[(NB - 1) * P:N, :], X[0:LAST, NB - 1, :]), out_lane[g % 4])

        dense([AGG, Y], [[(0, "Wl"), (1, "Wr")]], lambda g: [mean(g)], sage_out)
        finish(*squared[-1])
        SP.wait(*[(lane.handle, lane.count) for lane in out_lane])

        block = ctx.enter_context(nc.Block())
        for engine in (VE, AE, PE, GE, SP):
            def emit(e, engine=engine):
                for instruction in engine.queue:
                    instruction(e)
            {"vector": block.vector, "scalar": block.scalar, "tensor": block.tensor, "gpsimd": block.gpsimd,
             "sync": block.sync}[engine.name](emit)


_NAMES = ["x", "src", "dst", "edge_attr_128", "edge_weight", "edge_weight1", "L0_gnn_W0", "L0_gnn_b0", "L0_gnn_W1",
          "L0_gnn_b1", "L0_gnn_W2", "L0_gnn_b2", "L1_gnn_W1", "L1_gnn_b1", "L1_gnn_W2", "L1_gnn_b2", "L2_gnn_Wq",
          "L2_gnn_bq", "L2_gnn_Wk", "L2_gnn_bk", "L2_gnn_Wv", "L2_gnn_bv", "L2_gnn_Wo", "L2_gnn_bo", "L2_gnn_lam",
          "L3_gnn_W_l", "L3_gnn_b_l", "L3_gnn_W_r"]


def kernel(**inputs):
    import numpy as np
    import concourse.bacc as bacc
    from concourse.bass_utils import run_bass_kernel_spmd

    nc = bacc.Bacc("TRN2", target_bir_lowering=False, num_devices=1)
    arrays, args = {}, []
    for name in _NAMES:
        a = np.ascontiguousarray(inputs[name])
        if a.ndim == 0:
            a = a.reshape(1)
        arrays[name] = a
        args.append(nc.dram_tensor(name, a.shape, mybir.dt.from_np(a.dtype), kind="ExternalInput").ap())
    out = nc.dram_tensor("out", arrays["x"].shape, F32, kind="ExternalOutput").ap()
    build(nc, *args, out)
    result = run_bass_kernel_spmd(nc, [arrays], core_ids=[0])
    return result.results[0]["out"]
```
